# Optimizing a Trainium2 kernel written in Bass

```python
import numpy as np
import jax
import jax.numpy as jnp

def _softmax(x, axis=-1):
    return jax.nn.softmax(x, axis=axis)

def _gelu(x):
    return jax.nn.gelu(x, approximate=True)

def _silu(x):
    return jax.nn.silu(x)

def _sigmoid(x):
    return jax.nn.sigmoid(x)

def _layernorm(x, axis=-1, eps=1e-05):
    m = jnp.mean(x, axis=axis, keepdims=True)
    v = jnp.var(x, axis=axis, keepdims=True)
    return (x - m) / jnp.sqrt(v + eps)

def _scatter_add(tgt, idx, src, axis=0):
    return tgt.at[idx].add(src)

def _segment_sum(src, seg, n):
    return jax.ops.segment_sum(src, seg, n)
kernel_name = 'mk_cond_seq_d4_seqx_r8_04f84c'

def setup_inputs(seed: int=0):
    np.random.seed(seed)
    _w = jnp.asarray

    def _rec_inputs():
        import jax
        import jax.numpy as jnp
        _rk = jax.random.key(seed)
        x = -0.0002928 + 1 * jax.random.normal(jax.random.fold_in(_rk, 1), (32, 128, 128), jnp.float32)
        _lenS = 128 - jax.random.randint(jax.random.fold_in(_rk, 7), (32,), 0, max(1, 128 // 4) + 1, jnp.int32)
        _lenS2 = 128 - jax.random.randint(jax.random.fold_in(_rk, 8), (32,), 0, max(1, 128 // 4) + 1, jnp.int32)
        itok_B_6_14 = jax.random.randint(jax.random.fold_in(_rk, 11), (32,), 6, 15, jnp.int32)
        condB_dt = jax.random.uniform(jax.random.fold_in(_rk, 12), (32,), jnp.float32, 0.0, 0.981965)
        condB_gatescore = jax.random.uniform(jax.random.fold_in(_rk, 13), (32,), jnp.float32, 0.0, 0.581427)
        condB_theta = jax.random.uniform(jax.random.fold_in(_rk, 14), (32,), jnp.float32, 0.0, 0.983423)
        condB_phi = jax.random.uniform(jax.random.fold_in(_rk, 15), (32,), jnp.float32, 0.0, 0.961312)
        return (x, itok_B_6_14, condB_dt, condB_gatescore, condB_theta, condB_phi)
    x, itok_B_6_14, condB_dt, condB_gatescore, condB_theta, condB_phi = _rec_inputs()

    def _L0_cond_setup():
        import jax, jax.numpy as jnp
        import numpy as np
        D = 128
        E = 8
        FF = 512
        TOPK = 2
        S = 32
        SE = 64
        SH = 128
        B, T = (2, 256)

        def _forward(x, subject_ids, ln_g, ln_b, subj_emb, hyp_w1, hyp_b1, hyp_w2, hyp_b2, sty_w1, sty_b1, sty_w2, sty_b2, router_w, exp_w1, exp_b1, exp_w2, exp_b2):
            mu = x.mean(-1, keepdims=True)
            var = x.var(-1, keepdims=True)
            h = (x - mu) * jax.lax.rsqrt(var + 1e-05) * ln_g + ln_b
            m_t = h.mean(1, keepdims=True)
            v_t = h.var(1, keepdims=True)
            h_norm = (h - m_t) * jax.lax.rsqrt(v_t + 1e-08)
            se = subj_emb[subject_ids]
            hyp = jax.nn.relu(se @ hyp_w1 + hyp_b1) @ hyp_w2 + hyp_b2
            sty = jax.nn.relu(hyp @ sty_w1 + sty_b1) @ sty_w2 + sty_b2
            gamma, beta = jnp.split(sty, 2, axis=-1)
            gamma = jax.nn.softplus(gamma) + 1e-08
            h = h_norm * gamma[:, None, :] + beta[:, None, :]
            h_flat = h.reshape(-1, D)
            probs = jax.nn.softmax(h_flat @ router_w, axis=-1)
            gates, idx = jax.lax.top_k(probs, TOPK)
            gates = gates / gates.sum(-1, keepdims=True)
            N = h_flat.shape[0]
            combine = jnp.zeros((N, E), h_flat.dtype).at[jnp.arange(N)[:, None], idx].add(gates)
            hid = jax.nn.relu(jnp.einsum('nd,edf->nef', h_flat, exp_w1) + exp_b1)
            eout = jnp.einsum('nef,efd->ned', hid, exp_w2) + exp_b2
            y = jnp.einsum('ned,ne->nd', eout, combine)
            return x + y.reshape(x.shape)
        key = jax.random.key(seed)
        ks = jax.random.split(key, 16)
        n = lambda k, sh, s=0.02: jax.random.normal(k, sh, dtype=jnp.float32) * s
        return {'x': jax.random.normal(ks[0], (B, T, D), dtype=jnp.float32), 'subject_ids': jax.random.randint(ks[1], (B,), 0, S), 'ln_g': jnp.ones((D,), jnp.float32), 'ln_b': jnp.zeros((D,), jnp.float32), 'subj_emb': n(ks[2], (S, SE)), 'hyp_w1': n(ks[3], (SE, SH), 1.0 / np.sqrt(SE)), 'hyp_b1': jnp.zeros((SH,), jnp.float32), 'hyp_w2': n(ks[4], (SH, SH), 1.0 / np.sqrt(SH)), 'hyp_b2': jnp.zeros((SH,), jnp.float32), 'sty_w1': n(ks[5], (SH, SH // 2), 1.0 / np.sqrt(SH)), 'sty_b1': jnp.zeros((SH // 2,), jnp.float32), 'sty_w2': n(ks[6], (SH // 2, 2 * D), 1.0 / np.sqrt(SH // 2)), 'sty_b2': jnp.zeros((2 * D,), jnp.float32), 'router_w': n(ks[7], (D, E), 1.0 / np.sqrt(D)), 'exp_w1': n(ks[8], (E, D, FF), 1.0 / np.sqrt(D)), 'exp_b1': jnp.zeros((E, FF), jnp.float32), 'exp_w2': n(ks[9], (E, FF, D), 1.0 / np.sqrt(FF)), 'exp_b2': jnp.zeros((E, D), jnp.float32)}
    _L0_cond_all = _L0_cond_setup()
    _L0_cond_in = {k: v for k, v in _L0_cond_all.items() if k in ('ln_g', 'ln_b', 'subj_emb', 'hyp_w1', 'hyp_b1', 'hyp_w2', 'hyp_b2', 'sty_w1', 'sty_b1', 'sty_w2', 'sty_b2', 'router_w', 'exp_w1', 'exp_b1', 'exp_w2', 'exp_b2')}
    del _L0_cond_all

    def _L1_cond_setup():
        import jax, jax.numpy as jnp
        import numpy as np
        B, NX, NY = (16, 128, 128)

        def _grad(f, axis):
            fm = jnp.moveaxis(f, axis, -1)
            g = (jnp.roll(fm, -1, -1) - jnp.roll(fm, 1, -1)) * 0.5
            g0 = (-3.0 * fm[..., 0] + 4.0 * fm[..., 1] - fm[..., 2]) * 0.5
            gN = (3.0 * fm[..., -1] - 4.0 * fm[..., -2] + fm[..., -3]) * 0.5
            g = g.at[..., 0].set(g0).at[..., -1].set(gN)
            return jnp.moveaxis(g, -1, axis)

        def _grad2(f, axis):
            fm = jnp.moveaxis(f, axis, -1)
            g = jnp.roll(fm, -1, -1) - 2.0 * fm + jnp.roll(fm, 1, -1)
            g0 = 2.0 * fm[..., 0] - 5.0 * fm[..., 1] + 4.0 * fm[..., 2] - fm[..., 3]
            gN = 2.0 * fm[..., -1] - 5.0 * fm[..., -2] + 4.0 * fm[..., -3] - fm[..., -4]
            g = g.at[..., 0].set(g0).at[..., -1].set(gN)
            return jnp.moveaxis(g, -1, axis)
        key = jax.random.key(seed)
        k1, k2, k3, k4 = jax.random.split(key, 4)
        f = jax.random.uniform(k1, (B, NX, NY), dtype=jnp.float32)
        A_grid = jax.random.normal(k2, (2, NX, NY), dtype=jnp.float32)
        B_grid = jax.random.uniform(k3, (3, NX, NY), dtype=jnp.float32)
        dt = jax.random.uniform(k4, (B,), dtype=jnp.float32)
        return {'f': f, 'A_grid': A_grid, 'B_grid': B_grid, 'dt': dt}
    _L1_cond_all = _L1_cond_setup()
    _L1_cond_in = {k: v for k, v in _L1_cond_all.items() if k in ('A_grid', 'B_grid')}
    del _L1_cond_all

    def _L2_cond_setup():
        import jax, jax.numpy as jnp
        import numpy as np
        D_MODEL = 128
        N_HEADS = 16
        D_HEAD = D_MODEL // N_HEADS
        D_FF = 512
        EPS = 1e-05

        def layernorm(x, gamma, beta):
            mu = jnp.mean(x, axis=-1, keepdims=True)
            var = jnp.var(x, axis=-1, keepdims=True)
            return (x - mu) * jax.lax.rsqrt(var + EPS) * gamma + beta
        key = jax.random.key(seed)
        ks = jax.random.split(key, 16)
        B, T = (4, 256)
        s = 1.0 / np.sqrt(D_MODEL)
        sf = 1.0 / np.sqrt(D_FF)
        return {'x': jax.random.normal(ks[0], (B, T, D_MODEL), jnp.float32), 'gate_score': jax.random.uniform(ks[1], (B,), jnp.float32), 'Wq': jax.random.normal(ks[2], (D_MODEL, D_MODEL), jnp.float32) * s, 'bq': jnp.zeros((D_MODEL,), jnp.float32), 'Wk': jax.random.normal(ks[3], (D_MODEL, D_MODEL), jnp.float32) * s, 'bk': jnp.zeros((D_MODEL,), jnp.float32), 'Wv': jax.random.normal(ks[4], (D_MODEL, D_MODEL), jnp.float32) * s, 'bv': jnp.zeros((D_MODEL,), jnp.float32), 'Wo': jax.random.normal(ks[5], (D_MODEL, D_MODEL), jnp.float32) * s, 'bo': jnp.zeros((D_MODEL,), jnp.float32), 'W1': jax.random.normal(ks[6], (D_MODEL, D_FF), jnp.float32) * s, 'b1': jnp.zeros((D_FF,), jnp.float32), 'W2': jax.random.normal(ks[7], (D_FF, D_MODEL), jnp.float32) * sf, 'b2': jnp.zeros((D_MODEL,), jnp.float32), 'gamma1': jnp.ones((D_MODEL,), jnp.float32), 'beta1': jnp.zeros((D_MODEL,), jnp.float32), 'gamma2': jnp.ones((D_MODEL,), jnp.float32), 'beta2': jnp.zeros((D_MODEL,), jnp.float32)}
    _L2_cond_all = _L2_cond_setup()
    _L2_cond_in = {k: v for k, v in _L2_cond_all.items() if k in ('Wq', 'bq', 'Wk', 'bk', 'Wv', 'bv', 'Wo', 'bo', 'W1', 'b1', 'W2', 'b2', 'gamma1', 'beta1', 'gamma2', 'beta2')}
    del _L2_cond_all

    def _L3_cond_setup():
        import jax, jax.numpy as jnp
        import numpy as np
        key = jax.random.key(seed)
        k1, k2, k3 = jax.random.split(key, 3)
        B, N, D = (16, 512, 128)
        embeddings = jax.random.normal(k1, (B, N, D), dtype=jnp.float32)
        theta = jax.random.uniform(k2, (B,), dtype=jnp.float32)
        phi = jax.random.uniform(k3, (B,), dtype=jnp.float32)
        return {'embeddings': embeddings, 'theta': theta, 'phi': phi}
    _L3_cond_all = _L3_cond_setup()
    _L3_cond_in = {k: v for k, v in _L3_cond_all.items() if k in ()}
    del _L3_cond_all
    return {'x': x, 'itok_B_6_14': itok_B_6_14, 'condB_dt': condB_dt, 'condB_gatescore': condB_gatescore, 'condB_theta': condB_theta, 'condB_phi': condB_phi, 'L0_cond_ln_g': _L0_cond_in['ln_g'], 'L0_cond_ln_b': _L0_cond_in['ln_b'], 'L0_cond_subj_emb': _L0_cond_in['subj_emb'], 'L0_cond_hyp_w1': _L0_cond_in['hyp_w1'], 'L0_cond_hyp_b1': _L0_cond_in['hyp_b1'], 'L0_cond_hyp_w2': _L0_cond_in['hyp_w2'], 'L0_cond_hyp_b2': _L0_cond_in['hyp_b2'], 'L0_cond_sty_w1': _L0_cond_in['sty_w1'], 'L0_cond_sty_b1': _L0_cond_in['sty_b1'], 'L0_cond_sty_w2': _L0_cond_in['sty_w2'], 'L0_cond_sty_b2': _L0_cond_in['sty_b2'], 'L0_cond_router_w': _L0_cond_in['router_w'], 'L0_cond_exp_w1': _L0_cond_in['exp_w1'], 'L0_cond_exp_b1': _L0_cond_in['exp_b1'], 'L0_cond_exp_w2': _L0_cond_in['exp_w2'], 'L0_cond_exp_b2': _L0_cond_in['exp_b2'], 'L1_cond_A_grid': _L1_cond_in['A_grid'], 'L1_cond_B_grid': _L1_cond_in['B_grid'], 'L2_cond_Wq': _L2_cond_in['Wq'], 'L2_cond_bq': _L2_cond_in['bq'], 'L2_cond_Wk': _L2_cond_in['Wk'], 'L2_cond_bk': _L2_cond_in['bk'], 'L2_cond_Wv': _L2_cond_in['Wv'], 'L2_cond_bv': _L2_cond_in['bv'], 'L2_cond_Wo': _L2_cond_in['Wo'], 'L2_cond_bo': _L2_cond_in['bo'], 'L2_cond_W1': _L2_cond_in['W1'], 'L2_cond_b1': _L2_cond_in['b1'], 'L2_cond_W2': _L2_cond_in['W2'], 'L2_cond_b2': _L2_cond_in['b2'], 'L2_cond_gamma1': _L2_cond_in['gamma1'], 'L2_cond_beta1': _L2_cond_in['beta1'], 'L2_cond_gamma2': _L2_cond_in['gamma2'], 'L2_cond_beta2': _L2_cond_in['beta2']}

def reference(x, itok_B_6_14, condB_dt, condB_gatescore, condB_theta, condB_phi, L0_cond_ln_g, L0_cond_ln_b, L0_cond_subj_emb, L0_cond_hyp_w1, L0_cond_hyp_b1, L0_cond_hyp_w2, L0_cond_hyp_b2, L0_cond_sty_w1, L0_cond_sty_b1, L0_cond_sty_w2, L0_cond_sty_b2, L0_cond_router_w, L0_cond_exp_w1, L0_cond_exp_b1, L0_cond_exp_w2, L0_cond_exp_b2, L1_cond_A_grid, L1_cond_B_grid, L2_cond_Wq, L2_cond_bq, L2_cond_Wk, L2_cond_bk, L2_cond_Wv, L2_cond_bv, L2_cond_Wo, L2_cond_bo, L2_cond_W1, L2_cond_b1, L2_cond_W2, L2_cond_b2, L2_cond_gamma1, L2_cond_beta1, L2_cond_gamma2, L2_cond_beta2):
    import jax
    import jax.numpy as jnp

    def _L0_cond_ref(x, subject_ids, ln_g, ln_b, subj_emb, hyp_w1, hyp_b1, hyp_w2, hyp_b2, sty_w1, sty_b1, sty_w2, sty_b2, router_w, exp_w1, exp_b1, exp_w2, exp_b2):
        import jax, jax.numpy as jnp
        import numpy as np
        D = 128
        E = 8
        FF = 512
        TOPK = 2
        S = 32
        SE = 64
        SH = 128
        B, T = (2, 256)

        def _forward(x, subject_ids, ln_g, ln_b, subj_emb, hyp_w1, hyp_b1, hyp_w2, hyp_b2, sty_w1, sty_b1, sty_w2, sty_b2, router_w, exp_w1, exp_b1, exp_w2, exp_b2):
            mu = x.mean(-1, keepdims=True)
            var = x.var(-1, keepdims=True)
            h = (x - mu) * jax.lax.rsqrt(var + 1e-05) * ln_g + ln_b
            m_t = h.mean(1, keepdims=True)
            v_t = h.var(1, keepdims=True)
            h_norm = (h - m_t) * jax.lax.rsqrt(v_t + 1e-08)
            se = subj_emb[subject_ids]
            hyp = jax.nn.relu(se @ hyp_w1 + hyp_b1) @ hyp_w2 + hyp_b2
            sty = jax.nn.relu(hyp @ sty_w1 + sty_b1) @ sty_w2 + sty_b2
            gamma, beta = jnp.split(sty, 2, axis=-1)
            gamma = jax.nn.softplus(gamma) + 1e-08
            h = h_norm * gamma[:, None, :] + beta[:, None, :]
            h_flat = h.reshape(-1, D)
            probs = jax.nn.softmax(h_flat @ router_w, axis=-1)
            gates, idx = jax.lax.top_k(probs, TOPK)
            gates = gates / gates.sum(-1, keepdims=True)
            N = h_flat.shape[0]
            combine = jnp.zeros((N, E), h_flat.dtype).at[jnp.arange(N)[:, None], idx].add(gates)
            hid = jax.nn.relu(jnp.einsum('nd,edf->nef', h_flat, exp_w1) + exp_b1)
            eout = jnp.einsum('nef,efd->ned', hid, exp_w2) + exp_b2
            y = jnp.einsum('ned,ne->nd', eout, combine)
            return x + y.reshape(x.shape)
        return _forward(x, subject_ids, ln_g, ln_b, subj_emb, hyp_w1, hyp_b1, hyp_w2, hyp_b2, sty_w1, sty_b1, sty_w2, sty_b2, router_w, exp_w1, exp_b1, exp_w2, exp_b2)

    def _L1_cond_ref(f, A_grid, B_grid, dt):
        import jax, jax.numpy as jnp
        import numpy as np
        B, NX, NY = (16, 128, 128)

        def _grad(f, axis):
            fm = jnp.moveaxis(f, axis, -1)
            g = (jnp.roll(fm, -1, -1) - jnp.roll(fm, 1, -1)) * 0.5
            g0 = (-3.0 * fm[..., 0] + 4.0 * fm[..., 1] - fm[..., 2]) * 0.5
            gN = (3.0 * fm[..., -1] - 4.0 * fm[..., -2] + fm[..., -3]) * 0.5
            g = g.at[..., 0].set(g0).at[..., -1].set(gN)
            return jnp.moveaxis(g, -1, axis)

        def _grad2(f, axis):
            fm = jnp.moveaxis(f, axis, -1)
            g = jnp.roll(fm, -1, -1) - 2.0 * fm + jnp.roll(fm, 1, -1)
            g0 = 2.0 * fm[..., 0] - 5.0 * fm[..., 1] + 4.0 * fm[..., 2] - fm[..., 3]
            gN = 2.0 * fm[..., -1] - 5.0 * fm[..., -2] + 4.0 * fm[..., -3] - fm[..., -4]
            g = g.at[..., 0].set(g0).at[..., -1].set(gN)
            return jnp.moveaxis(g, -1, axis)
        Af = A_grid[None] * f[:, None]
        Bf = B_grid[None] * f[:, None]
        gradv_Af = _grad(Af[:, 0], 1) + _grad(Af[:, 1], 2)
        gradvv_Bf = _grad2(Bf[:, 0], 1) + _grad2(Bf[:, 1], 2) + _grad(_grad(Bf[:, 2], 2), 1) + _grad(_grad(Bf[:, 2], 1), 2)
        df = -gradv_Af + gradvv_Bf * 0.5
        f_new = f + df * dt[:, None, None]
        return jnp.maximum(f_new, 0.0)

    def _L2_cond_ref(x, gate_score, Wq, bq, Wk, bk, Wv, bv, Wo, bo, W1, b1, W2, b2, gamma1, beta1, gamma2, beta2):
        import jax, jax.numpy as jnp
        import numpy as np
        D_MODEL = 128
        N_HEADS = 16
        D_HEAD = D_MODEL // N_HEADS
        D_FF = 512
        EPS = 1e-05

        def layernorm(x, gamma, beta):
            mu = jnp.mean(x, axis=-1, keepdims=True)
            var = jnp.var(x, axis=-1, keepdims=True)
            return (x - mu) * jax.lax.rsqrt(var + EPS) * gamma + beta
        B, T, C = x.shape
        h = layernorm(x, gamma1, beta1)
        Q = (h @ Wq + bq).reshape(B, T, N_HEADS, D_HEAD).transpose(0, 2, 1, 3)
        K = (h @ Wk + bk).reshape(B, T, N_HEADS, D_HEAD).transpose(0, 2, 1, 3)
        V = (h @ Wv + bv).reshape(B, T, N_HEADS, D_HEAD).transpose(0, 2, 1, 3)
        scores = jnp.einsum('bhqd,bhkd->bhqk', Q, K) / np.sqrt(D_HEAD)
        causal = jnp.tril(jnp.ones((T, T), dtype=bool))
        scores = jnp.where(causal, scores, -jnp.inf)
        attn = jax.nn.softmax(scores, axis=-1)
        ctx = jnp.einsum('bhqk,bhkd->bhqd', attn, V)
        ctx = ctx.transpose(0, 2, 1, 3).reshape(B, T, C)
        attn_out = ctx @ Wo + bo
        x1 = x + attn_out
        h2 = layernorm(x1, gamma2, beta2)
        ff = jax.nn.gelu(h2 @ W1 + b1, approximate=False) @ W2 + b2
        x2 = x1 + ff
        g = gate_score[:, None, None]
        return x + g * (x2 - x)

    def _L3_cond_ref(embeddings, theta, phi):
        import jax, jax.numpy as jnp
        import numpy as np
        B, N, D = embeddings.shape
        e = embeddings.reshape(B, N, D // 4, 4)
        ct = jnp.cos(theta)[:, None, None]
        st = jnp.sin(theta)[:, None, None]
        cp = jnp.cos(phi)[:, None, None]
        sp = jnp.sin(phi)[:, None, None]
        x0, x1, x2, x3 = (e[..., 0], e[..., 1], e[..., 2], e[..., 3])
        out = jnp.stack([x0 * ct + x1 * st, -x0 * st + x1 * ct, x2 * cp + x3 * sp, -x2 * sp + x3 * cp], axis=-1)
        return out.reshape(B, N, D)
    x = _L0_cond_ref(x, itok_B_6_14, L0_cond_ln_g, L0_cond_ln_b, L0_cond_subj_emb, L0_cond_hyp_w1, L0_cond_hyp_b1, L0_cond_hyp_w2, L0_cond_hyp_b2, L0_cond_sty_w1, L0_cond_sty_b1, L0_cond_sty_w2, L0_cond_sty_b2, L0_cond_router_w, L0_cond_exp_w1, L0_cond_exp_b1, L0_cond_exp_w2, L0_cond_exp_b2)
    x = _L1_cond_ref(x, L1_cond_A_grid, L1_cond_B_grid, condB_dt)
    x = _L2_cond_ref(x, condB_gatescore, L2_cond_Wq, L2_cond_bq, L2_cond_Wk, L2_cond_bk, L2_cond_Wv, L2_cond_bv, L2_cond_Wo, L2_cond_bo, L2_cond_W1, L2_cond_b1, L2_cond_W2, L2_cond_b2, L2_cond_gamma1, L2_cond_beta1, L2_cond_gamma2, L2_cond_beta2)
    x = _L3_cond_ref(x, condB_theta, condB_phi)
    return x

_drawn_inputs = setup_inputs


def setup_inputs(seed=0):
    import zlib

    import numpy as np

    out = dict(_drawn_inputs(seed))
    spreads = {'L0_cond_ln_g': (1.0, 0.6),
     'L0_cond_ln_b': (0.0, 0.8),
     'L0_cond_hyp_b1': (0.0, 0.1),
     'L0_cond_hyp_b2': (0.0, 0.1),
     'L0_cond_sty_b1': (0.0, 0.1),
     'L0_cond_sty_b2': (0.0, 0.1),
     'L0_cond_exp_b1': (0.0, 0.1),
     'L0_cond_exp_b2': (0.0, 0.1),
     'L2_cond_bq': (0.0, 0.468),
     'L2_cond_bk': (0.0, 0.8),
     'L2_cond_bv': (0.0, 0.1),
     'L2_cond_bo': (0.0, 0.1),
     'L2_cond_b1': (0.0, 0.1),
     'L2_cond_b2': (0.0, 0.1),
     'L2_cond_gamma1': (1.0, 0.2),
     'L2_cond_beta1': (0.0, 0.1),
     'L2_cond_gamma2': (1.0, 0.2),
     'L2_cond_beta2': (0.0, 0.1)}
    factors = {}
    for name, (base, spread) in spreads.items():
        noise = np.random.default_rng([zlib.crc32(name.encode()), seed]).standard_normal(out[name].shape)
        drawn = base * np.exp(spread * noise) if base else spread * noise
        out[name] = jnp.asarray(drawn.astype(out[name].dtype))
    for name, factor in factors.items():
        out[name] = (out[name] * factor).astype(out[name].dtype)
    return out
```

```python
from contextlib import ExitStack

import numpy as np

import concourse.bass as bass
from concourse import mybir

F32 = mybir.dt.float32
F32R = mybir.dt.float32r
BF16 = mybir.dt.bfloat16
I32 = mybir.dt.int32
U32 = mybir.dt.uint32
ALU = mybir.AluOpType
ACT = mybir.ActivationFunctionType
AX = mybir.AxisListType

P = 128
B, T, D = 32, 128, 128
GB = 4
NG = B // GB
GT = GB * T
E, FF = 8, 512
FT = FF // P
NH, DH = 16, 8
RG = 4
HJ = NH // RG
F_DVE = (1,)
F_ACT = (0, 2, 3)
NU = GB * RG
VW = DH + 1
LN_EPS, INORM_EPS = 1e-5, 1e-8
MASKED = -1.0e30
C_DT, C_GATE, C_COS, C_SIN, C_N = 0, 1, 2, 6, 10
TWO_PI_HI, TWO_PI_MID = 6.28125, 0.0019350051879882812
TWO_PI_LO = 2 * np.pi - 6.28125 - 0.0019350051879882812
ROUND = 12582912.0


def derivative_matrices(n):
    g, gg = np.zeros((n, n), np.float32), np.zeros((n, n), np.float32)
    for i in range(1, n - 1):
        g[i, i - 1], g[i, i + 1] = -0.5, 0.5
        gg[i, i - 1], gg[i, i], gg[i, i + 1] = 1, -2, 1
    g[0, :3], g[-1, -3:] = (-1.5, 2, -0.5), (0.5, -2, 1.5)
    gg[0, :4], gg[-1, -4:] = (2, -5, 4, -1), (-1, 4, -5, 2)
    return g, gg


R_B1 = 0
R_B2 = R_B1 + E * FT
R_LNG, R_LNB, R_HB1, R_HB2, R_SB1, R_SB2 = (R_B2 + E + i for i in range(6))
R_G1, R_BE1, R_G2, R_BE2 = (R_SB2 + 2 + i for i in range(4))
R_FB1 = R_BE2 + 1
R_N = R_FB1 + FT

N_ROW_LOADS, N_REST_LOADS, N_SPREAD, N_ANGLES, N_CONDS = 13, 24, 17, 16, 10

K_ID = 0
K_NEGID = K_ID + P
K_GX = K_NEGID + P
K_GXX = K_GX + P
K_MASK = K_GXX + P
K_MASKT = K_MASK + P
K_IOTA = K_MASKT + P
K_MQ, K_MK = K_IOTA + 1, K_IOTA + 2
K_E8 = K_IOTA + 3
K_GE = K_E8 + 8
K_AE = K_GE + 6
K_BE = K_AE + 8
K_N = K_BE + 8


def shape_constants():
    c = np.zeros((P, K_N), np.float32)
    g, gg = derivative_matrices(P)
    c[:, K_ID:K_ID + P] = np.eye(P)
    c[:, K_NEGID:K_NEGID + P] = -np.eye(P)
    c[:, K_GX:K_GX + P] = g.T
    c[:, K_GXX:K_GXX + P] = 0.5 * gg.T
    q, k = np.arange(P)[:, None], np.arange(P)[None, :]
    c[:, K_MASK:K_MASK + P] = np.where(k > q, MASKED, 0)
    c[:, K_MASKT:K_MASKT + P] = np.where(q > k, MASKED, 0)
    p = np.arange(P)
    c[:, K_IOTA] = p
    c[:, K_MQ] = (p // DH % 4) == 2
    c[:, K_MK] = (p // DH % 4) == 1
    c[:, K_E8:K_E8 + 8] = np.arange(8)
    c[:, K_GE:K_GE + 6] = (-3, 4, -1, 1, -4, 3)
    c[:, K_AE:K_AE + 8] = (1.5, -2, 0.5, 0, 0, -0.5, 2, -1.5)
    c[:, K_BE:K_BE + 8] = (1, -2.5, 2, -0.5, -0.5, 2, -2.5, 1)
    return c


class Signal:

    def __init__(self, sem, per):
        self.sem, self.per = sem, per

    def after(self, n, k=None):
        return n * self.per + (self.per if k is None else k)


def cond_seq_kernel(nc, a, out):
    with ExitStack() as ctx:
        def sb(name, shape, dt=F32):
            return ctx.enter_context(nc.sbuf_tensor(name, shape, dt))

        def bank(name):
            return ctx.enter_context(nc.psum_tensor(name, [P, 512], F32))

        def sem(name):
            return ctx.enter_context(nc.semaphore(name))

        def signal(name, per=1):
            return Signal(sem(name), per)

        def flat(t):
            return t[:].rearrange("p b d -> p (b d)")

        ps_hid = [bank("ps_hid0"), bank("ps_hid1")]
        ps_exp = bank("ps_exp")
        ps_pre = bank("ps_pre")
        ps_s = bank("ps_s")
        ps_x = [bank("ps_x0"), bank("ps_x1")]
        ps_c = bank("ps_c")

        cst = sb("cst", [P, K_N])
        ident = cst[:, K_ID:K_ID + P]
        negid = cst[:, K_NEGID:K_NEGID + P]
        id16 = sb("id16", [P, P], BF16)
        mask16 = sb("mask16", [P, P], BF16)
        maskT16 = sb("maskT16", [P, P], BF16)
        ones_r = sb("ones_r", [P, P], F32R)
        ones1 = sb("ones1", [1, 2])
        raw = sb("raw", [P, E * FF])

        def part(i, n=1):
            return raw[:, i * GT:(i + n) * GT]

        def part3(i):
            return part(i).rearrange("p (b d) -> p b d", b=GB)

        x2b, cx, x2a, xa2 = sb("x2b", [P, GB, D]), sb("cx", [P, GB, D]), sb("x2a", [P, GB, D]), sb("xa2", [P, GB, D])
        hn = sb("hn", [P, GT])
        w1h, w1l = sb("w1h", [P, E * FF], F32R), sb("w1l", [P, E * FF], F32R)
        w2 = sb("w2", [P, E, FT, D])
        rw = sb("rw", [P, E])
        rows = sb("rows", [R_N, P])
        cols = sb("cols", [P, R_N])
        wq_raw, wk_raw = sb("wq_raw", [P, D]), sb("wk_raw", [P, D])
        bq_row, bk_row = sb("bq_row", [1, D]), sb("bk_row", [1, D])
        wqe, wke = flat(cx), flat(xa2)
        bqe, bke = flat(x2b)[0:1, :], hn[0:1, :]
        wqh, wql = sb("wqh", [P, HJ * P], F32R), sb("wql", [P, HJ * P], F32R)
        wkh, wkl = sb("wkh", [P, HJ * P], F32R), sb("wkl", [P, HJ * P], F32R)
        qk_b = sb("qk_b", [P, 2, HJ])
        qk_mb = sb("qk_mb", [P, 2, HJ])
        wv_raw = sb("wv_raw", [P, D])
        wvh, wvl = sb("wvh", [P, D], F32R), sb("wvl", [P, D], F32R)
        wo = sb("wo", [P, D])
        f1_raw = flat(x2a)
        f1h, f1l = sb("f1h", [P, FF], F32R), sb("f1l", [P, FF], F32R)
        f2 = sb("f2", [P, FT, D])
        bv_b, bo_b, fb2_b = sb("bv_b", [P, D]), sb("bo_b", [P, D]), sb("fb2_b", [P, D])
        subj = sb("subj", [32, 64])
        hw1, hw2 = sb("hw1", [64, P]), sb("hw2", [P, P])
        sw1, sw2 = sb("sw1", [P, 64]), sb("sw2", [64, 2 * D])
        ln_eps, inorm_eps = sb("ln_eps", [P, GB]), sb("inorm_eps", [P, GB])
        carrier = sb("carrier", [P, 1])
        ag, bg = sb("ag", [P, 2, P]), sb("bg", [P, 3, P])
        g_p, g_m, g_b2 = sb("g_p", [P, P]), sb("g_m", [P, P]), sb("g_b2", [P, P])
        g_edge, edge_t = sb("g_edge", [P, 2, 4]), sb("edge_t", [P, 2, 4])
        ids_i, ids_f, onehot = sb("ids_i", [32, B], I32), sb("ids_f", [32, B]), sb("onehot", [32, B])
        se, hyp1, hyp2, sty1 = sb("se", [64, B]), sb("hyp1", [P, B]), sb("hyp2", [P, B]), sb("sty1", [64, B])
        style = sb("style", [P, 2, B])
        sp_a, sp_b, sp_c = sb("sp_a", [P, B]), sb("sp_b", [P, B]), sb("sp_c", [P, B])
        cond_in = sb("cond_in", [P, 4, B])
        ang, ang_k, ang_r = sb("ang", [P, 4, B]), sb("ang_k", [P, 4, B]), sb("ang_r", [P, 4, B])
        cond = sb("cond", [P, B, C_N])
        neg_half = sb("neg_half", [P, GB])

        xa = sb("xa", [P, GB, D])
        xn0, xn = sb("xn0", [P, GB, D]), sb("xn", [P, GB, D])
        h_aff, h32 = sb("h_aff", [P, GT]), sb("h32", [P, GT])
        hh = [sb("hh0", [P, GT], F32R), sb("hh1", [P, GT], F32R)]
        hl = [sb("hl0", [P, GT], F32R), sb("hl1", [P, GT], F32R)]
        st0, mv0, rs0 = sb("st0", [P, GB, 6]), sb("mv0", [P, GB, 2]), sb("rs0", [P, GB])
        sti, mvi, rsi = sb("sti", [P, GB, 6]), sb("mvi", [P, GB, 2]), sb("rsi", [P, GB])
        stn, mvn, rsn = sb("stn", [P, GB, 6]), sb("mvn", [P, GB, 2]), sb("rsn", [P, GB])
        in_s, in_ms, in_t = sb("in_s", [P, GB]), sb("in_ms", [P, GB]), sb("in_t", [P, GB])
        ve0, vei, ven = sb("ve0", [P, GB]), sb("vei", [P, GB]), sb("ven", [P, GB])
        sty_g = sb("sty_g", [P, 2, GB])
        lg, top, top_i = sb("lg", [P, GB, E]), sb("top", [P, GB, 8]), sb("top_i", [P, GB, 8], U32)
        top_f = sb("top_f", [P, 2, GB])
        gap, gexp, gsum, gates = sb("gap", [P, GB]), sb("gexp", [P, GB]), sb("gsum", [P, GB]), sb("gates", [P, 2, GB])
        pick = sb("pick", [P, 2, GB, E])
        comb = sb("comb", [P, GB, E])
        comb_t = sb("comb_t", [E, GT])
        gate_rows = nc.dram_tensor("gate_rows", (2, E, GT), F32).ap()
        comb_b = [sb("comb_b0", [P, GT]), sb("comb_b1", [P, GT])]

        hid = [sb("hid0", [P, FT, GT]), sb("hid1", [P, FT, GT])]
        gated = [sb("gated0", [P, GT]), sb("gated1", [P, GT])]
        y_t = [sb("y_t0", [P, GT]), sb("y_t1", [P, GT])]

        xb = sb("xb", [P, GB, D])
        f = sb("f", [P, GB, D])
        rb, u_, ua, v_, w_, wp, wm, bf = (part3(i) for i in range(8))
        eu, ew = sb("eu", [P, GB, 2, 3]), sb("ew", [P, GB, 2, 4])
        df, fn, x1in = rb, wp, sb("x1in", [P, GB, D])
        cond_g = sb("cond_g", [P, GB, C_N])
        hnh, hnl = sb("hnh", [P, GT], F32R), sb("hnl", [P, GT], F32R)
        lo_part = [part(1).bitcast(F32R), part(2).bitcast(F32R)]
        qs, ks = sb("qs", [P, HJ, GB, T], F32R), sb("ks", [P, HJ, GB, T], F32R)
        vs = sb("vs", [P, GB, NH, VW])
        mx = [sb("mx0", [P, HJ]), sb("mx1", [P, HJ])]
        dg = [sb("dg0", [P, HJ, T], F32R), sb("dg1", [P, HJ, T], F32R)]
        pt = [part3(4), part3(5)]
        rden = sb("rden", [P, RG, HJ])
        cxt, xa1, res = hn, cx, x2b
        gl = part(0, FT).rearrange("p (j t) -> p j t", j=FT)
        t1, t2, fin = part3(6), part3(7), sb("fin", [P, GB, D])

        cst_in, w1_in, w2_in, rest_in, rows_in = sem("cst_in"), sem("w1_in"), sem("w2_in"), sem("rest_in"), sem("rows_in")
        rows_zero, halves = sem("rows_zero"), sem("halves")
        cols_ps, cols_done = sem("cols_ps"), sem("cols_done")
        hot_step, se_ps, se_done = sem("hot_step"), sem("se_ps"), sem("se_done")
        hyp1_ps, hyp1_done, hyp2_ps, hyp2_done = sem("hyp1_ps"), sem("hyp1_done"), sem("hyp2_ps"), sem("hyp2_done")
        sty1_ps, sty1_done, style_ps, style_done = sem("sty1_ps"), sem("sty1_done"), sem("style_ps"), sem("style_done")
        soft_v, soft_a = sem("soft_v"), sem("soft_a")
        spread, bias_ps, bias_done, split_w = sem("spread"), sem("bias_ps"), sem("bias_done"), sem("split_w")
        w1_split = sem("w1_split")
        grids, angles, sines, conds, masks = sem("grids"), sem("angles"), sem("sines"), sem("conds"), sem("masks")
        xa_in = signal("xa_in", 16)
        ln0_stats, ln0_mv = signal("ln0_stats", GB), signal("ln0_mv", GB)
        ln0_ve, ln0_rs, ln0_xn = signal("ln0_ve"), signal("ln0_rs"), signal("ln0_xn")
        xn0_t = signal("xn0_t")
        haff = signal("haff")
        in_stats, in_mv, in_ve, in_rs = signal("in_stats", GB), signal("in_mv", GB), signal("in_ve"), signal("in_rs")
        in_styled, in_step, in_coef = signal("in_styled"), signal("in_step", 2), signal("in_coef")
        h32_done, hh_done, h_split = signal("h32_done"), signal("hh_done"), signal("h_split")
        logits = signal("logits")
        lg_copied, topped, topi_done = signal("lg_copied"), signal("topped", GB), signal("topi_done")
        gap_done, gap_exp, gate_step = signal("gap_done"), signal("gap_exp"), signal("gate_step", 7)
        comb_done, comb_tp, comb_ct, comb_rowed = signal("comb_done"), signal("comb_tp"), signal("comb_ct"), signal("comb_rowed", 16)
        comb_bc = [signal("comb_bc0", 16 * E // 2), signal("comb_bc1", 16 * E // 2)]
        hid_ps = signal("hid_ps", E * FT)
        hid_act, hid_dve = signal("hid_act", E * (FT - len(F_DVE))), signal("hid_dve", E * len(F_DVE))
        exp_ps = signal("exp_ps", E)
        gated_done, y_added = signal("gated_done", E), signal("y_added", E - 1)
        xb_in = signal("xb_in", 16)
        y_back, f_done = signal("y_back"), signal("f_done")
        cond_ready = signal("cond_ready")
        pde_pool = signal("pde_pool", 3)
        pde_v = signal("pde_v", 10)
        u_done, pde_ps, w_done = signal("u_done"), signal("pde_ps"), signal("w_done")
        df_done, fn_done, x1in_done = signal("df_done"), signal("fn_done", GB), signal("x1in_done")
        ln_stats = [signal("ln1_stats", GB), signal("ln2_stats", GB)]
        ln_mv = [signal("ln1_mv", GB), signal("ln2_mv", GB)]
        ln_ve = [signal("ln1_ve"), signal("ln2_ve")]
        ln_rs = [signal("ln1_rs"), signal("ln2_rs")]
        ln_xn = [signal("ln1_xn"), signal("ln2_xn")]
        xn_t = [signal("xn1_t"), signal("xn2_t")]
        hn_done = [signal("hn1_done"), signal("hn2_done")]
        hnh_done = [signal("hnh1_done"), signal("hnh2_done")]
        hn_split = [signal("hn1_split"), signal("hn2_split")]
        qk_ps, qk_lo, qk_done = signal("qk_ps", 2 * HJ), signal("qk_lo", 2 * HJ), signal("qk_done", 2 * HJ)
        v_ps, v_done = signal("v_ps"), signal("v_done")
        s_ps, mx_done, dg_done = signal("s_ps", NU), signal("mx_done", NU), signal("dg_done", NU)
        x_ps, exp_done, pv_done = signal("x_ps", NU), signal("exp_done", NU), signal("pv_done", NU)
        rden_done, cx_done = signal("rden_done", GB), signal("cx_done", GB)
        cx_t, cxt_done = signal("cx_t"), signal("cxt_done")
        wo_ps, xa1_done, xa2_done = signal("wo_ps"), signal("xa1_done"), signal("xa2_done")
        f1_ps, gelu_done, f2_ps = signal("f1_ps", FT), signal("gelu_done", FT), signal("f2_ps")
        x2a_done, x2b_done, delta_done, res_done = signal("x2a_done"), signal("x2b_done"), signal("delta_done"), signal("res_done", GB)
        rot_step, rotated, stored = signal("rot_step", 3), signal("rotated"), signal("stored", 16)

        def await_(eng, sig, n, k=None):
            if isinstance(n, int) and n < 0:
                return
            eng.wait_ge(sig.sem, sig.after(n, k))

        def apart(eng):
            eng.memset(carrier[:], 0.0)

        def bc(ap, n):
            return ap.unsqueeze(1).broadcast_to([ap.shape[0], n, ap.shape[1]])

        def inner(ap, n):
            return ap.unsqueeze(2).broadcast_to([ap.shape[0], ap.shape[1], n])

        def col(r):
            return cols[:, r:r + 1]

        def free_hidden(eng, n, e):
            if e >= 2:
                await_(eng, exp_ps, n, e - 1)
            else:
                await_(eng, exp_ps, n - 1, E - 1 + e)

        def iterations(eng, emit):
            emit(0, 0, back=False, experts=True, pre=True)
            with eng.Fori(0, (NG - 2) // 2) as i:
                for u in range(2):
                    emit(i * 2 + 1 + u, (1 + u) % 2, back=True, experts=True, pre=True)
            emit(NG - 1, (NG - 1) % 2, back=True, experts=True, pre=False)
            emit(NG, NG % 2, back=True, experts=False, pre=False)

        def broadcast_gates(eng, n, p, e):
            if e == 0:
                await_(eng, comb_rowed, n)
            if e >= 2:
                await_(eng, gated_done, n, e - 1)
            else:
                await_(eng, gated_done, n - 1, E - 1 + e)
            eng.dma_start(comb_b[e % 2][:], gate_rows[p, e].partition_broadcast(P)).then_inc(comb_bc[e % 2].sem, 16)

        block = ctx.enter_context(nc.Block())

        @block.sync
        def _(sp):
            def load(dst, src, sem_):
                sp.dma_start(dst, src).then_inc(sem_, 16)

            def load_xa(n):
                first = first_batch(n)
                if not (isinstance(n, int) and n == 0):
                    await_(sp, ln0_xn, n - 1)
                load(xa[:], x_grp(first), xa_in.sem)

            def load_xb(n):
                first = first_batch(n)
                if not (isinstance(n, int) and n == 0):
                    await_(sp, f_done, n - 1)
                load(xb[:], x_grp(first), xb_in.sem)

            def first_batch(n):
                return n * GB if isinstance(n, int) else sp.snap(n * GB)

            def x_grp(first):
                return a["x"][bass.ds(first, GB), :, :].rearrange("b t d -> t b d")

            load_xa(0)
            load(cst[:], a["cst"], cst_in)
            load(ids_i[:], a["itok_B_6_14"].partition_broadcast(32), rest_in)
            load(subj[:], a["L0_cond_subj_emb"], rest_in)
            load(hw1[:], a["L0_cond_hyp_w1"], rest_in)
            load(hw2[:], a["L0_cond_hyp_w2"], rest_in)
            load(sw1[:], a["L0_cond_sty_w1"], rest_in)
            load(sw2[:], a["L0_cond_sty_w2"], rest_in)
            load(rw[:], a["L0_cond_router_w"], rest_in)
            sp.wait_ge(rows_zero, 1)
            load(rows[R_B1:R_B1 + E * FT, :], a["L0_cond_exp_b1"].rearrange("e (t p) -> (e t) p", p=P), rows_in)
            load(rows[R_B2:R_B2 + E, :], a["L0_cond_exp_b2"], rows_in)
            for r, name in ((R_LNG, "L0_cond_ln_g"), (R_LNB, "L0_cond_ln_b"), (R_HB1, "L0_cond_hyp_b1"),
                            (R_HB2, "L0_cond_hyp_b2"), (R_G1, "L2_cond_gamma1"), (R_BE1, "L2_cond_beta1"),
                            (R_G2, "L2_cond_gamma2"), (R_BE2, "L2_cond_beta2")):
                load(rows[r:r + 1, :], a[name].unsqueeze(0), rows_in)
            load(rows[R_SB1:R_SB1 + 1, 0:64], a["L0_cond_sty_b1"].unsqueeze(0), rows_in)
            load(rows[R_SB2:R_SB2 + 2, :], a["L0_cond_sty_b2"].rearrange("(r p) -> r p", p=P), rows_in)
            load(rows[R_FB1:R_FB1 + FT, :], a["L2_cond_b1"].rearrange("(r p) -> r p", p=P), rows_in)
            for i, name in enumerate(("condB_dt", "condB_gatescore", "condB_theta", "condB_phi")):
                load(cond_in[:, i, :], a[name].partition_broadcast(P), rest_in)
            load(ag[:], a["L1_cond_A_grid"].rearrange("c x y -> x c y"), rest_in)
            load(bg[:], a["L1_cond_B_grid"].rearrange("c x y -> x c y"), rest_in)
            for dst, name in ((wq_raw, "L2_cond_Wq"), (wk_raw, "L2_cond_Wk"), (wv_raw, "L2_cond_Wv"),
                              (wo, "L2_cond_Wo"), (f1_raw, "L2_cond_W1")):
                load(dst[:], a[name], rest_in)
            load(f2[:], a["L2_cond_W2"].rearrange("(t p) d -> p t d", p=P), rest_in)
            load(bq_row[:], a["L2_cond_bq"].unsqueeze(0), rest_in)
            load(bk_row[:], a["L2_cond_bk"].unsqueeze(0), rest_in)
            for dst, name in ((bv_b, "L2_cond_bv"), (bo_b, "L2_cond_bo"), (fb2_b, "L2_cond_b2")):
                load(dst[:], a[name].partition_broadcast(P), rest_in)
            load_xb(0)

            def rows_of_gates(n, p):
                await_(sp, comb_ct, n)
                load(gate_rows[p], comb_t[:], comb_rowed.sem)

            def store(n):
                first = first_batch(n)
                await_(sp, rotated, n)
                sp.dma_start(out[bass.ds(first, GB), :, :].rearrange("b t d -> t b d"),
                             fin[:]).then_inc(stored.sem, 16)

            rows_of_gates(0, 0)
            def emit(g, p, back, experts, pre):
                if pre:
                    load_xa(g + 1)
                for e in range(1, E):
                    if experts and e == 2:
                        await_(sp, comb_rowed, g)
                    if experts and e >= 2:
                        broadcast_gates(sp, g, p, e)
                    if e == 3 and back and experts:
                        load_xb(g)
                    if e == 4 and pre:
                        rows_of_gates(g + 1, 1 - p)
                if back:
                    store(g - 1)

            iterations(sp, emit)
            await_(sp, stored, NG - 1)

        @block.scalar
        def _(act):
            for e in range(E):
                act.dma_start(raw[:, e * FF:(e + 1) * FF], a["L0_cond_exp_w1"][e]).then_inc(w1_in, 16)
            for e in range(E):
                act.dma_start(w2[:, e], a["L0_cond_exp_w2"][e].rearrange("(t p) d -> p t d", p=P)).then_inc(w2_in, 16)

            act.wait_ge(angles, N_ANGLES)
            act.activation(ang[:], ang_r[:], ACT.Sin).then_inc(sines, 1)
            act.wait_ge(cols_ps, 1)
            act.activation(cols[:], ps_s[:, 0:R_N], ACT.Identity).then_inc(cols_done, 1)
            act.wait_ge(cols_done, 1)
            act.wait_ge(hyp1_ps, 1)
            act.activation(hyp1[:], ps_x[1][:, 0:B], ACT.Relu, bias=col(R_HB1)).then_inc(hyp1_done, 1)
            act.wait_ge(hyp2_ps, 1)
            act.activation(hyp2[:], ps_c[:, 0:B], ACT.Identity, bias=col(R_HB2)).then_inc(hyp2_done, 1)
            act.wait_ge(sty1_ps, 1)
            act.activation(sty1[:], ps_hid[0][0:64, 0:B], ACT.Relu,
                           bias=cols[0:64, R_SB1:R_SB1 + 1]).then_inc(sty1_done, 1)
            act.wait_ge(style_ps, 2)
            act.activation(sp_a[:], ps_hid[1][:, 0:B], ACT.Identity, bias=col(R_SB2)).then_inc(style_done, 1)
            act.activation(style[:, 1, :], ps_exp[:, 0:B], ACT.Identity, bias=col(R_SB2 + 1)).then_inc(style_done, 1)
            act.wait_ge(soft_v, 1)
            act.activation(sp_c[:], sp_b[:], ACT.Exp).then_inc(soft_a, 1)
            act.wait_ge(soft_a, 1)
            act.activation(sp_b[:], sp_c[:], ACT.Ln, bias=1.0).then_inc(soft_a, 1)

            def affine(n):
                await_(act, xn0_t, n)
                await_(act, in_coef, n - 1)
                await_(act, h32_done, n - 1)
                act.activation(h_aff[:], ps_pre[:], ACT.Identity, bias=col(R_LNB), scale=col(R_LNG)).then_inc(haff.sem, 1)

            def gap_exponential(n):
                await_(act, gap_done, n)
                act.activation(gexp[:], gap[:], ACT.Exp).then_inc(gap_exp.sem, 1)

            def gates_out(n):
                await_(act, comb_tp, n)
                await_(act, comb_rowed, n - 1)
                act.activation(comb_t[:], ps_pre[0:E, :], ACT.Identity).then_inc(comb_ct.sem, 1)

            def relu(n, e, j):
                await_(act, hid_ps, n, e * FT + j + 1)
                free_hidden(act, n, e)
                act.activation(hid[e % 2][:, j, :], ps_hid[j % 2][:], ACT.Relu,
                               bias=col(R_B1 + e * FT + j)).then_inc(hid_act.sem, 1)

            def layernorm_affine(n, which):
                await_(act, xn_t[which], n)
                act.activation(hn[:], ps_c[:], ACT.Identity, bias=col(R_BE1 + 2 * which),
                               scale=col(R_G1 + 2 * which)).then_inc(hn_done[which].sem, 1)

            def qk_low(n, j, which):
                await_(act, qk_ps, n, 2 * j + which + 1)
                if j >= 1:
                    await_(act, qk_done, n, 2 * j - 1 + which)
                act.activation(lo_part[which][:], ps_x[which][:], ACT.Identity, bias=qk_mb[:, which, j:j + 1],
                               scale=cst[:, K_MQ + which:K_MQ + which + 1]).then_inc(qk_lo.sem, 1)

            def exponential(n, u):
                await_(act, x_ps, n, u + 1)
                if u >= 2:
                    await_(act, pv_done, n, u - 1)
                act.activation(flat(pt[u % 2]), ps_x[u % 2][:], ACT.Exp).then_inc(exp_done.sem, 1)

            def context_out(n):
                await_(act, cx_t, n)
                act.activation(cxt[:], ps_c[:], ACT.Identity).then_inc(cxt_done.sem, 1)

            def gelu(n, j):
                await_(act, f1_ps, n, j + 1)
                act.activation(gl[:, j, :], ps_x[j % 2][:], ACT.Gelu, bias=col(R_FB1 + j)).then_inc(gelu_done.sem, 1)

            def emit(g, p, back, experts, pre):
                n, m = g - 1, g + 1
                for s in range(E):
                    for j in range(FT):
                        at = s * FT + j
                        if experts and at == 1:
                            broadcast_gates(act, g, p, 1)
                        if experts and j in F_ACT:
                            relu(g, s, j)
                        if pre:
                            if at == 5:
                                affine(m)
                            if at == 12:
                                gap_exponential(m)
                            if at == 14:
                                gates_out(m)
                        if back:
                            if at == 11:
                                layernorm_affine(n, 0)
                            if 13 <= at < 17:
                                qk_low(n, at - 13, 0)
                                qk_low(n, at - 13, 1)
                            for u in range(NU):
                                if at == 17 + (u + 1) // 2:
                                    exponential(n, u)
                            if at == 26:
                                context_out(n)
                            if at == 29:
                                layernorm_affine(n, 1)
                if pre:
                    broadcast_gates(act, m, 1 - p, 0)
                if back:
                    for j in range(FT):
                        gelu(n, j)

            affine(0)
            gap_exponential(0)
            gates_out(0)
            broadcast_gates(act, 0, 0, 0)
            iterations(act, emit)

        @block.tensor
        def _(pe):
            def three(o, wh, wl, xh, xl, start=True):
                pe.matmul(o, wh, xh, start=start, stop=False)
                pe.matmul(o, wh, xl, start=False, stop=False)
                return pe.matmul(o, wl, xh, start=False, stop=True)

            pe.wait_ge(cst_in, 16)
            pe.wait_ge(rows_in, 16 * N_ROW_LOADS)
            pe.transpose(ps_s[:, 0:R_N], rows[:], ident[0:R_N, 0:R_N]).then_inc(cols_ps, 1)
            pe.wait_ge(rest_in, 16 * N_REST_LOADS)
            pe.wait_ge(hot_step, 2)
            pe.matmul(ps_x[0][0:64, 0:B], subj[:], onehot[:], start=True, stop=True).then_inc(se_ps, 1)
            pe.wait_ge(se_done, 1)
            pe.matmul(ps_x[1][:, 0:B], hw1[:], se[:], start=True, stop=True).then_inc(hyp1_ps, 1)
            pe.wait_ge(hyp1_done, 1)
            pe.matmul(ps_c[:, 0:B], hw2[:], hyp1[:], start=True, stop=True).then_inc(hyp2_ps, 1)
            pe.wait_ge(hyp2_done, 1)
            pe.matmul(ps_hid[0][0:64, 0:B], sw1[:], hyp2[:], start=True, stop=True).then_inc(sty1_ps, 1)
            pe.wait_ge(sty1_done, 1)
            pe.matmul(ps_hid[1][:, 0:B], sw2[:, 0:D], sty1[:], start=True, stop=True).then_inc(style_ps, 1)
            pe.matmul(ps_exp[:, 0:B], sw2[:, D:2 * D], sty1[:], start=True, stop=True).then_inc(style_ps, 1)
            pe.wait_ge(spread, N_SPREAD)
            for which, row in enumerate((bqe, bke)):
                for j in range(HJ):
                    mm = pe.matmul(ps_pre[:, which * HJ + j:which * HJ + j + 1], row[:, j * P:(j + 1) * P],
                                   ones1[:, 0:1], start=True, stop=True)
            mm.then_inc(bias_ps, 1)
            pe.wait_ge(bias_done, 2)
            pe.wait_ge(style_done, 2)
            pe.wait_ge(masks, 4)

            def pre_transpose(n):
                await_(pe, ln0_xn, n)
                await_(pe, comb_ct, n - 1)
                for b in range(GB):
                    mm = pe.transpose(ps_pre[:, b * T:(b + 1) * T], xn[:, b, :], ident)
                mm.then_inc(xn0_t.sem, 1)

            def router(n):
                await_(pe, h32_done, n)
                await_(pe, haff, n)
                for b in range(GB):
                    mm = pe.matmul(ps_pre[:, b * E:(b + 1) * E], h32[:, b * T:(b + 1) * T], rw[:],
                                   start=True, stop=True)
                mm.then_inc(logits.sem, 1)

            def gates_transpose(n):
                await_(pe, comb_done, n)
                await_(pe, lg_copied, n)
                for b in range(GB):
                    mm = pe.transpose(ps_pre[0:E, b * T:(b + 1) * T], comb[:, b, :], ident)
                mm.then_inc(comb_tp.sem, 1)

            def hidden(n, p, e, j):
                if e == 0 and j == 0:
                    await_(pe, h_split, n)
                if isinstance(n, int) and n == 0 and j == 0:
                    pe.wait_ge(w1_split, 2 * (e + 1))
                evicted(pe, n, e, j - 2)
                w = slice(e * FF + j * P, e * FF + (j + 1) * P)
                three(ps_hid[j % 2][:], w1h[:, w], w1l[:, w], hh[p][:], hl[p][:]).then_inc(hid_ps.sem, 1)

            def evicted(eng, n, e, j):
                if j < 0:
                    e, j = e - 1, j + FT
                if e < 0:
                    n, e = n - 1, E - 1
                fs, sig = (F_DVE, hid_dve) if j in F_DVE else (F_ACT, hid_act)
                await_(eng, sig, n, e * len(fs) + fs.index(j) + 1)

            def expert_out(n, e):
                if isinstance(n, int) and n == 0:
                    pe.wait_ge(w2_in, 16 * E)
                if e >= 1:
                    await_(pe, gated_done, n, e)
                else:
                    await_(pe, gated_done, n - 1)
                for j in range(FT):
                    evicted(pe, n, e, j)
                    mm = pe.matmul(ps_exp[:], w2[:, e, j, :], hid[e % 2][:, j, :], start=(j == 0), stop=(j == FT - 1))
                mm.then_inc(exp_ps.sem, 1)

            def y_transpose(n, p):
                await_(pe, y_added, n)
                for b in range(GB):
                    mm = pe.transpose(ps_c[:, b * D:(b + 1) * D], y_t[p][:, b * T:(b + 1) * T], ident)
                mm.then_inc(y_back.sem, 1)

            def pde_rows(n):
                await_(pe, u_done, n)
                await_(pe, pde_pool, n, 2)
                pe.matmul(ps_s[:], cst[:, K_GX:K_GX + P], flat(u_), start=True, stop=False)
                pe.matmul(ps_s[:], cst[:, K_GXX:K_GXX + P], flat(v_), start=False, stop=True).then_inc(pde_ps.sem, 1)

            def norm_transpose(n, which):
                await_(pe, ln_xn[which], n)
                await_(pe, (f_done, cxt_done)[which], n)
                for b in range(GB):
                    mm = pe.transpose(ps_c[:, b * T:(b + 1) * T], xn0[:, b, :], ident)
                mm.then_inc(xn_t[which].sem, 1)

            def project_v(n):
                await_(pe, hn_split[0], n)
                for b in range(GB):
                    t = slice(b * T, (b + 1) * T)
                    mm = three(ps_c[:, b * D:(b + 1) * D], hnh[:, t], hnl[:, t], wvh[:], wvl[:])
                mm.then_inc(v_ps.sem, 1)

            def project_qk(n, j):
                for which, (wh, wl) in enumerate(((wqh, wql), (wkh, wkl))):
                    if j >= 1:
                        await_(pe, qk_done, n, 2 * j - 1 + which)
                    w = slice(j * P, (j + 1) * P)
                    three(ps_x[which][:], wh[:, w], wl[:, w], hnh[:], hnl[:]).then_inc(qk_ps.sem, 1)

            def head_scores(o, lhs, rhs, b, i):
                r = slice(32 * i, 32 * i + 32)
                for j in range(HJ):
                    mm = pe.matmul(o[:, j * T:(j + 1) * T], lhs[r, j, b, :], rhs[r, j, b, :],
                                   start=False, stop=(j == HJ - 1), skip_group_check=True)
                return mm

            def scores(n, u):
                b, i = divmod(u, RG)
                if u == 0:
                    await_(pe, df_done, n)
                    await_(pe, qk_done, n)
                else:
                    await_(pe, mx_done, n, u)
                pe.matmul(ps_s[:], id16[:], bc(mask16[:], HJ), start=True, stop=False, skip_group_check=True)
                head_scores(ps_s, qs, ks, b, i).then_inc(s_ps.sem, 1)

            def scores_less_max(n, u):
                b, i = divmod(u, RG)
                if u >= 2:
                    await_(pe, exp_done, n, u - 1)
                o = ps_x[u % 2]
                pe.matmul(o[:], id16[:], bc(maskT16[:], HJ), start=True, stop=False, skip_group_check=True)
                head_scores(o, ks, qs, b, i)
                await_(pe, dg_done, n, u + 1)
                pe.matmul(o[:], ones_r[:], flat(dg[u % 2]), start=False, stop=True,
                          skip_group_check=True).then_inc(x_ps.sem, 1)

            def weighted_values(n, u):
                b, i = divmod(u, RG)
                await_(pe, exp_done, n, u + 1)
                if u == 0:
                    await_(pe, v_done, n)
                elif i == 0:
                    await_(pe, cx_done, n, b)
                for j in range(HJ):
                    c = (i * HJ + j) * VW
                    mm = pe.matmul(ps_c[:, c:c + VW], pt[u % 2][:, j, :], vs[:, b, j * RG + i, :], start=True, stop=True)
                mm.then_inc(pv_done.sem, 1)

            def context_transpose(n):
                await_(pe, cx_done, n)
                for b in range(GB):
                    mm = pe.transpose(ps_c[:, b * T:(b + 1) * T], cx[:, b, :], ident)
                mm.then_inc(cx_t.sem, 1)

            def project_out(n):
                await_(pe, cxt_done, n)
                await_(pe, mx_done, n)
                for b in range(GB):
                    mm = pe.matmul(ps_s[:, b * D:(b + 1) * D], cxt[:, b * T:(b + 1) * T], wo[:], start=True, stop=True)
                mm.then_inc(wo_ps.sem, 1)

            def ffn_hidden(n, j):
                if j == 0:
                    await_(pe, hn_split[1], n)
                if j < 2:
                    await_(pe, exp_done, n, NU - 1 + j)
                else:
                    await_(pe, gelu_done, n, j - 1)
                w = slice(j * P, (j + 1) * P)
                three(ps_x[j % 2][:], f1h[:, w], f1l[:, w], hnh[:], hnl[:]).then_inc(f1_ps.sem, 1)

            def ffn_out(n):
                await_(pe, gelu_done, n)
                await_(pe, xa1_done, n)
                for b in range(GB):
                    for j in range(FT):
                        mm = pe.matmul(ps_s[:, b * D:(b + 1) * D], gl[:, j, b * T:(b + 1) * T], f2[:, j, :],
                                       start=(j == 0), stop=(j == FT - 1))
                mm.then_inc(f2_ps.sem, 1)

            def attention_step(n, k):
                if k < NU:
                    scores(n, k)
                if 1 <= k <= NU:
                    scores_less_max(n, k - 1)
                if k >= 2:
                    weighted_values(n, k - 2)

            def emit(g, p, back, experts, pre):
                n, m = g - 1, g + 1
                for s in range(E):
                    for j in range(FT):
                        at = s * FT + j
                        if experts:
                            if j == 2 and s >= 1:
                                expert_out(g, s - 1)
                            hidden(g, p, s, j)
                        if pre:
                            if at == 4:
                                pre_transpose(m)
                            if at == 9:
                                router(m)
                            if at == 13:
                                gates_transpose(m)
                        if back:
                            if at == 1:
                                y_transpose(n, 1 - p)
                            if at == 7:
                                pde_rows(n)
                            if at == 11:
                                norm_transpose(n, 0)
                            if at == 13:
                                project_v(n)
                            if 13 <= at < 17:
                                project_qk(n, at - 13)
                            if 17 <= at < 26:
                                attention_step(n, 2 * (at - 17))
                                attention_step(n, 2 * (at - 17) + 1)
                            if at == 26:
                                context_transpose(n)
                            if at == 27:
                                project_out(n)
                            if at == 29:
                                norm_transpose(n, 1)
                if back:
                    for j in range(FT):
                        ffn_hidden(n, j)
                if experts:
                    expert_out(g, E - 1)
                if back:
                    ffn_out(n)

            pre_transpose(0)
            router(0)
            gates_transpose(0)
            iterations(pe, emit)

        @block.vector
        def _(dve):
            V = nc.vector
            dve.wait_ge(cst_in, 16)
            dve.wait_ge(rest_in, 16 * N_REST_LOADS)
            V.tensor_copy(ids_f[:], ids_i[:]).then_inc(hot_step, 1)
            dve.wait_ge(hot_step, 1)
            V.tensor_scalar(onehot[:], ids_f[:], cst[0:32, K_IOTA:K_IOTA + 1], None, ALU.is_equal).then_inc(hot_step, 1)
            k = 0
            for dst, src, scale in ((wqe, wq_raw, DH ** -0.5), (wke, wk_raw, 1.0), (bqe, bq_row, DH ** -0.5), (bke, bk_row, 1.0)):
                V.memset(dst[:], 0.0).then_inc(spread, 1)
                k += 1
                dve.wait_ge(spread, k)
                for r in range(3):
                    V.tensor_scalar(dst[:].rearrange("p (h r d) -> p r h d", r=4, d=DH)[:, r],
                                    src[:].rearrange("p (h d) -> p h d", d=DH), scale, None, ALU.mult).then_inc(spread, 1)
                    k += 1
            V.memset(ones1[:], 1.0).then_inc(spread, 1)
            assert k + 1 == N_SPREAD
            dve.wait_ge(spread, N_SPREAD)
            dve.wait_ge(se_ps, 1)
            V.tensor_copy(se[:], ps_x[0][0:64, 0:B]).then_inc(se_done, 1)
            k = 0

            def step(ins):
                nonlocal k
                k += 1
                ins.then_inc(angles, 1)
                dve.wait_ge(angles, k)

            for quarter in range(2):
                c = slice(2 * quarter, 2 * quarter + 2)
                step(V.tensor_scalar(ang_k[:, c], cond_in[:, 2:4, :], 1 / (2 * np.pi), 0.25 * quarter, ALU.mult, ALU.add))
                step(V.tensor_scalar(ang_r[:, c], ang_k[:, c], ROUND, None, ALU.add))
                step(V.tensor_scalar(ang_k[:, c], ang_r[:, c], ROUND, None, ALU.subtract))
                step(V.scalar_tensor_tensor(ang_r[:, c], ang_k[:, c], -TWO_PI_HI, cond_in[:, 2:4, :], ALU.mult, ALU.add))
                step(V.scalar_tensor_tensor(ang_r[:, c], ang_k[:, c], -TWO_PI_MID, ang_r[:, c], ALU.mult, ALU.add))
                step(V.scalar_tensor_tensor(ang_r[:, c], ang_k[:, c], -TWO_PI_LO, ang_r[:, c], ALU.mult, ALU.add))
                step(V.tensor_scalar(ang_r[:, c], ang_r[:, c], 0.5 * np.pi * quarter, 3.1415925, ALU.add, ALU.min))
                step(V.tensor_scalar(ang_r[:, c], ang_r[:, c], -3.1415925, None, ALU.max))
            assert k == N_ANGLES
            dve.wait_ge(sines, 1)
            for c, src in ((C_DT, cond_in[:, 0, :]), (C_GATE, cond_in[:, 1, :]), (C_COS, ang[:, 2, :]),
                           (C_COS + 1, ang[:, 2, :]), (C_COS + 2, ang[:, 3, :]), (C_COS + 3, ang[:, 3, :]),
                           (C_SIN, ang[:, 0, :]), (C_SIN + 2, ang[:, 1, :])):
                V.tensor_copy(cond[:, :, c], src).then_inc(conds, 1)
            for c, src in ((C_SIN + 1, ang[:, 0, :]), (C_SIN + 3, ang[:, 1, :])):
                V.tensor_scalar(cond[:, :, c], src, -1.0, None, ALU.mult).then_inc(conds, 1)
            V.tensor_copy(id16[:], ident).then_inc(masks, 1)
            V.tensor_copy(mask16[:], cst[:, K_MASK:K_MASK + P]).then_inc(masks, 1)
            V.tensor_copy(maskT16[:], cst[:, K_MASKT:K_MASKT + P]).then_inc(masks, 1)
            V.tensor_scalar(ones_r[:], ident, 0.0, 1.0, ALU.mult, ALU.add).then_inc(masks, 1)
            dve.wait_ge(bias_ps, 1)
            V.tensor_copy(qk_b[:].rearrange("p w j -> p (w j)"), ps_pre[:, 0:2 * HJ]).then_inc(bias_done, 1)
            dve.wait_ge(bias_done, 1)
            V.tensor_tensor(qk_mb[:], qk_b[:], inner(cst[:, K_MQ:K_MQ + 2], HJ), ALU.mult).then_inc(bias_done, 1)
            dve.wait_ge(style_done, 2)
            V.scalar_tensor_tensor(sp_b[:], sp_a[:], -1.0, sp_a[:], ALU.mult, ALU.min).then_inc(soft_v, 1)
            dve.wait_ge(soft_a, 2)
            V.scalar_tensor_tensor(sp_c[:], sp_a[:], 0.0, sp_b[:], ALU.max, ALU.add).then_inc(soft_v, 1)
            dve.wait_ge(soft_v, 2)
            V.tensor_scalar(style[:, 0, :], sp_c[:], 1e-8, None, ALU.add).then_inc(soft_v, 1)
            k = 0

            def grid(ins):
                nonlocal k
                k += 1
                ins.then_inc(grids, 1)
                dve.wait_ge(grids, k)

            grid(V.tensor_scalar(g_b2[:], bg[:, 2, :], 0.5, None, ALU.mult))
            grid(V.tensor_tensor(g_p[:], bg[:, 1, :], ag[:, 1, :], ALU.subtract))
            grid(V.tensor_scalar(g_p[:], g_p[:], 0.5, None, ALU.mult))
            grid(V.tensor_tensor(g_m[:], bg[:, 1, :], ag[:, 1, :], ALU.add))
            grid(V.tensor_scalar(g_m[:], g_m[:], 0.5, None, ALU.mult))
            for side, lo in enumerate((0, D - 4)):
                ka = cst[:, K_AE + 4 * side:K_AE + 4 * side + 4]
                kb = cst[:, K_BE + 4 * side:K_BE + 4 * side + 4]
                grid(V.tensor_tensor(edge_t[:, side, :], ag[:, 1, lo:lo + 4], ka, ALU.mult))
                grid(V.tensor_tensor(g_edge[:, side, :], bg[:, 1, lo:lo + 4], kb, ALU.mult))
                grid(V.tensor_tensor(g_edge[:, side, :], g_edge[:, side, :], edge_t[:, side, :], ALU.add))

            def split(raw_, hi, lo, sem_, k):
                V.tensor_copy(hi, raw_).then_inc(sem_, 1)
                dve.wait_ge(sem_, k + 1)
                V.tensor_tensor(lo, raw_, hi, ALU.subtract).then_inc(sem_, 1)

            for i, (r_, hi, lo) in enumerate(((wqe, wqh, wql), (wke, wkh, wkl), (wv_raw, wvh, wvl), (f1_raw, f1h, f1l))):
                split(r_[:], hi[:], lo[:], split_w, 2 * i)

            def split_w1(e):
                dve.wait_ge(w1_in, 16 * E)
                w = slice(e * FF, (e + 1) * FF)
                split(raw[:, w], w1h[:, w], w1l[:, w], w1_split, 2 * e)

            def mean_var(n, src, st, mv, s_stats, s_mv):
                for b in range(GB):
                    V.bn_stats(st[:, b, :], src(b)).then_inc(s_stats.sem, 1)
                await_(dve, s_stats, n)
                apart(nc.vector)
                for b in range(GB):
                    V.bn_aggr(mv[:, b, :], st[:, b, :]).then_inc(s_mv.sem, 1)

            def normalize(dst, src, mv, rs):
                for b in range(GB):
                    ins = V.tensor_scalar(dst[:, b, :], src[:, b, :], mv[:, b, 0:1], rs[:, b:b + 1],
                                          ALU.subtract, ALU.mult)
                return ins

            def pre_stats(n):
                await_(dve, xa_in, n)
                await_(dve, ln0_ve, n - 1)
                mean_var(n, lambda b: xa[:, b, :], st0, mv0, ln0_stats, ln0_mv)

            def pre_normalize(n):
                await_(dve, ln0_rs, n)
                await_(dve, ln0_mv, n)
                await_(dve, xn0_t, n - 1)
                normalize(xn, xa, mv0, rs0).then_inc(ln0_xn.sem, 1)

            def inorm_stats(n):
                await_(dve, haff, n)
                mean_var(n, lambda b: h_aff[:, b * T:(b + 1) * T], sti, mvi, in_stats, in_mv)

            def inorm_apply(n):
                await_(dve, in_coef, n)
                await_(dve, logits, n - 1)
                for b in range(GB):
                    t = slice(b * T, (b + 1) * T)
                    ins = V.tensor_scalar(h32[:, t], h_aff[:, t], in_s[:, b:b + 1], in_t[:, b:b + 1], ALU.mult, ALU.add)
                ins.then_inc(h32_done.sem, 1)

            def h_high(n, p):
                await_(dve, h32_done, n)
                await_(dve, hid_ps, n - 2)
                V.tensor_copy(hh[p][:], h32[:]).then_inc(hh_done.sem, 1)

            def h_low(n, p):
                await_(dve, hh_done, n)
                V.tensor_tensor(hl[p][:], h32[:], hh[p][:], ALU.subtract).then_inc(h_split.sem, 1)

            def top_two(n):
                await_(dve, logits, n)
                V.tensor_copy(lg[:].rearrange("p b e -> p (b e)"), ps_pre[:, 0:GB * E]).then_inc(lg_copied.sem, 1)
                await_(dve, lg_copied, n)
                apart(nc.vector)
                for b in range(GB):
                    V.max(top[:, b, :], lg[:, b, :]).then_inc(topped.sem, 1)
                await_(dve, topped, n)
                V.tensor_tensor(gap[:], top[:, :, 1], top[:, :, 0], ALU.subtract).then_inc(gap_done.sem, 1)
                for b in range(GB):
                    ins = V.max_index(top_i[:, b, :], top[:, b, :], lg[:, b, :])
                ins.then_inc(topi_done.sem, 1)

            def gates_of_two(n):
                await_(dve, topi_done, n)
                V.tensor_copy(top_f[:], top_i[:, :, 0:2].rearrange("p b k -> p k b")).then_inc(gate_step.sem, 1)
                await_(dve, gap_exp, n)
                V.tensor_scalar(gsum[:], gexp[:], 1.0, None, ALU.add).then_inc(gate_step.sem, 1)
                await_(dve, gate_step, n, 2)
                V.reciprocal(gates[:, 0, :], gsum[:]).then_inc(gate_step.sem, 1)
                await_(dve, gate_step, n, 3)
                V.tensor_tensor(gates[:, 1, :], gates[:, 0, :], gexp[:], ALU.mult).then_inc(gate_step.sem, 1)
                for k in range(2):
                    V.tensor_tensor(pick[:, k], inner(top_f[:, k, :], E), bc(cst[:, K_E8:K_E8 + E], GB),
                                    ALU.is_equal).then_inc(gate_step.sem, 1)
                await_(dve, gate_step, n, 6)
                V.tensor_tensor(pick[:], pick[:], gates[:].unsqueeze(3).broadcast_to([P, 2, GB, E]),
                                ALU.mult).then_inc(gate_step.sem, 1)
                await_(dve, gate_step, n, 7)
                await_(dve, comb_tp, n - 1)
                V.tensor_tensor(comb[:], pick[:, 0], pick[:, 1], ALU.add).then_inc(comb_done.sem, 1)

            def relu(n, e, j):
                await_(dve, hid_ps, n, e * FT + j + 1)
                free_hidden(dve, n, e)
                V.tensor_scalar(hid[e % 2][:, j, :], ps_hid[j % 2][:], col(R_B1 + e * FT + j), 0.0,
                                ALU.add, ALU.max).then_inc(hid_dve.sem, 1)

            def gate(n, p, e):
                await_(dve, exp_ps, n, e + 1)
                await_(dve, comb_bc[e % 2], n, 16 * (e // 2 + 1))
                if e >= 1:
                    dst = gated[e % 2]
                    if e >= 3:
                        await_(dve, y_added, n, e - 2)
                    else:
                        await_(dve, y_added, n - 1)
                else:
                    dst = y_t[p]
                V.scalar_tensor_tensor(dst[:], ps_exp[:], col(R_B2 + e), comb_b[e % 2][:],
                                       ALU.add, ALU.mult).then_inc(gated_done.sem, 1)

            def pde(n, piece):
                if piece == 0:
                    await_(dve, y_back, n)
                    await_(dve, xb_in, n)
                    V.tensor_tensor(flat(f), ps_c[:], flat(xb), ALU.add).then_inc(f_done.sem, 1)
                    await_(dve, f_done, n)
                if piece == 1:
                    V.tensor_tensor(rb[:], f[:], bc(g_b2[:], GB), ALU.mult).then_inc(pde_v.sem, 1)
                    await_(dve, pde_v, n, 1)
                    V.tensor_tensor(u_[:, :, 1:D - 1], rb[:, :, 2:D], rb[:, :, 0:D - 2], ALU.subtract).then_inc(pde_v.sem, 1)
                if piece == 2:
                    V.tensor_tensor(eu[:], edges(rb, 3), cst[:, K_GE:K_GE + 6].rearrange("p (s k) -> p s k", s=2)
                                    .unsqueeze(1).broadcast_to([P, GB, 2, 3]), ALU.mult).then_inc(pde_v.sem, 1)
                    await_(dve, pde_v, n, 3)
                    V.tensor_reduce(u_[:, :, 0:D:D - 1], eu[:], AX.X, ALU.add).then_inc(pde_v.sem, 1)
                    await_(dve, pde_v, n, 4)
                    await_(dve, pde_pool, n, 1)
                    V.tensor_tensor(u_[:], u_[:], ua[:], ALU.subtract).then_inc(u_done.sem, 1)
                if piece == 3:
                    V.tensor_tensor(wp[:], f[:], bc(g_p[:], GB), ALU.mult).then_inc(pde_v.sem, 1)
                    V.tensor_tensor(wm[:], f[:], bc(g_m[:], GB), ALU.mult).then_inc(pde_v.sem, 1)
                if piece == 4:
                    await_(dve, pde_v, n, 6)
                    V.tensor_tensor(w_[:, :, 1:D - 1], wp[:, :, 2:D], wm[:, :, 0:D - 2], ALU.add).then_inc(pde_v.sem, 1)
                    V.tensor_tensor(ew[:], edges(f, 4), g_edge[:].unsqueeze(1).broadcast_to([P, GB, 2, 4]),
                                    ALU.mult).then_inc(pde_v.sem, 1)
                    await_(dve, pde_v, n, 8)
                    V.tensor_reduce(w_[:, :, 0:D:D - 1], ew[:], AX.X, ALU.add).then_inc(pde_v.sem, 1)
                    await_(dve, pde_pool, n)
                    V.tensor_tensor(w_[:, :, 1:D - 1], w_[:, :, 1:D - 1], bf[:, :, 1:D - 1], ALU.subtract).then_inc(pde_v.sem, 1)
                if piece == 5:
                    await_(dve, pde_v, n)
                    await_(dve, pde_ps, n)
                    V.tensor_tensor(flat(df), ps_s[:], flat(w_), ALU.add).then_inc(df_done.sem, 1)
                    await_(dve, df_done, n)
                    await_(dve, cond_ready, n)
                    for b in range(GB):
                        V.scalar_tensor_tensor(fn[:, b, :], df[:, b, :], cond_g[:, b, C_DT:C_DT + 1], f[:, b, :],
                                               ALU.mult, ALU.add).then_inc(fn_done.sem, 1)
                    await_(dve, fn_done, n)
                    V.tensor_scalar(x1in[:], fn[:], 0.0, None, ALU.max).then_inc(x1in_done.sem, 1)

            def edges(t, w):
                v = t[:]
                return bass.AP(v.tensor, v.offset, [list(v.ap[0]), list(v.ap[1]), [D - w, 2], [1, w]])

            def norm_stats(n, which):
                src = (x1in, xa2)[which]
                await_(dve, (x1in_done, xa2_done)[which], n)
                mean_var(n, lambda b: src[:, b, :], stn, mvn, ln_stats[which], ln_mv[which])

            def norm_apply(n, which):
                await_(dve, ln_rs[which], n)
                await_(dve, ln_mv[which], n)
                if which == 1:
                    await_(dve, xn_t[0], n)
                normalize(xn0, (x1in, xa2)[which], mvn, rsn).then_inc(ln_xn[which].sem, 1)

            def norm_split(n, which):
                await_(dve, hn_done[which], n)
                V.tensor_copy(hnh[:], hn[:]).then_inc(hnh_done[which].sem, 1)
                await_(dve, hnh_done[which], n)
                V.tensor_tensor(hnl[:], hn[:], hnh[:], ALU.subtract).then_inc(hn_split[which].sem, 1)

            def qk_out(n, j, which):
                await_(dve, qk_lo, n, 2 * j + which + 1)
                dst = (qs, ks)[which]
                V.scalar_tensor_tensor(dst[:, j].rearrange("p b t -> p (b t)"), ps_x[which][:], qk_b[:, which, j:j + 1],
                                       lo_part[which][:], ALU.add, ALU.subtract).then_inc(qk_done.sem, 1)

            def v_out(n):
                await_(dve, v_ps, n)
                V.tensor_tensor(vs[:, :, :, 0:DH], ps_c[:].rearrange("p (b h d) -> p b h d", b=GB, d=DH),
                                bv_b[:].rearrange("p (h d) -> p h d", d=DH).unsqueeze(1).broadcast_to([P, GB, NH, DH]),
                                ALU.add).then_inc(v_done.sem, 1)

            def maximum(n, u):
                await_(dve, s_ps, n, u + 1)
                if u >= 2:
                    await_(dve, dg_done, n, u - 1)
                V.tensor_reduce(mx[u % 2][:], ps_s[:].rearrange("p (j t) -> p j t", j=HJ), AX.X, ALU.max).then_inc(mx_done.sem, 1)

            def context(n, b):
                await_(dve, pv_done, n, (b + 1) * RG)
                c = ps_c[:, 0:NH * VW].rearrange("p (i j d) -> p i j d", i=RG, d=VW)
                V.reciprocal(rden[:], c[:, :, :, DH]).then_inc(rden_done.sem, 1)
                await_(dve, rden_done, n, b + 1)
                V.tensor_tensor(cx[:, b, :].rearrange("p (j i d) -> p i j d", i=RG, d=DH), c[:, :, :, 0:DH],
                                rden[:].unsqueeze(3).broadcast_to([P, RG, HJ, DH]), ALU.mult).then_inc(cx_done.sem, 1)

            def residual_1(n):
                await_(dve, wo_ps, n)
                V.tensor_tensor(flat(xa1), ps_s[:], flat(x1in), ALU.add).then_inc(xa1_done.sem, 1)

            def residual_2(n):
                await_(dve, f2_ps, n)
                V.tensor_tensor(flat(x2a), ps_s[:], flat(xa2), ALU.add).then_inc(x2a_done.sem, 1)

            def blend(n):
                await_(dve, x2b_done, n)
                V.tensor_tensor(x2a[:], x2b[:], x1in[:], ALU.subtract).then_inc(delta_done.sem, 1)
                await_(dve, delta_done, n)
                for b in range(GB):
                    V.scalar_tensor_tensor(res[:, b, :], x2a[:, b, :], cond_g[:, b, C_GATE:C_GATE + 1], x1in[:, b, :],
                                           ALU.mult, ALU.add).then_inc(res_done.sem, 1)

            def emit(g, p, back, experts, pre):
                n, m = g - 1, g + 1
                if back:
                    await_(dve, cond_ready, n)
                for s in range(E):
                    for j in range(FT):
                        at = s * FT + j
                        if experts:
                            if isinstance(g, int) and g == 0 and j == 0 and s >= 1:
                                split_w1(s)
                            if j in F_DVE:
                                relu(g, s, j)
                            if j == 2 and s >= 1:
                                gate(g, p, s - 1)
                        if back:
                            if at in (1, 2, 3, 4, 5):
                                pde(n, at - 1)
                            if at == 7:
                                pde(n, 5)
                                norm_stats(n, 0)
                            if at == 10:
                                norm_apply(n, 0)
                            if at == 12:
                                norm_split(n, 0)
                            if 13 <= at < 17:
                                qk_out(n, at - 13, 0)
                                qk_out(n, at - 13, 1)
                            if at == 16:
                                v_out(n)
                            for u in range(NU):
                                if at == 17 + u // 2:
                                    maximum(n, u)
                                if at == 17 + (u + 3) // 2 and u % RG == RG - 1:
                                    context(n, u // RG)
                            if at == 27:
                                residual_1(n)
                            if at == 28:
                                norm_stats(n, 1)
                            if at == 29:
                                norm_apply(n, 1)
                            if at == 30:
                                norm_split(n, 1)
                        if pre:
                            if at == 3:
                                pre_stats(m)
                            if at == 4:
                                pre_normalize(m)
                            if at == 6:
                                inorm_stats(m)
                            if at == 8:
                                inorm_apply(m)
                            if at == 9:
                                h_high(m, 1 - p)
                                h_low(m, 1 - p)
                            if at == 10:
                                top_two(m)
                            if at == 12:
                                gates_of_two(m)
                if experts:
                    gate(g, p, E - 1)
                if back:
                    residual_2(n)
                    blend(n)

            pre_stats(0)
            pre_normalize(0)
            inorm_stats(0)
            inorm_apply(0)
            h_high(0, 0)
            h_low(0, 0)
            split_w1(0)
            top_two(0)
            gates_of_two(0)
            iterations(dve, emit)

        @block.gpsimd
        def _(pool):
            G = nc.gpsimd
            G.memset(rows[:], 0.0).then_inc(rows_zero, 1)
            G.memset(neg_half[:], -0.5).then_inc(halves, 1)
            G.memset(ln_eps[:], LN_EPS).then_inc(halves, 1)
            G.memset(inorm_eps[:], INORM_EPS).then_inc(halves, 1)
            G.memset(vs[:], 1.0).then_inc(halves, 1)
            pool.wait_ge(halves, 4)
            pool.wait_ge(cst_in, 16)

            def rsqrt(n, ve, rs, mv, eps, s_mv, s_ve, s_rs, reader):
                await_(pool, s_mv, n)
                G.tensor_tensor(ve[:], mv[:, :, 1], eps[:], ALU.add).then_inc(s_ve.sem, 1)
                await_(pool, s_ve, n)
                if reader is not None:
                    await_(pool, reader, n - 1)
                G.tensor_tensor(rs[:], ve[:], neg_half[:], ALU.pow).then_inc(s_rs.sem, 1)

            def pre_root(n):
                rsqrt(n, ve0, rs0, mv0, ln_eps, ln0_mv, ln0_ve, ln0_rs, ln0_xn)

            def inorm_coefficients(n):
                rsqrt(n, vei, rsi, mvi, inorm_eps, in_mv, in_ve, in_rs, None)
                if isinstance(n, int) and n == 0:
                    pool.wait_ge(soft_v, 3)
                G.tensor_copy(sty_g[:], style[:, :, bass.ds(n * GB, GB)]).then_inc(in_styled.sem, 1)
                await_(pool, in_rs, n)
                await_(pool, in_styled, n)
                await_(pool, h32_done, n - 1)
                G.tensor_tensor(in_s[:], rsi[:], sty_g[:, 0, :], ALU.mult).then_inc(in_step.sem, 1)
                await_(pool, in_step, n, 1)
                G.tensor_tensor(in_ms[:], mvi[:, :, 0], in_s[:], ALU.mult).then_inc(in_step.sem, 1)
                await_(pool, in_step, n, 2)
                G.tensor_tensor(in_t[:], sty_g[:, 1, :], in_ms[:], ALU.subtract).then_inc(in_coef.sem, 1)

            def add_expert(n, p, e):
                await_(pool, gated_done, n, e + 1)
                if e >= 2:
                    await_(pool, y_added, n, e - 1)
                G.tensor_tensor(y_t[p][:], y_t[p][:], gated[e % 2][:], ALU.add).then_inc(y_added.sem, 1)

            def pde_products(n):
                await_(pool, f_done, n)
                for dst, grid_ in ((ua, ag[:, 0, :]), (v_, bg[:, 0, :]), (bf, bg[:, 1, :])):
                    G.tensor_tensor(dst[:], f[:], bc(grid_, GB), ALU.mult).then_inc(pde_pool.sem, 1)

            def conditions(n):
                if isinstance(n, int) and n == 0:
                    pool.wait_ge(conds, N_CONDS)
                G.tensor_copy(cond_g[:], cond[:, bass.ds(n * GB, GB), :]).then_inc(cond_ready.sem, 1)

            def norm_root(n, which):
                rsqrt(n, ven, rsn, mvn, ln_eps, ln_mv[which], ln_ve[which], ln_rs[which], None)

            def minus_maximum(n, u):
                await_(pool, mx_done, n, u + 1)
                if u >= 2:
                    await_(pool, x_ps, n, u - 1)
                G.tensor_tensor(dg[u % 2][:], bc(negid, HJ), inner(mx[u % 2][:], T), ALU.mult).then_inc(dg_done.sem, 1)

            def add_row(n, dst, src, row, sig, done):
                await_(pool, sig, n)
                G.tensor_tensor(dst[:], src[:], bc(row[:], GB), ALU.add).then_inc(done.sem, 1)

            def rotate(n):
                await_(pool, res_done, n)
                r = res[:].rearrange("p b (k c) -> p b k c", c=4)
                w = t2[:].rearrange("p b (k c) -> p b k c", c=4)

                def coef(c, m):
                    v = cond_g[:, :, c:c + 4 if m == 1 else c + 3:m]
                    return v.unsqueeze(2).broadcast_to([P, GB, D // 4, 4 // m])

                G.tensor_tensor(t1[:].rearrange("p b (k c) -> p b k c", c=4), r, coef(C_COS, 1), ALU.mult).then_inc(rot_step.sem, 1)
                G.tensor_tensor(w[:, :, :, 0::2], r[:, :, :, 1::2], coef(C_SIN, 2), ALU.mult).then_inc(rot_step.sem, 1)
                G.tensor_tensor(w[:, :, :, 1::2], r[:, :, :, 0::2], coef(C_SIN + 1, 2), ALU.mult).then_inc(rot_step.sem, 1)
                await_(pool, rot_step, n)
                pool.wait_ge(stored.sem, n * 16)
                G.tensor_tensor(fin[:], t1[:], t2[:], ALU.add).then_inc(rotated.sem, 1)

            def emit(g, p, back, experts, pre):
                n, m = g - 1, g + 1
                if back:
                    conditions(n)
                for s in range(E):
                    for j in range(FT):
                        at = s * FT + j
                        if experts:
                            if j == 3 and s >= 2:
                                add_expert(g, p, s - 1)
                        if back:
                            if at == 1:
                                pde_products(n)
                            if at == 8:
                                norm_root(n, 0)
                            for u in range(NU):
                                if at == 17 + u // 2:
                                    minus_maximum(n, u)
                            if at == 27:
                                add_row(n, xa2, xa1, bo_b, xa1_done, xa2_done)
                            if at == 28:
                                norm_root(n, 1)
                        if pre:
                            if at == 3:
                                pre_root(m)
                            if at == 7:
                                inorm_coefficients(m)
                if experts:
                    add_expert(g, p, E - 1)
                if back:
                    add_row(n, x2b, x2a, fb2_b, x2a_done, x2b_done)
                    rotate(n)

            pre_root(0)
            inorm_coefficients(0)
            iterations(pool, emit)


def kernel(**inputs):
    import concourse.bacc as bacc
    from concourse.bass_utils import run_bass_kernel_spmd

    nc = bacc.Bacc("TRN2", target_bir_lowering=False, num_devices=1)
    arrays, args = {}, {}
    for name, value in list(inputs.items()) + [("cst", shape_constants())]:
        v = np.ascontiguousarray(value)
        arrays["in_" + name] = v
        args[name] = nc.dram_tensor("in_" + name, v.shape, mybir.dt.from_np(v.dtype), kind="ExternalInput").ap()
    out = nc.dram_tensor("out", (B, T, D), F32, kind="ExternalOutput").ap()
    cond_seq_kernel(nc, args, out)
    r = run_bass_kernel_spmd(nc, [arrays], core_ids=[0])
    return r.results[0]["out"]
```

```python
from contextlib import ExitStack

import numpy as np

import concourse.bass as bass
from concourse import mybir

F32 = mybir.dt.float32
F32R = mybir.dt.float32r
BF16 = mybir.dt.bfloat16
I32 = mybir.dt.int32
U32 = mybir.dt.uint32
ALU = mybir.AluOpType
ACT = mybir.ActivationFunctionType
AX = mybir.AxisListType

P = 128
B, T, D = 32, 128, 128
GB = 4
NG = B // GB
GT = GB * T
E, FF = 8, 512
FT = FF // P
NH, DH = 16, 8
RG = 4
HJ = NH // RG
NU = GB * RG
VW = DH + 1
LN_EPS, INORM_EPS = 1e-5, 1e-8
MASKED = -1.0e30
C_DT, C_GATE, C_COS, C_SIN, C_N = 0, 1, 2, 6, 10
TWO_PI_HI, TWO_PI_MID = 6.28125, 0.0019350051879882812
TWO_PI_LO = 2 * np.pi - 6.28125 - 0.0019350051879882812
ROUND = 12582912.0


def derivative_matrices(n):
    g, gg = np.zeros((n, n), np.float32), np.zeros((n, n), np.float32)
    for i in range(1, n - 1):
        g[i, i - 1], g[i, i + 1] = -0.5, 0.5
        gg[i, i - 1], gg[i, i], gg[i, i + 1] = 1, -2, 1
    g[0, :3], g[-1, -3:] = (-1.5, 2, -0.5), (0.5, -2, 1.5)
    gg[0, :4], gg[-1, -4:] = (2, -5, 4, -1), (-1, 4, -5, 2)
    return g, gg


R_B1 = 0
R_B2 = R_B1 + E * FT
R_LNG, R_LNB, R_HB1, R_HB2, R_SB1, R_SB2 = (R_B2 + E + i for i in range(6))
R_G1, R_BE1, R_G2, R_BE2 = (R_SB2 + 2 + i for i in range(4))
R_FB1 = R_BE2 + 1
R_N = R_FB1 + FT

N_ROW_LOADS, N_REST_LOADS, N_SPREAD, N_ANGLES, N_CONDS = 13, 23, 17, 16, 10

K_ID = 0
K_NEGID = K_ID + P
K_GX = K_NEGID + P
K_GXX = K_GX + P
K_MASK = K_GXX + P
K_MASKT = K_MASK + P
K_IOTA = K_MASKT + P
K_MQ, K_MK = K_IOTA + 1, K_IOTA + 2
K_E8 = K_IOTA + 3
K_GE = K_E8 + 8
K_AE = K_GE + 6
K_BE = K_AE + 8
K_N = K_BE + 8


def shape_constants():
    c = np.zeros((P, K_N), np.float32)
    g, gg = derivative_matrices(P)
    c[:, K_ID:K_ID + P] = np.eye(P)
    c[:, K_NEGID:K_NEGID + P] = -np.eye(P)
    c[:, K_GX:K_GX + P] = g.T
    c[:, K_GXX:K_GXX + P] = 0.5 * gg.T
    q, k = np.arange(P)[:, None], np.arange(P)[None, :]
    c[:, K_MASK:K_MASK + P] = np.where(k > q, MASKED, 0)
    c[:, K_MASKT:K_MASKT + P] = np.where(q > k, MASKED, 0)
    p = np.arange(P)
    c[:, K_IOTA] = p
    c[:, K_MQ] = (p // DH % 4) == 2
    c[:, K_MK] = (p // DH % 4) == 1
    c[:, K_E8:K_E8 + 8] = np.arange(8)
    c[:, K_GE:K_GE + 6] = (-3, 4, -1, 1, -4, 3)
    c[:, K_AE:K_AE + 8] = (1.5, -2, 0.5, 0, 0, -0.5, 2, -1.5)
    c[:, K_BE:K_BE + 8] = (1, -2.5, 2, -0.5, -0.5, 2, -2.5, 1)
    return c


class Signal:

    def __init__(self, sem, per):
        self.sem, self.per = sem, per

    def after(self, n, k=None):
        return n * self.per + (self.per if k is None else k)


def cond_seq_kernel(nc, a, out):
    with ExitStack() as ctx:
        def sb(name, shape, dt=F32):
            return ctx.enter_context(nc.sbuf_tensor(name, shape, dt))

        def bank(name):
            return ctx.enter_context(nc.psum_tensor(name, [P, 512], F32))

        def sem(name):
            return ctx.enter_context(nc.semaphore(name))

        def signal(name, per=1):
            return Signal(sem(name), per)

        def flat(t):
            return t[:].rearrange("p b d -> p (b d)")

        ps_hid = [bank("ps_hid0"), bank("ps_hid1")]
        ps_exp = bank("ps_exp")
        ps_pre = bank("ps_pre")
        ps_s = bank("ps_s")
        ps_x = [bank("ps_x0"), bank("ps_x1")]
        ps_c = bank("ps_c")

        cst = sb("cst", [P, K_N])
        ident = cst[:, K_ID:K_ID + P]
        negid = cst[:, K_NEGID:K_NEGID + P]
        id16 = sb("id16", [P, P], BF16)
        mask16 = sb("mask16", [P, P], BF16)
        maskT16 = sb("maskT16", [P, P], BF16)
        ones_r = sb("ones_r", [P, P], F32R)
        ones1 = sb("ones1", [1, 2])
        raw = sb("raw", [P, E * FF])

        def part(i, n=1):
            return raw[:, i * GT:(i + n) * GT]

        def part3(i):
            return part(i).rearrange("p (b d) -> p b d", b=GB)

        x2b, cx, x2a, xa2 = sb("x2b", [P, GB, D]), sb("cx", [P, GB, D]), sb("x2a", [P, GB, D]), sb("xa2", [P, GB, D])
        hn = sb("hn", [P, GT])
        w1h, w1l = sb("w1h", [P, E * FF], F32R), sb("w1l", [P, E * FF], F32R)
        w2 = sb("w2", [P, E, FT, D])
        rw = sb("rw", [P, E])
        rows = sb("rows", [R_N, P])
        cols = sb("cols", [P, R_N])
        wq_raw, wk_raw = sb("wq_raw", [P, D]), sb("wk_raw", [P, D])
        bq_row, bk_row = sb("bq_row", [1, D]), sb("bk_row", [1, D])
        wqe, wke = flat(cx), flat(xa2)
        bqe, bke = flat(x2b)[0:1, :], hn[0:1, :]
        wqh, wql = sb("wqh", [P, HJ * P], F32R), sb("wql", [P, HJ * P], F32R)
        wkh, wkl = sb("wkh", [P, HJ * P], F32R), sb("wkl", [P, HJ * P], F32R)
        qk_b = sb("qk_b", [P, 2, HJ])
        qk_mb = sb("qk_mb", [P, 2, HJ])
        wv_raw = sb("wv_raw", [P, D])
        wvh, wvl = sb("wvh", [P, D], F32R), sb("wvl", [P, D], F32R)
        wo = sb("wo", [P, D])
        f1_raw = flat(x2a)
        f1h, f1l = sb("f1h", [P, FF], F32R), sb("f1l", [P, FF], F32R)
        f2 = sb("f2", [P, FT, D])
        bv_b, bo_b, fb2_b = sb("bv_b", [P, D]), sb("bo_b", [P, D]), sb("fb2_b", [P, D])
        subj = sb("subj", [32, 64])
        hw1, hw2 = sb("hw1", [64, P]), sb("hw2", [P, P])
        sw1, sw2 = sb("sw1", [P, 64]), sb("sw2", [64, 2 * D])
        ln_eps, inorm_eps = sb("ln_eps", [P, GB]), sb("inorm_eps", [P, GB])
        carrier = sb("carrier", [P, 1])
        ag, bg = sb("ag", [P, 2, P]), sb("bg", [P, 3, P])
        g_p, g_m, g_b2 = sb("g_p", [P, P]), sb("g_m", [P, P]), sb("g_b2", [P, P])
        g_edge, edge_t = sb("g_edge", [P, 2, 4]), sb("edge_t", [P, 2, 4])
        ids_i, ids_f, onehot = sb("ids_i", [32, B], I32), sb("ids_f", [32, B]), sb("onehot", [32, B])
        se, hyp1, hyp2, sty1 = sb("se", [64, B]), sb("hyp1", [P, B]), sb("hyp2", [P, B]), sb("sty1", [64, B])
        style = sb("style", [P, 2, B])
        sp_a, sp_b, sp_c = sb("sp_a", [P, B]), sb("sp_b", [P, B]), sb("sp_c", [P, B])
        cond_in = sb("cond_in", [P, 4, B])
        ang, ang_k, ang_r = sb("ang", [P, 4, B]), sb("ang_k", [P, 4, B]), sb("ang_r", [P, 4, B])
        cond = sb("cond", [P, B, C_N])
        neg_half = sb("neg_half", [P, GB])

        xa = sb("xa", [P, GB, D])
        xn0, xn = sb("xn0", [P, GB, D]), sb("xn", [P, GB, D])
        h_aff, h32 = sb("h_aff", [P, GT]), sb("h32", [P, GT])
        hh = [sb("hh0", [P, GT], F32R), sb("hh1", [P, GT], F32R)]
        hl = [sb("hl0", [P, GT], F32R), sb("hl1", [P, GT], F32R)]
        st0, mv0, rs0 = sb("st0", [P, GB, 6]), sb("mv0", [P, GB, 2]), sb("rs0", [P, GB])
        sti, mvi, rsi = sb("sti", [P, GB, 6]), sb("mvi", [P, GB, 2]), sb("rsi", [P, GB])
        stn, mvn, rsn = sb("stn", [P, GB, 6]), sb("mvn", [P, GB, 2]), sb("rsn", [P, GB])
        in_s, in_ms, in_t = sb("in_s", [P, GB]), sb("in_ms", [P, GB]), sb("in_t", [P, GB])
        ve0, vei, ven = sb("ve0", [P, GB]), sb("vei", [P, GB]), sb("ven", [P, GB])
        sty_g = sb("sty_g", [P, 2, GB])
        lg, top, top_i = sb("lg", [P, GB, E]), sb("top", [P, GB, 8]), sb("top_i", [P, GB, 8], U32)
        top_f = sb("top_f", [P, 2, GB])
        gap, gexp, gsum, gates = sb("gap", [P, GB]), sb("gexp", [P, GB]), sb("gsum", [P, GB]), sb("gates", [P, 2, GB])
        pick = sb("pick", [P, 2, GB, E])
        comb = sb("comb", [P, GB, E])
        comb_t = sb("comb_t", [E, GT])
        gate_rows = nc.dram_tensor("gate_rows", (2, E, GT), F32).ap()
        comb_b = [sb("comb_b0", [P, GT]), sb("comb_b1", [P, GT])]

        hid = [sb("hid0", [P, FT, GT]), sb("hid1", [P, FT, GT])]
        gated = [sb("gated0", [P, GT]), sb("gated1", [P, GT])]
        y_t = [sb("y_t0", [P, GT]), sb("y_t1", [P, GT])]

        xb = sb("xb", [P, GB, D])
        f = sb("f", [P, GB, D])
        rb, u_, ua, v_, w_, wp, wm, bf = (part3(i) for i in range(8))
        eu, ew = sb("eu", [P, GB, 2, 3]), sb("ew", [P, GB, 2, 4])
        df, fn, x1in = rb, wp, sb("x1in", [P, GB, D])
        cond_g = sb("cond_g", [P, GB, C_N])
        hnh, hnl = sb("hnh", [P, GT], F32R), sb("hnl", [P, GT], F32R)
        lo_part = [part(1).bitcast(F32R), part(2).bitcast(F32R)]
        qs, ks = sb("qs", [P, HJ, GB, T], F32R), sb("ks", [P, HJ, GB, T], F32R)
        vs = sb("vs", [P, GB, NH, VW])
        mx = [sb("mx0", [P, HJ]), sb("mx1", [P, HJ])]
        dg = [sb("dg0", [P, HJ, T], F32R), sb("dg1", [P, HJ, T], F32R)]
        pt = [part3(4), part3(5)]
        rden = sb("rden", [P, RG, HJ])
        pvt = hn
        cxt, xbo, res = hn, sb("xbo", [P, GB, D]), x2b
        gl = part(0, FT).rearrange("p (j t) -> p j t", j=FT)
        t1, t2, fin = part3(6), part3(7), sb("fin", [P, GB, D])

        cst_in, w1_in, w2_in, rest_in, rows_in = sem("cst_in"), sem("w1_in"), sem("w2_in"), sem("rest_in"), sem("rows_in")
        rows_zero, halves = sem("rows_zero"), sem("halves")
        cols_ps, cols_done = sem("cols_ps"), sem("cols_done")
        hot_step, se_ps, se_done = sem("hot_step"), sem("se_ps"), sem("se_done")
        hyp1_ps, hyp1_done, hyp2_ps, hyp2_done = sem("hyp1_ps"), sem("hyp1_done"), sem("hyp2_ps"), sem("hyp2_done")
        sty1_ps, sty1_done, style_ps, style_done = sem("sty1_ps"), sem("sty1_done"), sem("style_ps"), sem("style_done")
        soft_v, soft_a = sem("soft_v"), sem("soft_a")
        spread, bias_ps, bias_done, split_w = sem("spread"), sem("bias_ps"), sem("bias_done"), sem("split_w")
        w1_split = sem("w1_split")
        grids, angles, sines, conds, masks = sem("grids"), sem("angles"), sem("sines"), sem("conds"), sem("masks")
        xa_in = signal("xa_in", 16)
        ln0_stats, ln0_mv = signal("ln0_stats", GB), signal("ln0_mv", GB)
        ln0_ve, ln0_rs, ln0_xn = signal("ln0_ve"), signal("ln0_rs"), signal("ln0_xn")
        xn0_t = signal("xn0_t")
        haff = signal("haff")
        in_stats, in_mv, in_ve, in_rs = signal("in_stats", GB), signal("in_mv", GB), signal("in_ve"), signal("in_rs")
        in_styled, in_step, in_coef = signal("in_styled"), signal("in_step", 2), signal("in_coef")
        h32_done, hh_done, h_split = signal("h32_done"), signal("hh_done"), signal("h_split")
        logits = signal("logits")
        lg_copied, topped, topi_done = signal("lg_copied"), signal("topped", GB), signal("topi_done")
        gap_done, gap_exp, gate_step = signal("gap_done"), signal("gap_exp"), signal("gate_step", 7)
        comb_done, comb_tp, comb_ct, comb_rowed = signal("comb_done"), signal("comb_tp"), signal("comb_ct"), signal("comb_rowed", 16)
        comb_bc = [signal("comb_bc0", 16 * E // 2), signal("comb_bc1", 16 * E // 2)]
        hid_ps = signal("hid_ps", E * FT)
        hid_done = signal("hid_done", E * FT)
        exp_ps = signal("exp_ps", E)
        gated_done, y_added = signal("gated_done", E), signal("y_added", E - 1)
        xb_in = signal("xb_in", 16)
        y_back, f_done = signal("y_back"), signal("f_done")
        cond_ready = signal("cond_ready")
        pde_pool = signal("pde_pool", 3)
        pde_v = signal("pde_v", 10)
        u_done, pde_ps, w_done = signal("u_done"), signal("pde_ps"), signal("w_done")
        df_done, fn_done, x1in_done = signal("df_done"), signal("fn_done", GB), signal("x1in_done")
        ln_stats = [signal("ln1_stats", GB), signal("ln2_stats", GB)]
        ln_mv = [signal("ln1_mv", GB), signal("ln2_mv", GB)]
        ln_ve = [signal("ln1_ve"), signal("ln2_ve")]
        ln_rs = [signal("ln1_rs"), signal("ln2_rs")]
        ln_xn = [signal("ln1_xn"), signal("ln2_xn")]
        xn_t = [signal("xn1_t"), signal("xn2_t")]
        hn_done = [signal("hn1_done"), signal("hn2_done")]
        hnh_done = [signal("hnh1_done"), signal("hnh2_done")]
        hn_split = [signal("hn1_split"), signal("hn2_split")]
        qk_ps, qk_lo, qk_done = signal("qk_ps", 2 * HJ), signal("qk_lo", 2 * HJ), signal("qk_done", 2 * HJ)
        v_ps, v_done = signal("v_ps"), signal("v_done")
        s_ps, mx_done, dg_done = signal("s_ps", NU), signal("mx_done", NU), signal("dg_done", NU)
        x_ps, exp_done, pv_done = signal("x_ps", NU), signal("exp_done", NU), signal("pv_done", NU)
        rden_done, cx_done = signal("rden_done", GB), signal("cx_done", GB)
        pv_out, pv_turned = signal("pv_out", GB), signal("pv_turned", GB)
        cx_t, cxt_done = signal("cx_t"), signal("cxt_done")
        wo_ps, xbo_done, xa2_done = signal("wo_ps"), signal("xbo_done"), signal("xa2_done")
        f1_ps, gelu_done, f2_ps = signal("f1_ps", FT), signal("gelu_done", FT), signal("f2_ps")
        x2b_done, sofar_done, delta_done, res_done = signal("x2b_done"), signal("sofar_done"), signal("delta_done"), signal("res_done", GB)
        rot_step, rotated, stored = signal("rot_step", 3), signal("rotated"), signal("stored", 16)

        def await_(eng, sig, n, k=None):
            if isinstance(n, int) and n < 0:
                return
            eng.wait_ge(sig.sem, sig.after(n, k))

        def apart(eng):
            eng.memset(carrier[:], 0.0)

        def bc(ap, n):
            return ap.unsqueeze(1).broadcast_to([ap.shape[0], n, ap.shape[1]])

        def inner(ap, n):
            return ap.unsqueeze(2).broadcast_to([ap.shape[0], ap.shape[1], n])

        def col(r):
            return cols[:, r:r + 1]

        def free_hidden(eng, n, e):
            if e >= 2:
                await_(eng, exp_ps, n, e - 1)
            else:
                await_(eng, exp_ps, n - 1, E - 1 + e)

        def iterations(eng, emit):
            emit(0, 0, back=False, experts=True, pre=True)
            with eng.Fori(0, (NG - 2) // 2) as i:
                for u in range(2):
                    emit(i * 2 + 1 + u, (1 + u) % 2, back=True, experts=True, pre=True)
            emit(NG - 1, (NG - 1) % 2, back=True, experts=True, pre=False)
            emit(NG, NG % 2, back=True, experts=False, pre=False)

        A_Y, A_PDE, A_STATS1, A_NORM1, A_QK = 2, 7, 8, 10, 12
        A_STATS, A_AFFINE = 12, 15
        A_STEPS, STEPS, NK = 16, 6, NU + 4
        K_INORM, K_ROUTER, K_GATES, K_GATES_T = 1, 8, 10, 16
        A_CONTEXT, A_WO, A_STATS2, A_NORM2, A_FFN, A_FFN_OUT = 20, 21, 22, 24, 27, 31

        def steps(at):
            lo = (at - A_STEPS) * STEPS
            return range(max(lo, 0), min(lo + STEPS, NK)) if lo >= 0 else range(0)

        def turned(k):
            b, r_ = divmod(k - (RG - 1 + 4), RG)
            return b if r_ == 0 and 0 <= b < GB else None

        def broadcast_gates(eng, n, p, e):
            if e == 0:
                await_(eng, comb_rowed, n)
            if e >= 2:
                await_(eng, gated_done, n, e - 1)
            else:
                await_(eng, gated_done, n - 1, E - 1 + e)
            eng.dma_start(comb_b[e % 2][:], gate_rows[p, e].partition_broadcast(P)).then_inc(comb_bc[e % 2].sem, 16)

        block = ctx.enter_context(nc.Block())

        @block.sync
        def _(sp):
            def load(dst, src, sem_):
                sp.dma_start(dst, src).then_inc(sem_, 16)

            def load_xa(n):
                first = first_batch(n)
                if not (isinstance(n, int) and n == 0):
                    await_(sp, ln0_xn, n - 1)
                load(xa[:], x_grp(first), xa_in.sem)

            def load_xb(n):
                first = first_batch(n)
                if not (isinstance(n, int) and n == 0):
                    await_(sp, f_done, n - 1)
                load(xb[:], x_grp(first), xb_in.sem)

            def first_batch(n):
                return n * GB if isinstance(n, int) else sp.snap(n * GB)

            def x_grp(first):
                return a["x"][bass.ds(first, GB), :, :].rearrange("b t d -> t b d")

            load_xa(0)
            load(cst[:], a["cst"], cst_in)
            load(ids_i[:], a["itok_B_6_14"].partition_broadcast(32), rest_in)
            load(subj[:], a["L0_cond_subj_emb"], rest_in)
            load(hw1[:], a["L0_cond_hyp_w1"], rest_in)
            load(hw2[:], a["L0_cond_hyp_w2"], rest_in)
            load(sw1[:], a["L0_cond_sty_w1"], rest_in)
            load(sw2[:], a["L0_cond_sty_w2"], rest_in)
            load(rw[:], a["L0_cond_router_w"], rest_in)
            sp.wait_ge(rows_zero, 1)
            load(rows[R_B1:R_B1 + E * FT, :], a["L0_cond_exp_b1"].rearrange("e (t p) -> (e t) p", p=P), rows_in)
            load(rows[R_B2:R_B2 + E, :], a["L0_cond_exp_b2"], rows_in)
            for r, name in ((R_LNG, "L0_cond_ln_g"), (R_LNB, "L0_cond_ln_b"), (R_HB1, "L0_cond_hyp_b1"),
                            (R_HB2, "L0_cond_hyp_b2"), (R_G1, "L2_cond_gamma1"), (R_BE1, "L2_cond_beta1"),
                            (R_G2, "L2_cond_gamma2"), (R_BE2, "L2_cond_beta2")):
                load(rows[r:r + 1, :], a[name].unsqueeze(0), rows_in)
            load(rows[R_SB1:R_SB1 + 1, 0:64], a["L0_cond_sty_b1"].unsqueeze(0), rows_in)
            load(rows[R_SB2:R_SB2 + 2, :], a["L0_cond_sty_b2"].rearrange("(r p) -> r p", p=P), rows_in)
            load(rows[R_FB1:R_FB1 + FT, :], a["L2_cond_b1"].rearrange("(r p) -> r p", p=P), rows_in)
            for i, name in enumerate(("condB_dt", "condB_gatescore", "condB_theta", "condB_phi")):
                load(cond_in[:, i, :], a[name].partition_broadcast(P), rest_in)
            load(ag[:], a["L1_cond_A_grid"].rearrange("c x y -> x c y"), rest_in)
            load(bg[:], a["L1_cond_B_grid"].rearrange("c x y -> x c y"), rest_in)
            for dst, name in ((wq_raw, "L2_cond_Wq"), (wk_raw, "L2_cond_Wk"), (wv_raw, "L2_cond_Wv"),
                              (wo, "L2_cond_Wo"), (f1_raw, "L2_cond_W1")):
                load(dst[:], a[name], rest_in)
            load(f2[:], a["L2_cond_W2"].rearrange("(t p) d -> p t d", p=P), rest_in)
            load(bq_row[:], a["L2_cond_bq"].unsqueeze(0), rest_in)
            load(bk_row[:], a["L2_cond_bk"].unsqueeze(0), rest_in)
            for dst, name in ((bv_b, "L2_cond_bv"), (bo_b, "L2_cond_bo")):
                load(dst[:], a[name].partition_broadcast(P), rest_in)
            load(fb2_b[:], a["L2_cond_b2"].partition_broadcast(P), stored.sem)
            load_xb(0)

            def rows_of_gates(n, p):
                await_(sp, comb_ct, n)
                load(gate_rows[p], comb_t[:], comb_rowed.sem)

            def store(n):
                first = first_batch(n)
                await_(sp, rotated, n)
                sp.dma_start(out[bass.ds(first, GB), :, :].rearrange("b t d -> t b d"),
                             fin[:]).then_inc(stored.sem, 16)

            rows_of_gates(0, 0)
            def emit(g, p, back, experts, pre):
                if pre:
                    load_xa(g + 1)
                for e in range(1, E):
                    if experts and e == 2:
                        await_(sp, comb_rowed, g)
                    if experts and e >= 2:
                        broadcast_gates(sp, g, p, e)
                    if e == 3 and back and experts:
                        load_xb(g)
                    if e == 4 and pre:
                        rows_of_gates(g + 1, 1 - p)
                if back:
                    store(g - 1)

            iterations(sp, emit)
            await_(sp, stored, NG)

        @block.scalar
        def _(act):
            for e in range(E):
                act.dma_start(raw[:, e * FF:(e + 1) * FF], a["L0_cond_exp_w1"][e]).then_inc(w1_in, 16)
            for e in range(E):
                act.dma_start(w2[:, e], a["L0_cond_exp_w2"][e].rearrange("(t p) d -> p t d", p=P)).then_inc(w2_in, 16)

            act.wait_ge(angles, N_ANGLES)
            act.activation(ang[:], ang_r[:], ACT.Sin).then_inc(sines, 1)
            act.wait_ge(cols_ps, 1)
            act.activation(cols[:], ps_s[:, 0:R_N], ACT.Identity).then_inc(cols_done, 1)
            act.wait_ge(cols_done, 1)
            act.wait_ge(hyp1_ps, 1)
            act.activation(hyp1[:], ps_x[1][:, 0:B], ACT.Relu, bias=col(R_HB1)).then_inc(hyp1_done, 1)
            act.wait_ge(hyp2_ps, 1)
            act.activation(hyp2[:], ps_c[:, 0:B], ACT.Identity, bias=col(R_HB2)).then_inc(hyp2_done, 1)
            act.wait_ge(sty1_ps, 1)
            act.activation(sty1[:], ps_hid[0][0:64, 0:B], ACT.Relu,
                           bias=cols[0:64, R_SB1:R_SB1 + 1]).then_inc(sty1_done, 1)
            act.wait_ge(style_ps, 2)
            act.activation(sp_a[:], ps_hid[1][:, 0:B], ACT.Identity, bias=col(R_SB2)).then_inc(style_done, 1)
            act.activation(style[:, 1, :], ps_exp[:, 0:B], ACT.Identity, bias=col(R_SB2 + 1)).then_inc(style_done, 1)
            act.wait_ge(soft_v, 1)
            act.activation(sp_c[:], sp_b[:], ACT.Exp).then_inc(soft_a, 1)
            act.wait_ge(soft_a, 1)
            act.activation(sp_b[:], sp_c[:], ACT.Ln, bias=1.0).then_inc(soft_a, 1)

            def affine(n):
                await_(act, xn0_t, n)
                await_(act, in_coef, n - 1)
                await_(act, h32_done, n - 1)
                act.activation(h_aff[:], ps_pre[:], ACT.Identity, bias=col(R_LNB), scale=col(R_LNG)).then_inc(haff.sem, 1)

            def gap_exponential(n):
                await_(act, gap_done, n)
                act.activation(gexp[:], gap[:], ACT.Exp).then_inc(gap_exp.sem, 1)

            def gates_out(n):
                await_(act, comb_tp, n)
                await_(act, comb_rowed, n - 1)
                act.activation(comb_t[:], ps_pre[0:E, :], ACT.Identity).then_inc(comb_ct.sem, 1)

            def relu(n, e, j):
                await_(act, hid_ps, n, e * FT + j + 1)
                free_hidden(act, n, e)
                act.activation(hid[e % 2][:, j, :], ps_hid[j % 2][:], ACT.Relu,
                               bias=col(R_B1 + e * FT + j)).then_inc(hid_done.sem, 1)

            def layernorm_affine(n, which):
                await_(act, xn_t[which], n)
                act.activation(hn[:], ps_c[:], ACT.Identity, bias=col(R_BE1 + 2 * which),
                               scale=col(R_G1 + 2 * which)).then_inc(hn_done[which].sem, 1)

            def qk_low(n, j, which):
                await_(act, qk_ps, n, 2 * j + which + 1)
                if j >= 1:
                    await_(act, qk_done, n, 2 * j - 1 + which)
                act.activation(lo_part[which][:], ps_x[which][:], ACT.Identity, bias=qk_mb[:, which, j:j + 1],
                               scale=cst[:, K_MQ + which:K_MQ + which + 1]).then_inc(qk_lo.sem, 1)

            def exponential(n, u):
                await_(act, x_ps, n, u + 1)
                if u >= 2:
                    await_(act, pv_done, n, u - 1)
                act.activation(flat(pt[u % 2]), ps_x[u % 2][:], ACT.Exp).then_inc(exp_done.sem, 1)

            def values_out(n, b):
                await_(act, pv_done, n, RG * (b + 1))
                if b >= 1:
                    await_(act, pv_turned, n, b)
                act.activation(pvt[:], ps_c[:], ACT.Identity).then_inc(pv_out.sem, 1)

            def context_out(n):
                await_(act, cx_t, n)
                act.activation(cxt[:], ps_c[:], ACT.Identity).then_inc(cxt_done.sem, 1)

            def gelu(n, j):
                await_(act, f1_ps, n, j + 1)
                act.activation(gl[:, j, :], ps_x[j % 2][:], ACT.Gelu, bias=col(R_FB1 + j)).then_inc(gelu_done.sem, 1)

            def emit(g, p, back, experts, pre):
                n, m = g - 1, g + 1
                for s in range(E):
                    for j in range(FT):
                        at = s * FT + j
                        if experts and at == 1:
                            broadcast_gates(act, g, p, 1)
                        if experts:
                            relu(g, s, j)
                        if back and at == A_NORM1:
                            layernorm_affine(n, 0)
                        if back and A_QK <= at < A_QK + HJ:
                            qk_low(n, at - A_QK, 0)
                            qk_low(n, at - A_QK, 1)
                        if pre and at == A_AFFINE:
                            affine(m)
                        for k in steps(at):
                            if back and turned(k + 1) is not None:
                                values_out(n, turned(k + 1))
                            if back and 1 <= k <= NU:
                                exponential(n, k - 1)
                            if pre and k == K_GATES:
                                gap_exponential(m)
                            if pre and k == K_GATES_T:
                                gates_out(m)
                        if back and at == A_CONTEXT:
                            context_out(n)
                        if back and at == A_NORM2:
                            layernorm_affine(n, 1)
                        if back and A_FFN <= at < A_FFN + FT:
                            gelu(n, at - A_FFN)
                if pre:
                    broadcast_gates(act, m, 1 - p, 0)

            affine(0)
            gap_exponential(0)
            gates_out(0)
            broadcast_gates(act, 0, 0, 0)
            iterations(act, emit)

        @block.tensor
        def _(pe):
            def three(o, wh, wl, xh, xl, start=True):
                pe.matmul(o, wh, xh, start=start, stop=False)
                pe.matmul(o, wh, xl, start=False, stop=False)
                return pe.matmul(o, wl, xh, start=False, stop=True)

            pe.wait_ge(cst_in, 16)
            pe.wait_ge(rows_in, 16 * N_ROW_LOADS)
            pe.transpose(ps_s[:, 0:R_N], rows[:], ident[0:R_N, 0:R_N]).then_inc(cols_ps, 1)
            pe.wait_ge(rest_in, 16 * N_REST_LOADS)
            pe.wait_ge(hot_step, 2)
            pe.matmul(ps_x[0][0:64, 0:B], subj[:], onehot[:], start=True, stop=True).then_inc(se_ps, 1)
            pe.wait_ge(se_done, 1)
            pe.matmul(ps_x[1][:, 0:B], hw1[:], se[:], start=True, stop=True).then_inc(hyp1_ps, 1)
            pe.wait_ge(hyp1_done, 1)
            pe.matmul(ps_c[:, 0:B], hw2[:], hyp1[:], start=True, stop=True).then_inc(hyp2_ps, 1)
            pe.wait_ge(hyp2_done, 1)
            pe.matmul(ps_hid[0][0:64, 0:B], sw1[:], hyp2[:], start=True, stop=True).then_inc(sty1_ps, 1)
            pe.wait_ge(sty1_done, 1)
            pe.matmul(ps_hid[1][:, 0:B], sw2[:, 0:D], sty1[:], start=True, stop=True).then_inc(style_ps, 1)
            pe.matmul(ps_exp[:, 0:B], sw2[:, D:2 * D], sty1[:], start=True, stop=True).then_inc(style_ps, 1)
            pe.wait_ge(spread, N_SPREAD)
            for which, row in enumerate((bqe, bke)):
                for j in range(HJ):
                    mm = pe.matmul(ps_pre[:, which * HJ + j:which * HJ + j + 1], row[:, j * P:(j + 1) * P],
                                   ones1[:, 0:1], start=True, stop=True)
            mm.then_inc(bias_ps, 1)
            pe.wait_ge(bias_done, 2)
            pe.wait_ge(style_done, 2)
            pe.wait_ge(masks, 4)

            def pre_transpose(n):
                await_(pe, ln0_xn, n)
                await_(pe, comb_ct, n - 1)
                for b in range(GB):
                    mm = pe.transpose(ps_pre[:, b * T:(b + 1) * T], xn[:, b, :], ident)
                mm.then_inc(xn0_t.sem, 1)

            def router(n, back):
                await_(pe, h32_done, n)
                await_(pe, haff, n)
                if back:
                    await_(pe, cx_done, n - 2, 1)
                for b in range(GB):
                    mm = pe.matmul(ps_pre[:, b * E:(b + 1) * E], h32[:, b * T:(b + 1) * T], rw[:],
                                   start=True, stop=True)
                mm.then_inc(logits.sem, 1)

            def gates_transpose(n, back):
                await_(pe, comb_done, n)
                await_(pe, lg_copied, n)
                if back:
                    await_(pe, cx_done, n - 2, 3)
                for b in range(GB):
                    mm = pe.transpose(ps_pre[0:E, b * T:(b + 1) * T], comb[:, b, :], ident)
                mm.then_inc(comb_tp.sem, 1)

            def hidden(n, p, e, j):
                if e == 0 and j == 0:
                    await_(pe, h_split, n)
                if isinstance(n, int) and n == 0 and j == 0:
                    pe.wait_ge(w1_split, 2 * (e + 1))
                evicted(pe, n, e, j - 2)
                w = slice(e * FF + j * P, e * FF + (j + 1) * P)
                three(ps_hid[j % 2][:], w1h[:, w], w1l[:, w], hh[p][:], hl[p][:]).then_inc(hid_ps.sem, 1)

            def evicted(eng, n, e, j):
                if j < 0:
                    e, j = e - 1, j + FT
                if e < 0:
                    n, e = n - 1, E - 1
                await_(eng, hid_done, n, e * FT + j + 1)

            def expert_out(n, e):
                if isinstance(n, int) and n == 0:
                    pe.wait_ge(w2_in, 16 * E)
                if e >= 1:
                    await_(pe, gated_done, n, e)
                else:
                    await_(pe, gated_done, n - 1)
                for j in range(FT):
                    evicted(pe, n, e, j)
                    mm = pe.matmul(ps_exp[:], w2[:, e, j, :], hid[e % 2][:, j, :], start=(j == 0), stop=(j == FT - 1))
                mm.then_inc(exp_ps.sem, 1)

            def y_transpose(n, p):
                await_(pe, y_added, n)
                for b in range(GB):
                    mm = pe.transpose(ps_c[:, b * D:(b + 1) * D], y_t[p][:, b * T:(b + 1) * T], ident)
                mm.then_inc(y_back.sem, 1)

            def pde_rows(n):
                await_(pe, u_done, n)
                await_(pe, pde_pool, n, 2)
                pe.matmul(ps_s[:], cst[:, K_GX:K_GX + P], flat(u_), start=True, stop=False)
                pe.matmul(ps_s[:], cst[:, K_GXX:K_GXX + P], flat(v_), start=False, stop=True).then_inc(pde_ps.sem, 1)

            def norm_transpose(n, which):
                await_(pe, ln_xn[which], n)
                await_(pe, (f_done, cxt_done)[which], n)
                for b in range(GB):
                    mm = pe.transpose(ps_c[:, b * T:(b + 1) * T], xn0[:, b, :], ident)
                mm.then_inc(xn_t[which].sem, 1)

            def project_v(n):
                await_(pe, hn_split[0], n)
                for b in range(GB):
                    t = slice(b * T, (b + 1) * T)
                    mm = three(ps_c[:, b * D:(b + 1) * D], hnh[:, t], hnl[:, t], wvh[:], wvl[:])
                mm.then_inc(v_ps.sem, 1)

            def project_qk(n, j):
                for which, (wh, wl) in enumerate(((wqh, wql), (wkh, wkl))):
                    if j >= 1:
                        await_(pe, qk_done, n, 2 * j - 1 + which)
                    w = slice(j * P, (j + 1) * P)
                    three(ps_x[which][:], wh[:, w], wl[:, w], hnh[:], hnl[:]).then_inc(qk_ps.sem, 1)

            def head_scores(o, lhs, rhs, b, i):
                r = slice(32 * i, 32 * i + 32)
                for j in range(HJ):
                    mm = pe.matmul(o[:, j * T:(j + 1) * T], lhs[r, j, b, :], rhs[r, j, b, :],
                                   start=False, stop=(j == HJ - 1), skip_group_check=True)
                return mm

            def scores(n, u):
                b, i = divmod(u, RG)
                if u == 0:
                    await_(pe, df_done, n)
                    await_(pe, qk_done, n)
                else:
                    await_(pe, mx_done, n, u)
                pe.matmul(ps_s[:], id16[:], bc(mask16[:], HJ), start=True, stop=False, skip_group_check=True)
                head_scores(ps_s, qs, ks, b, i).then_inc(s_ps.sem, 1)

            def scores_less_max(n, u):
                b, i = divmod(u, RG)
                if u >= 2:
                    await_(pe, exp_done, n, u - 1)
                o = ps_x[u % 2]
                pe.matmul(o[:], id16[:], bc(maskT16[:], HJ), start=True, stop=False, skip_group_check=True)
                head_scores(o, ks, qs, b, i)
                await_(pe, dg_done, n, u + 1)
                pe.matmul(o[:], ones_r[:], flat(dg[u % 2]), start=False, stop=True,
                          skip_group_check=True).then_inc(x_ps.sem, 1)

            def weighted_values(n, u):
                b, i = divmod(u, RG)
                await_(pe, exp_done, n, u + 1)
                if u == 0:
                    await_(pe, v_done, n)
                elif i == 0:
                    await_(pe, pv_out, n, b)
                for j in range(HJ):
                    mm = pe.matmul(ps_c[32 * j:32 * j + VW, i * T:(i + 1) * T], vs[:, b, j * RG + i, :],
                                   pt[u % 2][:, j, :], start=True, stop=True)
                mm.then_inc(pv_done.sem, 1)

            def turn_values(n, m, b):
                await_(pe, pv_out, n, b + 1)
                if m is not None and b < 2:
                    await_(pe, (haff, lg_copied)[b], m)
                elif m is not None and b == 3:
                    await_(pe, comb_ct, m)
                if b >= 1:
                    await_(pe, cx_done, n, b)
                for i in range(RG):
                    mm = pe.transpose(ps_pre[:, i * P:(i + 1) * P], pvt[:, i * T:(i + 1) * T], ident)
                mm.then_inc(pv_turned.sem, 1)

            def context_transpose(n):
                await_(pe, cx_done, n)
                for b in range(GB):
                    mm = pe.transpose(ps_c[:, b * T:(b + 1) * T], cx[:, b, :], ident)
                mm.then_inc(cx_t.sem, 1)

            def project_out(n):
                await_(pe, cxt_done, n)
                await_(pe, mx_done, n)
                for b in range(GB):
                    mm = pe.matmul(ps_s[:, b * D:(b + 1) * D], cxt[:, b * T:(b + 1) * T], wo[:], start=True, stop=True)
                mm.then_inc(wo_ps.sem, 1)

            def ffn_hidden(n, j):
                if j == 0:
                    await_(pe, hn_split[1], n)
                if j < 2:
                    await_(pe, exp_done, n, NU - 1 + j)
                else:
                    await_(pe, gelu_done, n, j - 1)
                w = slice(j * P, (j + 1) * P)
                three(ps_x[j % 2][:], f1h[:, w], f1l[:, w], hnh[:], hnl[:]).then_inc(f1_ps.sem, 1)

            def ffn_out(n):
                await_(pe, gelu_done, n)
                await_(pe, xa2_done, n)
                for b in range(GB):
                    for j in range(FT):
                        mm = pe.matmul(ps_s[:, b * D:(b + 1) * D], gl[:, j, b * T:(b + 1) * T], f2[:, j, :],
                                       start=(j == 0), stop=(j == FT - 1))
                mm.then_inc(f2_ps.sem, 1)

            def attention_step(n, m, k):
                if k < NU:
                    scores(n, k)
                if 1 <= k <= NU:
                    scores_less_max(n, k - 1)
                if 2 <= k < NU + 2:
                    weighted_values(n, k - 2)
                if turned(k) is not None:
                    turn_values(n, m, turned(k))

            def emit(g, p, back, experts, pre):
                n, m = g - 1, g + 1
                for s in range(E):
                    for j in range(FT):
                        at = s * FT + j
                        if experts:
                            if j == 2 and s >= 1:
                                expert_out(g, s - 1)
                            hidden(g, p, s, j)
                        if back and at == A_Y:
                            y_transpose(n, 1 - p)
                        if back and at == A_PDE:
                            pde_rows(n)
                        if back and at == A_NORM1:
                            norm_transpose(n, 0)
                        if back and at == A_QK:
                            project_v(n)
                        if back and A_QK <= at < A_QK + HJ:
                            project_qk(n, at - A_QK)
                        if pre and at == A_AFFINE:
                            pre_transpose(m)
                        for k in steps(at):
                                if back:
                                    attention_step(n, m if pre else None, k)
                                if pre and k == K_ROUTER:
                                    router(m, back)
                                if pre and k == K_GATES_T:
                                    gates_transpose(m, back)
                        if back and at == A_CONTEXT:
                            context_transpose(n)
                        if back and at == A_WO:
                            project_out(n)
                        if back and at == A_NORM2:
                            norm_transpose(n, 1)
                        if back and A_FFN <= at < A_FFN + FT:
                            ffn_hidden(n, at - A_FFN)
                        if back and at == A_FFN_OUT:
                            ffn_out(n)
                if experts:
                    expert_out(g, E - 1)

            pre_transpose(0)
            router(0, False)
            gates_transpose(0, False)
            iterations(pe, emit)

        @block.vector
        def _(dve):
            V = nc.vector
            dve.wait_ge(cst_in, 16)
            dve.wait_ge(rest_in, 16 * N_REST_LOADS)
            V.tensor_copy(ids_f[:], ids_i[:]).then_inc(hot_step, 1)
            dve.wait_ge(hot_step, 1)
            V.tensor_scalar(onehot[:], ids_f[:], cst[0:32, K_IOTA:K_IOTA + 1], None, ALU.is_equal).then_inc(hot_step, 1)
            k = 0
            for dst, src, scale in ((wqe, wq_raw, DH ** -0.5), (wke, wk_raw, 1.0), (bqe, bq_row, DH ** -0.5), (bke, bk_row, 1.0)):
                V.memset(dst[:], 0.0).then_inc(spread, 1)
                k += 1
                dve.wait_ge(spread, k)
                for r in range(3):
                    V.tensor_scalar(dst[:].rearrange("p (h r d) -> p r h d", r=4, d=DH)[:, r],
                                    src[:].rearrange("p (h d) -> p h d", d=DH), scale, None, ALU.mult).then_inc(spread, 1)
                    k += 1
            V.memset(ones1[:], 1.0).then_inc(spread, 1)
            assert k + 1 == N_SPREAD
            dve.wait_ge(spread, N_SPREAD)
            dve.wait_ge(se_ps, 1)
            V.tensor_copy(se[:], ps_x[0][0:64, 0:B]).then_inc(se_done, 1)
            k = 0

            def step(ins):
                nonlocal k
                k += 1
                ins.then_inc(angles, 1)
                dve.wait_ge(angles, k)

            for quarter in range(2):
                c = slice(2 * quarter, 2 * quarter + 2)
                step(V.tensor_scalar(ang_k[:, c], cond_in[:, 2:4, :], 1 / (2 * np.pi), 0.25 * quarter, ALU.mult, ALU.add))
                step(V.tensor_scalar(ang_r[:, c], ang_k[:, c], ROUND, None, ALU.add))
                step(V.tensor_scalar(ang_k[:, c], ang_r[:, c], ROUND, None, ALU.subtract))
                step(V.scalar_tensor_tensor(ang_r[:, c], ang_k[:, c], -TWO_PI_HI, cond_in[:, 2:4, :], ALU.mult, ALU.add))
                step(V.scalar_tensor_tensor(ang_r[:, c], ang_k[:, c], -TWO_PI_MID, ang_r[:, c], ALU.mult, ALU.add))
                step(V.scalar_tensor_tensor(ang_r[:, c], ang_k[:, c], -TWO_PI_LO, ang_r[:, c], ALU.mult, ALU.add))
                step(V.tensor_scalar(ang_r[:, c], ang_r[:, c], 0.5 * np.pi * quarter, 3.1415925, ALU.add, ALU.min))
                step(V.tensor_scalar(ang_r[:, c], ang_r[:, c], -3.1415925, None, ALU.max))
            assert k == N_ANGLES
            dve.wait_ge(sines, 1)
            for c, src in ((C_DT, cond_in[:, 0, :]), (C_GATE, cond_in[:, 1, :]), (C_COS, ang[:, 2, :]),
                           (C_COS + 1, ang[:, 2, :]), (C_COS + 2, ang[:, 3, :]), (C_COS + 3, ang[:, 3, :]),
                           (C_SIN, ang[:, 0, :]), (C_SIN + 2, ang[:, 1, :])):
                V.tensor_copy(cond[:, :, c], src).then_inc(conds, 1)
            for c, src in ((C_SIN + 1, ang[:, 0, :]), (C_SIN + 3, ang[:, 1, :])):
                V.tensor_scalar(cond[:, :, c], src, -1.0, None, ALU.mult).then_inc(conds, 1)
            V.tensor_copy(id16[:], ident).then_inc(masks, 1)
            V.tensor_copy(mask16[:], cst[:, K_MASK:K_MASK + P]).then_inc(masks, 1)
            V.tensor_copy(maskT16[:], cst[:, K_MASKT:K_MASKT + P]).then_inc(masks, 1)
            V.tensor_scalar(ones_r[:], ident, 0.0, 1.0, ALU.mult, ALU.add).then_inc(masks, 1)
            dve.wait_ge(bias_ps, 1)
            V.tensor_copy(qk_b[:].rearrange("p w j -> p (w j)"), ps_pre[:, 0:2 * HJ]).then_inc(bias_done, 1)
            dve.wait_ge(bias_done, 1)
            V.tensor_tensor(qk_mb[:], qk_b[:], inner(cst[:, K_MQ:K_MQ + 2], HJ), ALU.mult).then_inc(bias_done, 1)
            dve.wait_ge(style_done, 2)
            V.scalar_tensor_tensor(sp_b[:], sp_a[:], -1.0, sp_a[:], ALU.mult, ALU.min).then_inc(soft_v, 1)
            dve.wait_ge(soft_a, 2)
            V.scalar_tensor_tensor(sp_c[:], sp_a[:], 0.0, sp_b[:], ALU.max, ALU.add).then_inc(soft_v, 1)
            dve.wait_ge(soft_v, 2)
            V.tensor_scalar(style[:, 0, :], sp_c[:], 1e-8, None, ALU.add).then_inc(soft_v, 1)
            k = 0

            def grid(ins):
                nonlocal k
                k += 1
                ins.then_inc(grids, 1)
                dve.wait_ge(grids, k)

            grid(V.tensor_scalar(g_b2[:], bg[:, 2, :], 0.5, None, ALU.mult))
            grid(V.tensor_tensor(g_p[:], bg[:, 1, :], ag[:, 1, :], ALU.subtract))
            grid(V.tensor_scalar(g_p[:], g_p[:], 0.5, None, ALU.mult))
            grid(V.tensor_tensor(g_m[:], bg[:, 1, :], ag[:, 1, :], ALU.add))
            grid(V.tensor_scalar(g_m[:], g_m[:], 0.5, None, ALU.mult))
            for side, lo in enumerate((0, D - 4)):
                ka = cst[:, K_AE + 4 * side:K_AE + 4 * side + 4]
                kb = cst[:, K_BE + 4 * side:K_BE + 4 * side + 4]
                grid(V.tensor_tensor(edge_t[:, side, :], ag[:, 1, lo:lo + 4], ka, ALU.mult))
                grid(V.tensor_tensor(g_edge[:, side, :], bg[:, 1, lo:lo + 4], kb, ALU.mult))
                grid(V.tensor_tensor(g_edge[:, side, :], g_edge[:, side, :], edge_t[:, side, :], ALU.add))

            def split(raw_, hi, lo, sem_, k):
                V.tensor_copy(hi, raw_).then_inc(sem_, 1)
                dve.wait_ge(sem_, k + 1)
                V.tensor_tensor(lo, raw_, hi, ALU.subtract).then_inc(sem_, 1)

            for i, (r_, hi, lo) in enumerate(((wqe, wqh, wql), (wke, wkh, wkl), (wv_raw, wvh, wvl), (f1_raw, f1h, f1l))):
                split(r_[:], hi[:], lo[:], split_w, 2 * i)

            def split_w1(e):
                dve.wait_ge(w1_in, 16 * E)
                w = slice(e * FF, (e + 1) * FF)
                split(raw[:, w], w1h[:, w], w1l[:, w], w1_split, 2 * e)

            def mean_var(n, src, st, mv, s_stats, s_mv):
                for b in range(GB):
                    V.bn_stats(st[:, b, :], src(b)).then_inc(s_stats.sem, 1)
                await_(dve, s_stats, n)
                apart(nc.vector)
                for b in range(GB):
                    V.bn_aggr(mv[:, b, :], st[:, b, :]).then_inc(s_mv.sem, 1)

            def normalize(dst, src, mv, rs):
                for b in range(GB):
                    ins = V.tensor_scalar(dst[:, b, :], src[:, b, :], mv[:, b, 0:1], rs[:, b:b + 1],
                                          ALU.subtract, ALU.mult)
                return ins

            def pre_stats(n):
                await_(dve, xa_in, n)
                await_(dve, ln0_ve, n - 1)
                mean_var(n, lambda b: xa[:, b, :], st0, mv0, ln0_stats, ln0_mv)

            def pre_normalize(n):
                await_(dve, ln0_rs, n)
                await_(dve, ln0_mv, n)
                await_(dve, xn0_t, n - 1)
                normalize(xn, xa, mv0, rs0).then_inc(ln0_xn.sem, 1)

            def inorm_stats(n):
                await_(dve, haff, n)
                mean_var(n, lambda b: h_aff[:, b * T:(b + 1) * T], sti, mvi, in_stats, in_mv)

            def inorm_apply(n):
                await_(dve, in_coef, n)
                await_(dve, logits, n - 1)
                for b in range(GB):
                    t = slice(b * T, (b + 1) * T)
                    ins = V.tensor_scalar(h32[:, t], h_aff[:, t], in_s[:, b:b + 1], in_t[:, b:b + 1], ALU.mult, ALU.add)
                ins.then_inc(h32_done.sem, 1)

            def h_high(n, p):
                await_(dve, h32_done, n)
                await_(dve, hid_ps, n - 2)
                V.tensor_copy(hh[p][:], h32[:]).then_inc(hh_done.sem, 1)

            def h_low(n, p):
                await_(dve, hh_done, n)
                V.tensor_tensor(hl[p][:], h32[:], hh[p][:], ALU.subtract).then_inc(h_split.sem, 1)

            def top_two(n):
                await_(dve, logits, n)
                V.tensor_copy(lg[:].rearrange("p b e -> p (b e)"), ps_pre[:, 0:GB * E]).then_inc(lg_copied.sem, 1)
                await_(dve, lg_copied, n)
                apart(nc.vector)
                for b in range(GB):
                    V.max(top[:, b, :], lg[:, b, :]).then_inc(topped.sem, 1)
                await_(dve, topped, n)
                V.tensor_tensor(gap[:], top[:, :, 1], top[:, :, 0], ALU.subtract).then_inc(gap_done.sem, 1)
                for b in range(GB):
                    ins = V.max_index(top_i[:, b, :], top[:, b, :], lg[:, b, :])
                ins.then_inc(topi_done.sem, 1)

            def gates_of_two(n):
                await_(dve, topi_done, n)
                V.tensor_copy(top_f[:], top_i[:, :, 0:2].rearrange("p b k -> p k b")).then_inc(gate_step.sem, 1)
                await_(dve, gap_exp, n)
                V.tensor_scalar(gsum[:], gexp[:], 1.0, None, ALU.add).then_inc(gate_step.sem, 1)
                await_(dve, gate_step, n, 2)
                V.reciprocal(gates[:, 0, :], gsum[:]).then_inc(gate_step.sem, 1)
                await_(dve, gate_step, n, 3)
                V.tensor_tensor(gates[:, 1, :], gates[:, 0, :], gexp[:], ALU.mult).then_inc(gate_step.sem, 1)
                for k in range(2):
                    V.tensor_tensor(pick[:, k], inner(top_f[:, k, :], E), bc(cst[:, K_E8:K_E8 + E], GB),
                                    ALU.is_equal).then_inc(gate_step.sem, 1)
                await_(dve, gate_step, n, 6)
                V.tensor_tensor(pick[:], pick[:], gates[:].unsqueeze(3).broadcast_to([P, 2, GB, E]),
                                ALU.mult).then_inc(gate_step.sem, 1)
                await_(dve, gate_step, n, 7)
                await_(dve, comb_tp, n - 1)
                V.tensor_tensor(comb[:], pick[:, 0], pick[:, 1], ALU.add).then_inc(comb_done.sem, 1)

            def gate(n, p, e):
                await_(dve, exp_ps, n, e + 1)
                await_(dve, comb_bc[e % 2], n, 16 * (e // 2 + 1))
                if e >= 1:
                    dst = gated[e % 2]
                    if e >= 3:
                        await_(dve, y_added, n, e - 2)
                    else:
                        await_(dve, y_added, n - 1)
                else:
                    dst = y_t[p]
                V.scalar_tensor_tensor(dst[:], ps_exp[:], col(R_B2 + e), comb_b[e % 2][:],
                                       ALU.add, ALU.mult).then_inc(gated_done.sem, 1)

            def pde(n, piece):
                if piece == 0:
                    await_(dve, y_back, n)
                    await_(dve, xb_in, n)
                    V.tensor_tensor(flat(f), ps_c[:], flat(xb), ALU.add).then_inc(f_done.sem, 1)
                    await_(dve, f_done, n)
                if piece == 1:
                    V.tensor_tensor(rb[:], f[:], bc(g_b2[:], GB), ALU.mult).then_inc(pde_v.sem, 1)
                    await_(dve, pde_v, n, 1)
                    V.tensor_tensor(u_[:, :, 1:D - 1], rb[:, :, 2:D], rb[:, :, 0:D - 2], ALU.subtract).then_inc(pde_v.sem, 1)
                if piece == 2:
                    V.tensor_tensor(eu[:], edges(rb, 3), cst[:, K_GE:K_GE + 6].rearrange("p (s k) -> p s k", s=2)
                                    .unsqueeze(1).broadcast_to([P, GB, 2, 3]), ALU.mult).then_inc(pde_v.sem, 1)
                    await_(dve, pde_v, n, 3)
                    V.tensor_reduce(u_[:, :, 0:D:D - 1], eu[:], AX.X, ALU.add).then_inc(pde_v.sem, 1)
                    await_(dve, pde_v, n, 4)
                    await_(dve, pde_pool, n, 1)
                    V.tensor_tensor(u_[:], u_[:], ua[:], ALU.subtract).then_inc(u_done.sem, 1)
                if piece == 3:
                    V.tensor_tensor(wp[:], f[:], bc(g_p[:], GB), ALU.mult).then_inc(pde_v.sem, 1)
                    V.tensor_tensor(wm[:], f[:], bc(g_m[:], GB), ALU.mult).then_inc(pde_v.sem, 1)
                if piece == 4:
                    await_(dve, pde_v, n, 6)
                    V.tensor_tensor(w_[:, :, 1:D - 1], wp[:, :, 2:D], wm[:, :, 0:D - 2], ALU.add).then_inc(pde_v.sem, 1)
                    V.tensor_tensor(ew[:], edges(f, 4), g_edge[:].unsqueeze(1).broadcast_to([P, GB, 2, 4]),
                                    ALU.mult).then_inc(pde_v.sem, 1)
                    await_(dve, pde_v, n, 8)
                    V.tensor_reduce(w_[:, :, 0:D:D - 1], ew[:], AX.X, ALU.add).then_inc(pde_v.sem, 1)
                    await_(dve, pde_pool, n)
                    V.tensor_tensor(w_[:, :, 1:D - 1], w_[:, :, 1:D - 1], bf[:, :, 1:D - 1], ALU.subtract).then_inc(pde_v.sem, 1)
                if piece == 5:
                    await_(dve, pde_v, n)
                    await_(dve, pde_ps, n)
                    V.tensor_tensor(flat(df), ps_s[:], flat(w_), ALU.add).then_inc(df_done.sem, 1)
                    await_(dve, df_done, n)
                    await_(dve, cond_ready, n)
                    for b in range(GB):
                        V.scalar_tensor_tensor(fn[:, b, :], df[:, b, :], cond_g[:, b, C_DT:C_DT + 1], f[:, b, :],
                                               ALU.mult, ALU.add).then_inc(fn_done.sem, 1)
                    await_(dve, fn_done, n)
                    V.tensor_scalar(x1in[:], fn[:], 0.0, None, ALU.max).then_inc(x1in_done.sem, 1)

            def edges(t, w):
                v = t[:]
                return bass.AP(v.tensor, v.offset, [list(v.ap[0]), list(v.ap[1]), [D - w, 2], [1, w]])

            def norm_stats(n, which):
                src = (x1in, xa2)[which]
                await_(dve, (x1in_done, xa2_done)[which], n)
                mean_var(n, lambda b: src[:, b, :], stn, mvn, ln_stats[which], ln_mv[which])

            def norm_apply(n, which):
                await_(dve, ln_rs[which], n)
                await_(dve, ln_mv[which], n)
                if which == 1:
                    await_(dve, xn_t[0], n)
                normalize(xn0, (x1in, xa2)[which], mvn, rsn).then_inc(ln_xn[which].sem, 1)

            def norm_split(n, which):
                await_(dve, hn_done[which], n)
                V.tensor_copy(hnh[:], hn[:]).then_inc(hnh_done[which].sem, 1)
                await_(dve, hnh_done[which], n)
                V.tensor_tensor(hnl[:], hn[:], hnh[:], ALU.subtract).then_inc(hn_split[which].sem, 1)

            def qk_out(n, j, which):
                await_(dve, qk_lo, n, 2 * j + which + 1)
                dst = (qs, ks)[which]
                V.scalar_tensor_tensor(dst[:, j].rearrange("p b t -> p (b t)"), ps_x[which][:], qk_b[:, which, j:j + 1],
                                       lo_part[which][:], ALU.add, ALU.subtract).then_inc(qk_done.sem, 1)

            def v_out(n):
                await_(dve, v_ps, n)
                V.tensor_tensor(vs[:, :, :, 0:DH], ps_c[:].rearrange("p (b h d) -> p b h d", b=GB, d=DH),
                                bv_b[:].rearrange("p (h d) -> p h d", d=DH).unsqueeze(1).broadcast_to([P, GB, NH, DH]),
                                ALU.add).then_inc(v_done.sem, 1)

            def maximum(n, u):
                await_(dve, s_ps, n, u + 1)
                if u >= 2:
                    await_(dve, dg_done, n, u - 1)
                V.tensor_reduce(mx[u % 2][:], ps_s[:].rearrange("p (j t) -> p j t", j=HJ), AX.X, ALU.max).then_inc(mx_done.sem, 1)

            def context(n, b):
                await_(dve, pv_turned, n, b + 1)
                c = ps_pre[:].rearrange("p (i j d) -> p i j d", i=RG, d=32)
                V.reciprocal(rden[:], c[:, :, :, DH]).then_inc(rden_done.sem, 1)
                await_(dve, rden_done, n, b + 1)
                V.tensor_tensor(cx[:, b, :].rearrange("p (j i d) -> p i j d", i=RG, d=DH), c[:, :, :, 0:DH],
                                rden[:].unsqueeze(3).broadcast_to([P, RG, HJ, DH]), ALU.mult).then_inc(cx_done.sem, 1)

            def residual_1(n):
                await_(dve, wo_ps, n)
                await_(dve, xbo_done, n)
                V.tensor_tensor(flat(xa2), ps_s[:], flat(xbo), ALU.add).then_inc(xa2_done.sem, 1)

            def blend(n):
                await_(dve, f2_ps, n)
                await_(dve, sofar_done, n)
                V.tensor_tensor(flat(x2a), ps_s[:], flat(x2b), ALU.add).then_inc(delta_done.sem, 1)
                await_(dve, delta_done, n)
                for b in range(GB):
                    V.scalar_tensor_tensor(res[:, b, :], x2a[:, b, :], cond_g[:, b, C_GATE:C_GATE + 1], x1in[:, b, :],
                                           ALU.mult, ALU.add).then_inc(res_done.sem, 1)

            def emit(g, p, back, experts, pre):
                n, m = g - 1, g + 1
                for s in range(E):
                    for j in range(FT):
                        at = s * FT + j
                        if experts and isinstance(g, int) and g == 0 and j == 0 and s >= 1:
                            split_w1(s)
                        if experts and j == 2 and s >= 1:
                            gate(g, p, s - 1)
                        if back and A_Y <= at < A_Y + 5:
                            pde(n, at - A_Y)
                        if back and at == A_PDE:
                            pde(n, 5)
                        if back and at == A_STATS1:
                            norm_stats(n, 0)
                        if back and at == A_NORM1:
                            norm_apply(n, 0)
                        if back and at == A_QK:
                            norm_split(n, 0)
                            v_out(n)
                        if back and A_QK <= at < A_QK + HJ:
                            qk_out(n, at - A_QK, 0)
                            qk_out(n, at - A_QK, 1)
                        if pre and at == A_STATS:
                            pre_stats(m)
                        if pre and at == A_AFFINE:
                            pre_normalize(m)
                        for k in steps(at):
                            if pre and k == K_INORM:
                                inorm_stats(m)
                            if pre and k == K_INORM + 3:
                                inorm_apply(m)
                                h_high(m, 1 - p)
                                h_low(m, 1 - p)
                            if back and k < NU:
                                maximum(n, k)
                            if back and turned(k) is not None:
                                context(n, turned(k))
                            if pre and k == K_ROUTER:
                                top_two(m)
                            if pre and k == K_GATES + 1:
                                gates_of_two(m)
                        if back and at == A_WO:
                            residual_1(n)
                        if back and at == A_STATS2:
                            norm_stats(n, 1)
                        if back and at == A_NORM2:
                            norm_apply(n, 1)
                        if back and at == A_FFN - 1:
                            norm_split(n, 1)
                        if back and at == A_FFN_OUT:
                            blend(n)
                if experts:
                    gate(g, p, E - 1)

            pre_stats(0)
            pre_normalize(0)
            inorm_stats(0)
            inorm_apply(0)
            h_high(0, 0)
            h_low(0, 0)
            split_w1(0)
            top_two(0)
            gates_of_two(0)
            iterations(dve, emit)

        @block.gpsimd
        def _(pool):
            G = nc.gpsimd
            G.memset(rows[:], 0.0).then_inc(rows_zero, 1)
            G.memset(neg_half[:], -0.5).then_inc(halves, 1)
            G.memset(ln_eps[:], LN_EPS).then_inc(halves, 1)
            G.memset(inorm_eps[:], INORM_EPS).then_inc(halves, 1)
            G.memset(vs[:], 1.0).then_inc(halves, 1)
            pool.wait_ge(halves, 4)
            pool.wait_ge(cst_in, 16)

            def rsqrt(n, ve, rs, mv, eps, s_mv, s_ve, s_rs, reader):
                await_(pool, s_mv, n)
                G.tensor_tensor(ve[:], mv[:, :, 1], eps[:], ALU.add).then_inc(s_ve.sem, 1)
                await_(pool, s_ve, n)
                if reader is not None:
                    await_(pool, reader, n - 1)
                G.tensor_tensor(rs[:], ve[:], neg_half[:], ALU.pow).then_inc(s_rs.sem, 1)

            def pre_root(n):
                rsqrt(n, ve0, rs0, mv0, ln_eps, ln0_mv, ln0_ve, ln0_rs, ln0_xn)

            def inorm_coefficients(n):
                rsqrt(n, vei, rsi, mvi, inorm_eps, in_mv, in_ve, in_rs, None)
                if isinstance(n, int) and n == 0:
                    pool.wait_ge(soft_v, 3)
                G.tensor_copy(sty_g[:], style[:, :, bass.ds(n * GB, GB)]).then_inc(in_styled.sem, 1)
                await_(pool, in_rs, n)
                await_(pool, in_styled, n)
                await_(pool, h32_done, n - 1)
                G.tensor_tensor(in_s[:], rsi[:], sty_g[:, 0, :], ALU.mult).then_inc(in_step.sem, 1)
                await_(pool, in_step, n, 1)
                G.tensor_tensor(in_ms[:], mvi[:, :, 0], in_s[:], ALU.mult).then_inc(in_step.sem, 1)
                await_(pool, in_step, n, 2)
                G.tensor_tensor(in_t[:], sty_g[:, 1, :], in_ms[:], ALU.subtract).then_inc(in_coef.sem, 1)

            def add_expert(n, p, e):
                await_(pool, gated_done, n, e + 1)
                if e >= 2:
                    await_(pool, y_added, n, e - 1)
                G.tensor_tensor(y_t[p][:], y_t[p][:], gated[e % 2][:], ALU.add).then_inc(y_added.sem, 1)

            def pde_products(n):
                await_(pool, f_done, n)
                for dst, grid_ in ((ua, ag[:, 0, :]), (v_, bg[:, 0, :]), (bf, bg[:, 1, :])):
                    G.tensor_tensor(dst[:], f[:], bc(grid_, GB), ALU.mult).then_inc(pde_pool.sem, 1)

            def conditions(n):
                if isinstance(n, int) and n == 0:
                    pool.wait_ge(conds, N_CONDS)
                G.tensor_copy(cond_g[:], cond[:, bass.ds(n * GB, GB), :]).then_inc(cond_ready.sem, 1)

            def norm_root(n, which):
                rsqrt(n, ven, rsn, mvn, ln_eps, ln_mv[which], ln_ve[which], ln_rs[which], None)

            def minus_maximum(n, u):
                await_(pool, mx_done, n, u + 1)
                if u >= 2:
                    await_(pool, x_ps, n, u - 1)
                G.tensor_tensor(dg[u % 2][:], bc(negid, HJ), inner(mx[u % 2][:], T), ALU.mult).then_inc(dg_done.sem, 1)

            def input_and_bias(n):
                await_(pool, x1in_done, n)
                G.tensor_tensor(xbo[:], x1in[:], bc(bo_b[:], GB), ALU.add).then_inc(xbo_done.sem, 1)

            def change_so_far(n):
                await_(pool, xa2_done, n)
                G.tensor_tensor(x2b[:], xa2[:], bc(fb2_b[:], GB), ALU.add).then_inc(x2b_done.sem, 1)
                await_(pool, x2b_done, n)
                G.tensor_tensor(x2b[:], x2b[:], x1in[:], ALU.subtract).then_inc(sofar_done.sem, 1)

            def rotate(n):
                await_(pool, res_done, n)
                r = res[:].rearrange("p b (k c) -> p b k c", c=4)
                w = t2[:].rearrange("p b (k c) -> p b k c", c=4)

                def coef(c, m):
                    v = cond_g[:, :, c:c + 4 if m == 1 else c + 3:m]
                    return v.unsqueeze(2).broadcast_to([P, GB, D // 4, 4 // m])

                G.tensor_tensor(t1[:].rearrange("p b (k c) -> p b k c", c=4), r, coef(C_COS, 1), ALU.mult).then_inc(rot_step.sem, 1)
                G.tensor_tensor(w[:, :, :, 0::2], r[:, :, :, 1::2], coef(C_SIN, 2), ALU.mult).then_inc(rot_step.sem, 1)
                G.tensor_tensor(w[:, :, :, 1::2], r[:, :, :, 0::2], coef(C_SIN + 1, 2), ALU.mult).then_inc(rot_step.sem, 1)
                await_(pool, rot_step, n)
                await_(pool, stored, n)
                G.tensor_tensor(fin[:], t1[:], t2[:], ALU.add).then_inc(rotated.sem, 1)

            def emit(g, p, back, experts, pre):
                n, m = g - 1, g + 1
                if back:
                    conditions(n)
                for s in range(E):
                    for j in range(FT):
                        at = s * FT + j
                        if experts and j == 3 and s >= 2:
                            add_expert(g, p, s - 1)
                        if back and at == A_Y:
                            pde_products(n)
                        if back and at == A_STATS1:
                            norm_root(n, 0)
                        if back and at == A_QK:
                            input_and_bias(n)
                        if pre and at == A_STATS:
                            pre_root(m)
                        for k in steps(at):
                            if pre and k == K_INORM:
                                inorm_coefficients(m)
                            if back and k < NU:
                                minus_maximum(n, k)
                        if back and at == A_STATS2:
                            norm_root(n, 1)
                        if back and at == A_NORM2:
                            change_so_far(n)
                        if back and at == A_FFN_OUT:
                            rotate(n)
                if experts:
                    add_expert(g, p, E - 1)

            pre_root(0)
            inorm_coefficients(0)
            iterations(pool, emit)


def kernel(**inputs):
    import concourse.bacc as bacc
    from concourse.bass_utils import run_bass_kernel_spmd

    nc = bacc.Bacc("TRN2", target_bir_lowering=False, num_devices=1)
    arrays, args = {}, {}
    for name, value in list(inputs.items()) + [("cst", shape_constants())]:
        v = np.ascontiguousarray(value)
        arrays["in_" + name] = v
        args[name] = nc.dram_tensor("in_" + name, v.shape, mybir.dt.from_np(v.dtype), kind="ExternalInput").ap()
    out = nc.dram_tensor("out", (B, T, D), F32, kind="ExternalOutput").ap()
    cond_seq_kernel(nc, args, out)
    r = run_bass_kernel_spmd(nc, [arrays], core_ids=[0])
    return r.results[0]["out"]
```

```python
from contextlib import ExitStack

import numpy as np

import concourse.bass as bass
from concourse import mybir

F32 = mybir.dt.float32
F32R = mybir.dt.float32r
BF16 = mybir.dt.bfloat16
I32 = mybir.dt.int32
U32 = mybir.dt.uint32
ALU = mybir.AluOpType
ACT = mybir.ActivationFunctionType
AX = mybir.AxisListType

P = 128
B, T, D = 32, 128, 128
GB = 4
NG = B // GB
GT = GB * T
E, FF = 8, 512
FT = FF // P
NH, DH = 16, 8
RG = 4
HJ = NH // RG
NU = GB * RG
VW = DH + 1
LN_EPS, INORM_EPS = 1e-5, 1e-8
MASKED = -1.0e30
C_DT, C_GATE, C_COS, C_SIN, C_N = 0, 1, 2, 6, 10
TWO_PI_HI, TWO_PI_MID = 6.28125, 0.0019350051879882812
TWO_PI_LO = 2 * np.pi - 6.28125 - 0.0019350051879882812
ROUND = 12582912.0


def derivative_matrices(n):
    g, gg = np.zeros((n, n), np.float32), np.zeros((n, n), np.float32)
    for i in range(1, n - 1):
        g[i, i - 1], g[i, i + 1] = -0.5, 0.5
        gg[i, i - 1], gg[i, i], gg[i, i + 1] = 1, -2, 1
    g[0, :3], g[-1, -3:] = (-1.5, 2, -0.5), (0.5, -2, 1.5)
    gg[0, :4], gg[-1, -4:] = (2, -5, 4, -1), (-1, 4, -5, 2)
    return g, gg


R_B1 = 0
R_LNG, R_LNB, R_HB1, R_HB2, R_SB1, R_SB2 = (R_B1 + E * FT + i for i in range(6))
R_A = R_SB2 + 2
R_B2 = R_A
R_G1, R_BE1, R_G2, R_BE2 = (R_B2 + E + i for i in range(4))
R_FB1 = R_BE2 + 1
R_N = R_FB1 + FT

N_ROW_LOADS, N_NET_LOADS, N_LATE_LOADS, N_SPREAD, N_ANGLES, N_CONDS = 8, 5, 21, 17, 16, 10

K_ID = 0
K_NEGID = K_ID + P
K_GX = K_NEGID + P
K_GXX = K_GX + P
K_MASK = K_GXX + P
K_MASKT = K_MASK + P
K_IOTA = K_MASKT + P
K_MQ, K_MK = K_IOTA + 1, K_IOTA + 2
K_E8 = K_IOTA + 3
K_GE = K_E8 + 8
K_AE = K_GE + 6
K_BE = K_AE + 8
K_N = K_BE + 8

ACT_HIGH = [*range(1, 12), *range(14, 28)]
POOL_LOW = [*range(4, 11)]
DVE_HIGH = [t for t in range(E * FT) if t not in ACT_HIGH]
DVE_LOW = [t for t in range(E * FT) if t not in POOL_LOW]


def shape_constants():
    c = np.zeros((P, K_N), np.float32)
    g, gg = derivative_matrices(P)
    c[:, K_ID:K_ID + P] = np.eye(P)
    c[:, K_NEGID:K_NEGID + P] = -np.eye(P)
    c[:, K_GX:K_GX + P] = g.T
    c[:, K_GXX:K_GXX + P] = 0.5 * gg.T
    q, k = np.arange(P)[:, None], np.arange(P)[None, :]
    c[:, K_MASK:K_MASK + P] = np.where(k > q, MASKED, 0)
    c[:, K_MASKT:K_MASKT + P] = np.where(q > k, MASKED, 0)
    p = np.arange(P)
    c[:, K_IOTA] = p
    c[:, K_MQ] = (p // DH % 4) == 2
    c[:, K_MK] = (p // DH % 4) == 1
    c[:, K_E8:K_E8 + 8] = np.arange(8)
    c[:, K_GE:K_GE + 6] = (-3, 4, -1, 1, -4, 3)
    c[:, K_AE:K_AE + 8] = (1.5, -2, 0.5, 0, 0, -0.5, 2, -1.5)
    c[:, K_BE:K_BE + 8] = (1, -2.5, 2, -0.5, -0.5, 2, -2.5, 1)
    return c


class Signal:

    def __init__(self, sem, per):
        self.sem, self.per = sem, per

    def after(self, n, k=None):
        return n * self.per + (self.per if k is None else k)


def cond_seq_kernel(nc, a, out):
    with ExitStack() as ctx:
        def sb(name, shape, dt=F32):
            return ctx.enter_context(nc.sbuf_tensor(name, shape, dt))

        def sb_low(name, shape):
            with nc.sbuf_tensor(name, shape, F32) as full:
                pass
            return full, sb(name + "_low", shape, F32R)

        def bank(name):
            return ctx.enter_context(nc.psum_tensor(name, [P, 512], F32))

        def sem(name):
            return ctx.enter_context(nc.semaphore(name))

        def signal(name, per=1):
            return Signal(sem(name), per)

        def flat(t):
            return t[:].rearrange("p b d -> p (b d)")

        ps_hid = [bank("ps_hid0"), bank("ps_hid1")]
        ps_exp = bank("ps_exp")
        ps_pre = bank("ps_pre")
        ps_s = bank("ps_s")
        ps_x = [bank("ps_x0"), bank("ps_x1")]
        ps_c = bank("ps_c")

        cst = sb("cst", [P, K_N])
        ident = cst[:, K_ID:K_ID + P]
        negid = cst[:, K_NEGID:K_NEGID + P]
        id16 = sb("id16", [P, P], BF16)
        mask16 = sb("mask16", [P, P], BF16)
        maskT16 = sb("maskT16", [P, P], BF16)
        ones_r = sb("ones_r", [P, P], F32R)
        ones1 = sb("ones1", [1, 2])
        raw = sb("raw", [P, 8 * GT])

        def part(i, n=1):
            return raw[:, i * GT:(i + n) * GT]

        def part3(i):
            return part(i).rearrange("p (b d) -> p b d", b=GB)

        x2b, cx, xa2 = sb("x2b", [P, GB, D]), sb("cx", [P, GB, D]), sb("xa2", [P, GB, D])
        hn = sb("hn", [P, GT])
        w1h, w2h = sb("w1h", [P, E * FF], F32R), sb("w2h", [P, E, FT * D], F32R)
        (w1, w1l), (w2, w2l) = sb_low("w1", [P, E * FF]), sb_low("w2", [P, E, FT * D])
        rw = sb("rw", [P, E])
        cols = sb("cols", [P, R_N])
        wq_raw, wk_raw, hw2, hw1 = (raw[:, i * P:(i + 1) * P] for i in range(4))
        hw1 = hw1[0:64]
        sw1, sw2 = raw[:, 512:512 + 64], raw[0:64, 1024:1024 + 2 * D]
        rows_a, rows_b = raw[0:R_A, 1536:1536 + P], raw[0:R_N - R_A, 1664:1664 + P]
        subj = raw[0:32, 1792:1792 + 64]
        bq_row, bk_row = raw[0:1, 2048:2048 + D], raw[0:1, 2176:2176 + D]
        bqe, bke = raw[0:1, 2560:2560 + HJ * P], raw[0:1, 3072:3072 + HJ * P]
        wqh, wkh = sb("wqh", [P, HJ * P], F32R), sb("wkh", [P, HJ * P], F32R)
        (wqe, wql), (wke, wkl) = sb_low("wqe", [P, HJ * P]), sb_low("wke", [P, HJ * P])
        qk_b = sb("qk_b", [P, 2, HJ])
        qk_mb = sb("qk_mb", [P, 2, HJ])
        wvh, f1h = sb("wvh", [P, D], F32R), sb("f1h", [P, FF], F32R)
        (wv, wvl), (f1, f1l) = sb_low("wv", [P, D]), sb_low("f1", [P, FF])
        wo = sb("wo", [P, D])
        f2 = sb("f2", [P, FT, D])
        bv_b, bo_b, fb2_b = sb("bv_b", [P, D]), sb("bo_b", [P, D]), sb("fb2_b", [P, D])
        ln_eps, inorm_eps = sb("ln_eps", [P, GB]), sb("inorm_eps", [P, GB])
        carrier = sb("carrier", [P, 1])
        ag, bg = sb("ag", [P, 2, P]), sb("bg", [P, 3, P])
        g_p, g_m, g_b2 = sb("g_p", [P, P]), sb("g_m", [P, P]), sb("g_b2", [P, P])
        g_edge, edge_t = sb("g_edge", [P, 2, 4]), sb("edge_t", [P, 2, 4])
        ids_i, ids_f, onehot = sb("ids_i", [32, B], I32), sb("ids_f", [32, B]), sb("onehot", [32, B])
        se, hyp1, hyp2, sty1 = sb("se", [64, B]), sb("hyp1", [P, B]), sb("hyp2", [P, B]), sb("sty1", [64, B])
        style = sb("style", [P, 2, B])
        sp_a, sp_b, sp_c = sb("sp_a", [P, B]), sb("sp_b", [P, B]), sb("sp_c", [P, B])
        cond_in = sb("cond_in", [P, 4, B])
        ang, ang_k, ang_r = sb("ang", [P, 4, B]), sb("ang_k", [P, 4, B]), sb("ang_r", [P, 4, B])
        cond = sb("cond", [P, B, C_N])
        neg_half = sb("neg_half", [P, GB])

        xa = sb("xa", [P, GB, D])
        xn0, xn = sb("xn0", [P, GB, D]), sb("xn", [P, GB, D])
        h_aff, h32 = sb("h_aff", [P, GT]), sb("h32", [P, GT])
        hh = [sb("hh0", [P, GT], F32R), sb("hh1", [P, GT], F32R)]
        hl = [sb("hl0", [P, GT], F32R), sb("hl1", [P, GT], F32R)]
        st0, mv0, rs0 = sb("st0", [P, GB, 6]), sb("mv0", [P, GB, 2]), sb("rs0", [P, GB])
        sti, mvi, rsi = sb("sti", [P, GB, 6]), sb("mvi", [P, GB, 2]), sb("rsi", [P, GB])
        stn, mvn, rsn = sb("stn", [P, GB, 6]), sb("mvn", [P, GB, 2]), sb("rsn", [P, GB])
        in_s, in_ms, in_t = sb("in_s", [P, GB]), sb("in_ms", [P, GB]), sb("in_t", [P, GB])
        ve0, vei, ven = sb("ve0", [P, GB]), sb("vei", [P, GB]), sb("ven", [P, GB])
        sty_g = sb("sty_g", [P, 2, GB])
        lg, top, top_i = sb("lg", [P, GB, E]), sb("top", [P, GB, 8]), sb("top_i", [P, GB, 8], U32)
        top_f = sb("top_f", [P, 2, GB])
        gap, gexp, gsum, gates = sb("gap", [P, GB]), sb("gexp", [P, GB]), sb("gsum", [P, GB]), sb("gates", [P, 2, GB])
        pick = sb("pick", [P, 2, GB, E])
        comb = sb("comb", [P, GB, E])
        comb_t = sb("comb_t", [E, GT])
        gate_rows = nc.dram_tensor("gate_rows", (2, E, GT), F32).ap()
        comb_b = [sb("comb_b0", [P, GT]), sb("comb_b1", [P, GT])]

        hid_h, (hid, hid_l) = sb("hid_h", [P, FT, GT], F32R), sb_low("hid", [P, FT, GT])
        gated = [sb("gated0", [P, GT]), sb("gated1", [P, GT])]
        y_t = [sb("y_t0", [P, GT]), sb("y_t1", [P, GT])]

        xb = sb("xb", [P, GB, D])
        f = sb("f", [P, GB, D])
        rb, u_, ua, wm, w_, wp, v_, bf = (part3(i) for i in range(8))
        eu, ew = sb("eu", [P, GB, 2, 3]), sb("ew", [P, GB, 2, 4])
        df, fn, x1in = rb, wp, sb("x1in", [P, GB, D])
        cond_g = sb("cond_g", [P, GB, C_N])
        hnh, hnl = sb("hnh", [P, GT], F32R), sb("hnl", [P, GT], F32R)
        lo_part = [part(1).bitcast(F32R), part(2).bitcast(F32R)]
        qs, ks = sb("qs", [P, HJ, GB, T], F32R), sb("ks", [P, HJ, GB, T], F32R)
        vs = sb("vs", [P, GB, NH, VW])
        mx = [sb("mx0", [P, HJ]), sb("mx1", [P, HJ])]
        dg = [sb("dg0", [P, HJ, T], F32R), sb("dg1", [P, HJ, T], F32R)]
        pt = [part3(4), part3(5)]
        rden = sb("rden", [P, RG, HJ])
        pvt = hn
        cxt, xbo, res = hn, sb("xbo", [P, GB, D]), x2b
        gl = part(0, FT).rearrange("p (j t) -> p j t", j=FT)
        t1, t2, fin = cx, xbo, sb("fin", [P, GB, D])

        w1_in = [sem("w1_0_in"), sem("w1_rest_in")]
        w2_in = [sem("w2_0_in"), sem("w2_rest_in")]
        cst_in, late_in, rows_in = sem("cst_in"), sem("late_in"), sem("rows_in")
        ids_in, net_in, f2_in = sem("ids_in"), sem("net_in"), sem("f2_in")
        halves, ones_v = sem("halves"), sem("ones_v")
        cols_ps, cols_done = sem("cols_ps"), sem("cols_done")
        hot_step, se_ps, se_done = sem("hot_step"), sem("se_ps"), sem("se_done")
        hyp1_ps, hyp1_done, hyp2_ps, hyp2_done = sem("hyp1_ps"), sem("hyp1_done"), sem("hyp2_ps"), sem("hyp2_done")
        sty1_ps, sty1_done, style_ps, style_done = sem("sty1_ps"), sem("sty1_done"), sem("style_ps"), sem("style_done")
        soft_v, soft_a = sem("soft_v"), sem("soft_a")
        spread, bias_ps, bias_done = sem("spread"), sem("bias_ps"), sem("bias_done")
        split_w = [sem("split_qk"), sem("split_vf")]
        w1_split, w2_split = [sem("w1_split_v"), sem("w1_split_g")], sem("w2_split")
        grids, angles, sines, conds, masks = sem("grids"), sem("angles"), sem("sines"), sem("conds"), sem("masks")
        w1_high, w2_high = sem("w1_high"), sem("w2_high")
        xa_in = signal("xa_in", 16)
        ln0_stats, ln0_mv = signal("ln0_stats", GB), signal("ln0_mv", GB)
        ln0_ve, ln0_rs, ln0_xn = signal("ln0_ve"), signal("ln0_rs"), signal("ln0_xn")
        xn0_t = signal("xn0_t")
        haff = signal("haff")
        in_stats, in_mv, in_ve, in_rs = signal("in_stats", GB), signal("in_mv", GB), signal("in_ve"), signal("in_rs")
        in_styled, in_step, in_coef = signal("in_styled"), signal("in_step", 2), signal("in_coef")
        h32_done, hh_done, h_split = signal("h32_done"), signal("hh_done"), signal("h_split")
        logits = signal("logits")
        lg_copied, topped, topi_done = signal("lg_copied"), signal("topped", GB), signal("topi_done")
        gap_done, gap_exp, gate_step = signal("gap_done"), signal("gap_exp"), signal("gate_step", 7)
        comb_done, comb_tp, comb_ct, comb_rowed = signal("comb_done"), signal("comb_tp"), signal("comb_ct"), signal("comb_rowed", 16)
        comb_bc = [signal("comb_bc0", 16 * E // 2), signal("comb_bc1", 16 * E // 2)]
        hid_ps = signal("hid_ps", E * FT)
        hid_done = signal("hid_done", E * FT)
        hid_high = signal("hid_high", len(DVE_HIGH))
        hid_low, hid_low_g = signal("hid_low", len(DVE_LOW)), signal("hid_low_g", len(POOL_LOW))
        exp_ps = signal("exp_ps", E * FT)
        gated_done, y_added = signal("gated_done", E), signal("y_added", E - 1)
        xb_in = signal("xb_in", 16)
        y_back, f_done = signal("y_back"), signal("f_done")
        cond_ready = signal("cond_ready")
        pde_pool = signal("pde_pool", 2)
        pde_v = signal("pde_v", 11)
        u_done, pde_ps = signal("u_done"), signal("pde_ps")
        df_done, fn_done, x1in_done = signal("df_done"), signal("fn_done", GB), signal("x1in_done")
        ln_stats = [signal("ln1_stats", GB), signal("ln2_stats", GB)]
        ln_mv = [signal("ln1_mv", GB), signal("ln2_mv", GB)]
        ln_ve = [signal("ln1_ve"), signal("ln2_ve")]
        ln_rs = [signal("ln1_rs"), signal("ln2_rs")]
        ln_xn = [signal("ln1_xn"), signal("ln2_xn")]
        xn_t = [signal("xn1_t"), signal("xn2_t")]
        hn_done = [signal("hn1_done"), signal("hn2_done")]
        hnh_done = [signal("hnh1_done"), signal("hnh2_done")]
        hn_split = [signal("hn1_split"), signal("hn2_split")]
        qk_ps, qk_lo, qk_done = signal("qk_ps", 2 * HJ), signal("qk_lo", 2 * HJ), signal("qk_done", 2 * HJ)
        v_ps, v_done = signal("v_ps"), signal("v_done")
        s_ps, mx_done, dg_done = signal("s_ps", NU), signal("mx_done", NU), signal("dg_done", NU)
        x_ps, exp_done, pv_done = signal("x_ps", NU), signal("exp_done", NU), signal("pv_done", NU)
        rden_done, cx_done = signal("rden_done", GB), signal("cx_done", GB)
        pv_out, pv_turned = signal("pv_out", GB), signal("pv_turned", GB)
        cx_t, cxt_done = signal("cx_t"), signal("cxt_done")
        wo_ps, xbo_done, xa2_done = signal("wo_ps"), signal("xbo_done"), signal("xa2_done")
        f1_ps, gelu_done, f2_ps = signal("f1_ps", FT), signal("gelu_done", FT), signal("f2_ps")
        x2b_step, sofar_done, res_done = signal("x2b_step", 3), signal("sofar_done"), signal("res_done", GB)
        rot_step, rotated, stored = signal("rot_step", 3), signal("rotated"), signal("stored", 16)

        def await_(eng, sig, n, k=None):
            if isinstance(n, int) and n < 0:
                return
            eng.wait_ge(sig.sem, sig.after(n, k))

        def apart(eng):
            eng.memset(carrier[:], 0.0)

        def bc(ap, n):
            return ap.unsqueeze(1).broadcast_to([ap.shape[0], n, ap.shape[1]])

        def inner(ap, n):
            return ap.unsqueeze(2).broadcast_to([ap.shape[0], ap.shape[1], n])

        def col(r):
            return cols[:, r:r + 1]

        def free_hidden(eng, n, t):
            if t >= FT:
                await_(eng, exp_ps, n, t - FT + 1)
            else:
                await_(eng, exp_ps, n - 1, E * FT + t - FT + 1)

        def iterations(eng, emit):
            emit(0, 0, back=False, experts=True, pre=True)
            with eng.Fori(0, (NG - 2) // 2) as i:
                for u in range(2):
                    emit(i * 2 + 1 + u, (1 + u) % 2, back=True, experts=True, pre=True)
            emit(NG - 1, (NG - 1) % 2, back=True, experts=True, pre=False)
            emit(NG, NG % 2, back=True, experts=False, pre=False)

        A_Y, A_PDE, A_STATS1, A_NORM1, A_QK = 0, 5, 7, 9, 11
        A_V = A_QK + HJ
        A_CONTEXT, A_WO, A_STATS2, A_NORM2, A_FFN = 22, 23, 24, 26, 28
        A_STATS, A_NORM, A_AFFINE = 8, 11, 13
        A_SPREAD, A_ANGLES = 9, 14
        A_STEPS, NK = 15, NU + 5
        STEPS_AT = ((0, 1), (1, 2), (2, 3), (3, 9), (9, 14), (14, NK - 1), (NK - 1, NK))
        K_INORM, K_ROUTER, K_GATES, K_GATES_T = 0, 10, 12, 18

        PIECES = ((1,), (2, 3), (), ())

        def steps(at):
            return range(*STEPS_AT[at - A_STEPS]) if 0 <= at - A_STEPS < len(STEPS_AT) else range(0)

        def turned(k):
            b, r_ = divmod(k - (RG - 1 + 5), RG)
            return b if r_ == 0 and 0 <= b < GB else None

        def split(v, raw_, hi, lo, sem_, k):
            v.tensor_copy(hi, raw_).then_inc(sem_, 1)
            v.wait_ge(sem_, k + 1)
            v.tensor_tensor(lo, raw_, hi, ALU.subtract).then_inc(sem_, 1)

        def w1_of(e):
            return slice(e * FF, (e + 1) * FF)

        def split_w1_first(v, e):
            v.wait_ge(w1_in[e > 0], 16)
            split(v, w1[:, w1_of(e)], w1h[:, w1_of(e)], w1l[:, w1_of(e)], w1_split[0], 2 * e)

        def round_w1(act, e):
            act.wait_ge(w1_in[1], 16)
            act.activation(w1h[:, w1_of(e)], w1[:, w1_of(e)], ACT.Identity).then_inc(w1_high, 1)

        def split_w1(pool, e):
            pool.wait_ge(w1_high, e - 1)
            pool.tensor_tensor(w1l[:, w1_of(e)], w1[:, w1_of(e)], w1h[:, w1_of(e)], ALU.subtract).then_inc(w1_split[1], 1)

        def round_w2(act, e):
            act.wait_ge(w2_in[e > 0], 16)
            act.activation(w2h[:, e], w2[:, e], ACT.Identity).then_inc(w2_high, 1)

        def split_w2(pool, e):
            pool.wait_ge(w2_high, e + 1)
            pool.tensor_tensor(w2l[:, e], w2[:, e], w2h[:, e], ALU.subtract).then_inc(w2_split, 1)

        def split_rest(v, i):
            raw_, hi, lo = ((wqe, wqh, wql), (wke, wkh, wkl), (wv, wvh, wvl), (f1, f1h, f1l))[i]
            split(v, raw_[:], hi[:], lo[:], split_w[i // 2], 2 * (i % 2))

        def broadcast_gates(eng, n, p, e):
            if e == 0:
                await_(eng, comb_rowed, n)
            if e >= 2:
                await_(eng, gated_done, n, e - 1)
            else:
                await_(eng, gated_done, n - 1, E - 1 + e)
            eng.dma_start(comb_b[e % 2][:], gate_rows[p, e].partition_broadcast(P)).then_inc(comb_bc[e % 2].sem, 16)

        block = ctx.enter_context(nc.Block())

        @block.sync
        def _(sp):
            def load(dst, src, sem_):
                sp.dma_start(dst, src).then_inc(sem_, 16)

            def load_xa(n):
                first = first_batch(n)
                if not (isinstance(n, int) and n == 0):
                    await_(sp, ln0_xn, n - 1)
                load(xa[:], x_grp(first), xa_in.sem)

            def load_xb(n):
                first = first_batch(n)
                if not (isinstance(n, int) and n == 0):
                    await_(sp, f_done, n - 1)
                load(xb[:], x_grp(first), xb_in.sem)

            def first_batch(n):
                return n * GB if isinstance(n, int) else sp.snap(n * GB)

            def x_grp(first):
                return a["x"][bass.ds(first, GB), :, :].rearrange("b t d -> t b d")

            load_xa(0)
            load(ids_i[:], a["itok_B_6_14"].partition_broadcast(32), ids_in)
            load(subj, a["L0_cond_subj_emb"], ids_in)
            load(rows_a[R_B1:R_B1 + E * FT, :], a["L0_cond_exp_b1"].rearrange("e (t p) -> (e t) p", p=P), rows_in)
            for r, name in ((R_LNG, "L0_cond_ln_g"), (R_LNB, "L0_cond_ln_b")):
                load(rows_a[r:r + 1, :], a[name].unsqueeze(0), rows_in)
            for half in range(2):
                load(rows_a[R_SB1:R_SB1 + 1, 64 * half:64 * half + 64], a["L0_cond_sty_b1"].unsqueeze(0), rows_in)
            load_xa(1)
            r0 = R_A
            load(rows_b[R_B2 - r0:R_B2 - r0 + E, :], a["L0_cond_exp_b2"], late_in)
            for r, name in ((R_G1, "L2_cond_gamma1"), (R_BE1, "L2_cond_beta1"),
                            (R_G2, "L2_cond_gamma2"), (R_BE2, "L2_cond_beta2")):
                load(rows_b[r - r0:r - r0 + 1, :], a[name].unsqueeze(0), late_in)
            load(rows_b[R_FB1 - r0:R_FB1 - r0 + FT, :], a["L2_cond_b1"].rearrange("(r p) -> r p", p=P), late_in)
            for dst, name in ((wq_raw, "L2_cond_Wq"), (wk_raw, "L2_cond_Wk"), (wv[:], "L2_cond_Wv"),
                              (wo[:], "L2_cond_Wo"), (f1[:], "L2_cond_W1")):
                load(dst, a[name], late_in)
            load(bq_row, a["L2_cond_bq"].unsqueeze(0), late_in)
            load(bk_row, a["L2_cond_bk"].unsqueeze(0), late_in)
            for i, name in enumerate(("condB_dt", "condB_gatescore", "condB_theta", "condB_phi")):
                load(cond_in[:, i, :], a[name].partition_broadcast(P), late_in)
            load(ag[:], a["L1_cond_A_grid"].rearrange("c x y -> x c y"), late_in)
            load(bg[:], a["L1_cond_B_grid"].rearrange("c x y -> x c y"), late_in)
            load(fb2_b[:], a["L2_cond_b2"].partition_broadcast(P), stored.sem)
            for dst, name in ((bv_b, "L2_cond_bv"), (bo_b, "L2_cond_bo")):
                load(dst[:], a[name].partition_broadcast(P), late_in)
            load(f2[:], a["L2_cond_W2"].rearrange("(t p) d -> p t d", p=P), f2_in)
            load_xb(0)

            def rows_of_gates(n, p):
                await_(sp, comb_ct, n)
                load(gate_rows[p], comb_t[:], comb_rowed.sem)

            def store(n):
                first = first_batch(n)
                await_(sp, rotated, n)
                sp.dma_start(out[bass.ds(first, GB), :, :].rearrange("b t d -> t b d"),
                             fin[:]).then_inc(stored.sem, 16)

            rows_of_gates(0, 0)

            def emit(g, p, back, experts, pre):
                if pre and not (isinstance(g, int) and g == 0):
                    load_xa(g + 1)
                for e in range(1, E):
                    if experts and e == 2:
                        await_(sp, comb_rowed, g)
                    if experts and e >= 2:
                        broadcast_gates(sp, g, p, e)
                    if e == 3 and back and experts:
                        load_xb(g)
                    if e == 4 and pre:
                        rows_of_gates(g + 1, 1 - p)
                if back:
                    store(g - 1)

            iterations(sp, emit)
            await_(sp, stored, NG)

        @block.scalar
        def _(act):
            act.dma_start(cst[:], a["cst"]).then_inc(cst_in, 16)
            for r, n_, name in ((R_HB1, 1, "L0_cond_hyp_b1"), (R_HB2, 1, "L0_cond_hyp_b2"), (R_SB2, 2, "L0_cond_sty_b2")):
                act.dma_start(rows_a[r:r + n_, :], a[name].rearrange("(r p) -> r p", p=P)).then_inc(rows_in, 16)
            act.dma_start(w1[:, 0:FF], a["L0_cond_exp_w1"][0]).then_inc(w1_in[0], 16)
            for dst, name in ((hw1, "hyp_w1"), (hw2, "hyp_w2"), (sw1, "sty_w1"), (sw2, "sty_w2"), (rw[:], "router_w")):
                act.dma_start(dst, a["L0_cond_" + name]).then_inc(net_in, 16)

            def load_w2(e0, e1):
                act.dma_start(w2[:, e0:e1].rearrange("p e (t d) -> p e t d", d=D),
                              a["L0_cond_exp_w2"][e0:e1].rearrange("e (t p) d -> p e t d", p=P)).then_inc(w2_in[e0 > 0], 16)

            def large_loads():
                act.wait_ge(net_in, 16 * N_NET_LOADS)
                load_w2(0, 1)
                act.dma_start(w1[:, FF:].rearrange("p (e f) -> p e f", f=FF),
                              a["L0_cond_exp_w1"][1:E].rearrange("e d f -> d e f")).then_inc(w1_in[1], 16)
                load_w2(1, E)

            def style_network():
                act.wait_ge(hyp1_ps, 1)
                act.activation(hyp1[:], ps_x[1][:, 0:B], ACT.Relu, bias=col(R_HB1)).then_inc(hyp1_done, 1)
                large_loads()
                act.wait_ge(hyp2_ps, 1)
                act.activation(hyp2[:], ps_c[:, 0:B], ACT.Identity, bias=col(R_HB2)).then_inc(hyp2_done, 1)
                act.wait_ge(sty1_ps, 1)
                act.activation(sty1[:], ps_hid[0][0:64, 0:B], ACT.Relu,
                               bias=cols[0:64, R_SB1:R_SB1 + 1]).then_inc(sty1_done, 1)
                act.wait_ge(style_ps, 2)
                act.activation(sp_a[:], ps_hid[1][:, 0:B], ACT.Identity, bias=col(R_SB2)).then_inc(style_done, 1)
                act.activation(style[:, 1, :], ps_exp[:, 0:B], ACT.Identity, bias=col(R_SB2 + 1)).then_inc(style_done, 1)
                act.wait_ge(soft_v, 1)
                act.activation(sp_c[:], sp_b[:], ACT.Exp).then_inc(soft_a, 1)
                act.wait_ge(soft_a, 1)
                act.activation(sp_b[:], sp_c[:], ACT.Ln, bias=1.0).then_inc(soft_a, 1)

            def prepare(at):
                if at == 4:
                    act.wait_ge(cols_ps, 2)
                    act.activation(cols[:, R_A:R_N], ps_s[:, 0:R_N - R_A], ACT.Identity).then_inc(cols_done, 1)
                if at % FT == FT - 1 and at // FT + 2 < E:
                    round_w2(act, at // FT + 2)
                    if at // FT + 3 < E:
                        round_w1(act, at // FT + 3)
                if at == 0:
                    gap_exponential(0)
                if at == 1:
                    round_w2(act, 1)
                    round_w1(act, 2)
                if at == 2:
                    gates_out(0)
                if at == 4:
                    broadcast_gates(act, 0, 0, 0)
                if at == 5:
                    act.activation(id16[:], ident, ACT.Identity).then_inc(masks, 1)
                    act.activation(mask16[:], cst[:, K_MASK:K_MASK + P], ACT.Identity).then_inc(masks, 1)
                    act.activation(maskT16[:], cst[:, K_MASKT:K_MASKT + P], ACT.Identity).then_inc(masks, 1)
                    act.activation(ones_r[:], ident, ACT.Identity, scale=0.0, bias=1.0).then_inc(masks, 1)
                if at == A_ANGLES:
                    act.wait_ge(angles, N_ANGLES)
                    act.activation(ang[:], ang_r[:], ACT.Sin).then_inc(sines, 1)

            def affine(n):
                await_(act, xn0_t, n)
                await_(act, in_coef, n - 1)
                await_(act, h32_done, n - 1)
                act.activation(h_aff[:], ps_pre[:], ACT.Identity, bias=col(R_LNB), scale=col(R_LNG)).then_inc(haff.sem, 1)

            def gap_exponential(n):
                await_(act, gap_done, n)
                act.activation(gexp[:], gap[:], ACT.Exp).then_inc(gap_exp.sem, 1)

            def gates_out(n):
                await_(act, comb_tp, n)
                await_(act, comb_rowed, n - 1)
                act.activation(comb_t[:], ps_pre[0:E, :], ACT.Identity).then_inc(comb_ct.sem, 1)

            def relu(n, e, j):
                await_(act, hid_ps, n, e * FT + j + 1)
                free_hidden(act, n, e * FT + j)
                if e * FT + j in ACT_HIGH:
                    act.activation(hid_h[:, j, :], ps_hid[j % 2][:], ACT.Relu, bias=col(R_B1 + e * FT + j))
                act.activation(hid[:, j, :], ps_hid[j % 2][:], ACT.Relu,
                               bias=col(R_B1 + e * FT + j)).then_inc(hid_done.sem, 1)

            def layernorm_affine(n, which):
                await_(act, xn_t[which], n)
                act.activation(hn[:], ps_c[:], ACT.Identity, bias=col(R_BE1 + 2 * which),
                               scale=col(R_G1 + 2 * which)).then_inc(hn_done[which].sem, 1)

            def qk_low(n, j, which):
                await_(act, qk_ps, n, 2 * j + which + 1)
                if j >= 1:
                    await_(act, qk_done, n, 2 * j - 1 + which)
                act.activation(lo_part[which][:], ps_x[which][:], ACT.Identity, bias=qk_mb[:, which, j:j + 1],
                               scale=cst[:, K_MQ + which:K_MQ + which + 1]).then_inc(qk_lo.sem, 1)

            def exponential(n, u):
                await_(act, x_ps, n, u + 1)
                if u >= 2:
                    await_(act, pv_done, n, u - 1)
                act.activation(flat(pt[u % 2]), ps_x[u % 2][:], ACT.Exp).then_inc(exp_done.sem, 1)

            def values_out(n, b):
                await_(act, pv_done, n, RG * (b + 1))
                if b >= 1:
                    await_(act, pv_turned, n, b)
                act.activation(pvt[:], ps_c[:], ACT.Identity).then_inc(pv_out.sem, 1)

            def context_out(n):
                await_(act, cx_t, n)
                act.activation(cxt[:], ps_c[:], ACT.Identity).then_inc(cxt_done.sem, 1)

            def gelu(n, j):
                await_(act, f1_ps, n, j + 1)
                act.activation(gl[:, j, :], ps_x[j % 2][:], ACT.Gelu, bias=col(R_FB1 + j)).then_inc(gelu_done.sem, 1)

            def emit(g, p, back, experts, pre):
                n, m = g - 1, g + 1
                for s in range(E):
                    for j in range(FT):
                        at = s * FT + j
                        if experts and at == 5:
                            broadcast_gates(act, g, p, 1)
                        if experts:
                            relu(g, s, j)
                        if isinstance(g, int) and g == 0:
                            prepare(at)
                        if back and at == A_NORM1:
                            layernorm_affine(n, 0)
                        if back and A_QK <= at < A_QK + HJ:
                            qk_low(n, at - A_QK, 0)
                            qk_low(n, at - A_QK, 1)
                        if pre and at == A_AFFINE:
                            affine(m)
                        for k in steps(at):
                            if back and turned(k + 1) is not None:
                                values_out(n, turned(k + 1))
                            if back and 2 <= k < NU + 2:
                                exponential(n, k - 2)
                            if pre and k == K_GATES:
                                gap_exponential(m)
                            if pre and k == K_GATES_T:
                                gates_out(m)
                        if back and at == A_CONTEXT:
                            context_out(n)
                        if back and at == A_NORM2:
                            layernorm_affine(n, 1)
                        if back and A_FFN <= at < A_FFN + FT:
                            gelu(n, at - A_FFN)
                if pre:
                    broadcast_gates(act, m, 1 - p, 0)

            act.wait_ge(cols_ps, 1)
            act.activation(cols[:, 0:R_A], ps_s[:, 0:R_A], ACT.Identity).then_inc(cols_done, 1)
            act.wait_ge(cols_done, 1)
            affine(0)
            style_network()
            round_w2(act, 0)
            iterations(act, emit)

        @block.gpsimd
        def _(pool):
            G = nc.gpsimd
            G.memset(neg_half[:], -0.5).then_inc(halves, 1)
            G.memset(ln_eps[:], LN_EPS).then_inc(halves, 1)
            G.memset(inorm_eps[:], INORM_EPS).then_inc(halves, 1)
            pool.wait_ge(halves, 3)

            def rsqrt(n, ve, rs, mv, eps, s_mv, s_ve, s_rs, reader):
                await_(pool, s_mv, n)
                G.tensor_tensor(ve[:], mv[:, :, 1], eps[:], ALU.add).then_inc(s_ve.sem, 1)
                await_(pool, s_ve, n)
                if reader is not None:
                    await_(pool, reader, n - 1)
                G.tensor_tensor(rs[:], ve[:], neg_half[:], ALU.pow).then_inc(s_rs.sem, 1)

            def pre_root(n):
                rsqrt(n, ve0, rs0, mv0, ln_eps, ln0_mv, ln0_ve, ln0_rs, ln0_xn)

            def inorm_coefficients(n):
                rsqrt(n, vei, rsi, mvi, inorm_eps, in_mv, in_ve, in_rs, None)
                if isinstance(n, int) and n == 0:
                    pool.wait_ge(soft_v, 3)
                G.tensor_copy(sty_g[:], style[:, :, bass.ds(n * GB, GB)]).then_inc(in_styled.sem, 1)
                await_(pool, in_rs, n)
                await_(pool, in_styled, n)
                await_(pool, h32_done, n - 1)
                G.tensor_tensor(in_s[:], rsi[:], sty_g[:, 0, :], ALU.mult).then_inc(in_step.sem, 1)
                await_(pool, in_step, n, 1)
                G.tensor_tensor(in_ms[:], mvi[:, :, 0], in_s[:], ALU.mult).then_inc(in_step.sem, 1)
                await_(pool, in_step, n, 2)
                G.tensor_tensor(in_t[:], sty_g[:, 1, :], in_ms[:], ALU.subtract).then_inc(in_coef.sem, 1)

            def make_grids():
                k = 0

                def grid(ins):
                    nonlocal k
                    k += 1
                    ins.then_inc(grids, 1)
                    pool.wait_ge(grids, k)

                grid(G.tensor_scalar(g_b2[:], bg[:, 2, :], 0.5, None, ALU.mult))
                grid(G.tensor_tensor(g_p[:], bg[:, 1, :], ag[:, 1, :], ALU.subtract))
                grid(G.tensor_scalar(g_p[:], g_p[:], 0.5, None, ALU.mult))
                grid(G.tensor_tensor(g_m[:], bg[:, 1, :], ag[:, 1, :], ALU.add))
                grid(G.tensor_scalar(g_m[:], g_m[:], 0.5, None, ALU.mult))
                for side, lo in enumerate((0, D - 4)):
                    ka = cst[:, K_AE + 4 * side:K_AE + 4 * side + 4]
                    kb = cst[:, K_BE + 4 * side:K_BE + 4 * side + 4]
                    grid(G.tensor_tensor(edge_t[:, side, :], ag[:, 1, lo:lo + 4], ka, ALU.mult))
                    grid(G.tensor_tensor(g_edge[:, side, :], bg[:, 1, lo:lo + 4], kb, ALU.mult))
                    grid(G.tensor_tensor(g_edge[:, side, :], g_edge[:, side, :], edge_t[:, side, :], ALU.add))

            def add_expert(n, p, e):
                await_(pool, gated_done, n, e + 1)
                if e >= 2:
                    await_(pool, y_added, n, e - 1)
                G.tensor_tensor(y_t[p][:], y_t[p][:], gated[e % 2][:], ALU.add).then_inc(y_added.sem, 1)

            def hidden_low(n, t):
                await_(pool, hid_done, n, t + 1)
                j = t % FT
                G.tensor_tensor(hid_l[:, j, :], hid[:, j, :], hid_h[:, j, :], ALU.subtract).then_inc(hid_low_g.sem, 1)

            def pde_products(n):
                await_(pool, f_done, n)
                for dst, grid_ in ((v_, bg[:, 0, :]), (bf, bg[:, 1, :])):
                    G.tensor_tensor(dst[:], f[:], bc(grid_, GB), ALU.mult).then_inc(pde_pool.sem, 1)

            def conditions(n):
                G.tensor_copy(cond_g[:], cond[:, bass.ds(n * GB, GB), :]).then_inc(cond_ready.sem, 1)

            def norm_root(n, which):
                rsqrt(n, ven, rsn, mvn, ln_eps, ln_mv[which], ln_ve[which], ln_rs[which], None)

            def minus_maximum(n, u):
                await_(pool, mx_done, n, u + 1)
                if u >= 2:
                    await_(pool, x_ps, n, u - 1)
                G.tensor_tensor(dg[u % 2][:], bc(negid, HJ), inner(mx[u % 2][:], T), ALU.mult).then_inc(dg_done.sem, 1)

            def input_and_bias(n):
                await_(pool, x1in_done, n)
                G.tensor_tensor(xbo[:], x1in[:], bc(bo_b[:], GB), ALU.add).then_inc(xbo_done.sem, 1)

            def blend_so_far(n):
                await_(pool, xa2_done, n)
                G.tensor_tensor(x2b[:], xa2[:], bc(fb2_b[:], GB), ALU.add).then_inc(x2b_step.sem, 1)
                await_(pool, x2b_step, n, 1)
                G.tensor_tensor(x2b[:], x2b[:], x1in[:], ALU.subtract).then_inc(x2b_step.sem, 1)
                await_(pool, x2b_step, n, 2)
                G.tensor_tensor(x2b[:], x2b[:], inner(cond_g[:, :, C_GATE], D), ALU.mult).then_inc(x2b_step.sem, 1)
                await_(pool, x2b_step, n, 3)
                G.tensor_tensor(x2b[:], x2b[:], x1in[:], ALU.add).then_inc(sofar_done.sem, 1)

            def rotate(n):
                await_(pool, res_done, n)
                r = res[:].rearrange("p b (k c) -> p b k c", c=4)
                w = t2[:].rearrange("p b (k c) -> p b k c", c=4)

                def coef(c, m):
                    v = cond_g[:, :, c:c + 4 if m == 1 else c + 3:m]
                    return v.unsqueeze(2).broadcast_to([P, GB, D // 4, 4 // m])

                G.tensor_tensor(t1[:].rearrange("p b (k c) -> p b k c", c=4), r, coef(C_COS, 1), ALU.mult).then_inc(rot_step.sem, 1)
                G.tensor_tensor(w[:, :, :, 0::2], r[:, :, :, 1::2], coef(C_SIN, 2), ALU.mult).then_inc(rot_step.sem, 1)
                G.tensor_tensor(w[:, :, :, 1::2], r[:, :, :, 0::2], coef(C_SIN + 1, 2), ALU.mult).then_inc(rot_step.sem, 1)
                await_(pool, rot_step, n)
                await_(pool, stored, n)
                G.tensor_tensor(fin[:], t1[:], t2[:], ALU.add).then_inc(rotated.sem, 1)
                await_(pool, rotated, n)

            def emit(g, p, back, experts, pre):
                n, m = g - 1, g + 1
                if back and experts:
                    conditions(n)
                for s in range(E):
                    for j in range(FT):
                        at = s * FT + j
                        if experts and at - 1 in POOL_LOW:
                            hidden_low(g, at - 1)
                        if experts and j == 3 and s >= 2:
                            add_expert(g, p, s - 1)
                        if isinstance(g, int) and g == 0 and j == 0:
                            if s + 1 < E:
                                split_w2(pool, s + 1)
                            if s + 2 < E:
                                split_w1(pool, s + 2)
                            if s == E - 2:
                                pool.wait_ge(late_in, 16 * N_LATE_LOADS)
                                make_grids()
                            if s == E - 1:
                                split_rest(pool, 2)
                                split_rest(pool, 3)
                        if back and at == A_Y:
                            pde_products(n)
                            if not experts:
                                rotate(n - 1)
                                conditions(n)
                        if back and at == A_STATS1 + 1:
                            norm_root(n, 0)
                        if back and at == A_QK:
                            input_and_bias(n)
                        if pre and at == A_STATS + 2:
                            pre_root(m)
                        for k in steps(at):
                            if pre and k == K_INORM:
                                inorm_coefficients(m)
                            if back and k < NU:
                                minus_maximum(n, k)
                        if back and at == A_STATS2:
                            norm_root(n, 1)
                        if back and at == A_NORM2:
                            blend_so_far(n)
                if experts:
                    add_expert(g, p, E - 1)
                if back and (pre or not experts):
                    rotate(n)
                if isinstance(g, int) and g == 0:
                    pool.wait_ge(conds, N_CONDS)

            pre_root(0)
            inorm_coefficients(0)
            split_w2(pool, 0)
            G.memset(vs[:], 1.0).then_inc(ones_v, 1)
            pool.wait_ge(ones_v, 1)
            pool.wait_ge(cst_in, 16)
            iterations(pool, emit)

        @block.vector
        def _(dve):
            V = nc.vector
            def one_hot():
                dve.wait_ge(cst_in, 16)
                dve.wait_ge(ids_in, 32)
                V.tensor_copy(ids_f[:], ids_i[:]).then_inc(hot_step, 1)
                dve.wait_ge(hot_step, 1)
                V.tensor_scalar(onehot[:], ids_f[:], cst[0:32, K_IOTA:K_IOTA + 1], None, ALU.is_equal).then_inc(hot_step, 1)
                dve.wait_ge(se_ps, 1)
                V.tensor_copy(se[:], ps_x[0][0:64, 0:B]).then_inc(se_done, 1)

            def softplus():
                dve.wait_ge(style_done, 2)
                V.scalar_tensor_tensor(sp_b[:], sp_a[:], -1.0, sp_a[:], ALU.mult, ALU.min).then_inc(soft_v, 1)
                dve.wait_ge(soft_a, 2)
                V.scalar_tensor_tensor(sp_c[:], sp_a[:], 0.0, sp_b[:], ALU.max, ALU.add).then_inc(soft_v, 1)
                dve.wait_ge(soft_v, 2)
                V.tensor_scalar(style[:, 0, :], sp_c[:], 1e-8, None, ALU.add).then_inc(soft_v, 1)

            def spread_qk():
                dve.wait_ge(late_in, 16 * N_LATE_LOADS)
                k = 0
                for dst, src, scale in ((wqe[:], wq_raw, DH ** -0.5), (wke[:], wk_raw, 1.0),
                                        (bqe, bq_row, DH ** -0.5), (bke, bk_row, 1.0)):
                    V.memset(dst, 0.0).then_inc(spread, 1)
                    k += 1
                    dve.wait_ge(spread, k)
                    for r in range(3):
                        V.tensor_scalar(dst.rearrange("p (h r d) -> p r h d", r=4, d=DH)[:, r],
                                        src.rearrange("p (h d) -> p h d", d=DH), scale, None, ALU.mult).then_inc(spread, 1)
                        k += 1
                V.memset(ones1[:], 1.0).then_inc(spread, 1)
                assert k + 1 == N_SPREAD
                dve.wait_ge(spread, N_SPREAD)

            def bias_columns():
                dve.wait_ge(bias_ps, 1)
                V.tensor_copy(qk_b[:].rearrange("p w j -> p (w j)"), ps_s[:, 0:2 * HJ]).then_inc(bias_done, 1)
                dve.wait_ge(bias_done, 1)
                V.tensor_tensor(qk_mb[:], qk_b[:], inner(cst[:, K_MQ:K_MQ + 2], HJ), ALU.mult).then_inc(bias_done, 1)

            def rotation_angles():
                k = 0

                def step(ins):
                    nonlocal k
                    k += 1
                    ins.then_inc(angles, 1)
                    dve.wait_ge(angles, k)

                for quarter in range(2):
                    c = slice(2 * quarter, 2 * quarter + 2)
                    step(V.tensor_scalar(ang_k[:, c], cond_in[:, 2:4, :], 1 / (2 * np.pi), 0.25 * quarter, ALU.mult, ALU.add))
                    step(V.tensor_scalar(ang_r[:, c], ang_k[:, c], ROUND, None, ALU.add))
                    step(V.tensor_scalar(ang_k[:, c], ang_r[:, c], ROUND, None, ALU.subtract))
                    step(V.scalar_tensor_tensor(ang_r[:, c], ang_k[:, c], -TWO_PI_HI, cond_in[:, 2:4, :], ALU.mult, ALU.add))
                    step(V.scalar_tensor_tensor(ang_r[:, c], ang_k[:, c], -TWO_PI_MID, ang_r[:, c], ALU.mult, ALU.add))
                    step(V.scalar_tensor_tensor(ang_r[:, c], ang_k[:, c], -TWO_PI_LO, ang_r[:, c], ALU.mult, ALU.add))
                    step(V.tensor_scalar(ang_r[:, c], ang_r[:, c], 0.5 * np.pi * quarter, 3.1415925, ALU.add, ALU.min))
                    step(V.tensor_scalar(ang_r[:, c], ang_r[:, c], -3.1415925, None, ALU.max))
                assert k == N_ANGLES

            def conditions():
                dve.wait_ge(sines, 1)
                for c, src in ((C_DT, cond_in[:, 0, :]), (C_GATE, cond_in[:, 1, :]), (C_COS, ang[:, 2, :]),
                               (C_COS + 1, ang[:, 2, :]), (C_COS + 2, ang[:, 3, :]), (C_COS + 3, ang[:, 3, :]),
                               (C_SIN, ang[:, 0, :]), (C_SIN + 2, ang[:, 1, :])):
                    V.tensor_copy(cond[:, :, c], src).then_inc(conds, 1)
                for c, src in ((C_SIN + 1, ang[:, 0, :]), (C_SIN + 3, ang[:, 1, :])):
                    V.tensor_scalar(cond[:, :, c], src, -1.0, None, ALU.mult).then_inc(conds, 1)

            def prepare(at):
                if at == A_SPREAD - 1:
                    spread_qk()
                if at == A_SPREAD + 4:
                    bias_columns()
                if at == A_ANGLES - 1:
                    rotation_angles()
                if at == A_ANGLES + 1:
                    conditions()
                if at in (A_SPREAD + 1, A_SPREAD + 2):
                    split_rest(dve, at - A_SPREAD - 1)

            def hidden_split(n, t):
                e, j = divmod(t, FT)
                if t in DVE_HIGH + DVE_LOW:
                    await_(dve, hid_done, n, t + 1)
                if t in DVE_HIGH:
                    V.tensor_copy(hid_h[:, j, :], hid[:, j, :]).then_inc(hid_high.sem, 1)
                    await_(dve, hid_high, n, DVE_HIGH.index(t) + 1)
                if t in DVE_LOW:
                    V.tensor_tensor(hid_l[:, j, :], hid[:, j, :], hid_h[:, j, :], ALU.subtract).then_inc(hid_low.sem, 1)

            def mean_var(n, src, st, mv, s_stats, s_mv):
                for b in range(GB):
                    V.bn_stats(st[:, b, :], src(b)).then_inc(s_stats.sem, 1)
                await_(dve, s_stats, n)
                apart(nc.vector)
                for b in range(GB):
                    V.bn_aggr(mv[:, b, :], st[:, b, :]).then_inc(s_mv.sem, 1)

            def normalize(dst, src, mv, rs):
                for b in range(GB):
                    ins = V.tensor_scalar(dst[:, b, :], src[:, b, :], mv[:, b, 0:1], rs[:, b:b + 1],
                                          ALU.subtract, ALU.mult)
                return ins

            def pre_stats(n):
                await_(dve, xa_in, n)
                await_(dve, ln0_ve, n - 1)
                mean_var(n, lambda b: xa[:, b, :], st0, mv0, ln0_stats, ln0_mv)

            def pre_normalize(n):
                await_(dve, ln0_rs, n)
                await_(dve, ln0_mv, n)
                await_(dve, xn0_t, n - 1)
                normalize(xn, xa, mv0, rs0).then_inc(ln0_xn.sem, 1)

            def inorm_stats(n):
                await_(dve, haff, n)
                mean_var(n, lambda b: h_aff[:, b * T:(b + 1) * T], sti, mvi, in_stats, in_mv)

            def inorm_apply(n):
                await_(dve, in_coef, n)
                await_(dve, logits, n - 1)
                for b in range(GB):
                    t = slice(b * T, (b + 1) * T)
                    ins = V.tensor_scalar(h32[:, t], h_aff[:, t], in_s[:, b:b + 1], in_t[:, b:b + 1], ALU.mult, ALU.add)
                ins.then_inc(h32_done.sem, 1)

            def h_high(n, p):
                await_(dve, h32_done, n)
                await_(dve, hid_ps, n - 2)
                V.tensor_copy(hh[p][:], h32[:]).then_inc(hh_done.sem, 1)

            def h_low(n, p):
                await_(dve, hh_done, n)
                V.tensor_tensor(hl[p][:], h32[:], hh[p][:], ALU.subtract).then_inc(h_split.sem, 1)

            def top_two(n):
                await_(dve, logits, n)
                V.tensor_copy(lg[:].rearrange("p b e -> p (b e)"), ps_pre[:, 0:GB * E]).then_inc(lg_copied.sem, 1)
                await_(dve, lg_copied, n)
                apart(nc.vector)
                for b in range(GB):
                    V.max(top[:, b, :], lg[:, b, :]).then_inc(topped.sem, 1)
                await_(dve, topped, n)
                V.tensor_tensor(gap[:], top[:, :, 1], top[:, :, 0], ALU.subtract).then_inc(gap_done.sem, 1)
                for b in range(GB):
                    ins = V.max_index(top_i[:, b, :], top[:, b, :], lg[:, b, :])
                ins.then_inc(topi_done.sem, 1)

            def gates_of_two(n):
                await_(dve, topi_done, n)
                V.tensor_copy(top_f[:], top_i[:, :, 0:2].rearrange("p b k -> p k b")).then_inc(gate_step.sem, 1)
                await_(dve, gap_exp, n)
                V.tensor_scalar(gsum[:], gexp[:], 1.0, None, ALU.add).then_inc(gate_step.sem, 1)
                await_(dve, gate_step, n, 2)
                V.reciprocal(gates[:, 0, :], gsum[:]).then_inc(gate_step.sem, 1)
                await_(dve, gate_step, n, 3)
                V.tensor_tensor(gates[:, 1, :], gates[:, 0, :], gexp[:], ALU.mult).then_inc(gate_step.sem, 1)
                for k in range(2):
                    V.tensor_tensor(pick[:, k], inner(top_f[:, k, :], E), bc(cst[:, K_E8:K_E8 + E], GB),
                                    ALU.is_equal).then_inc(gate_step.sem, 1)
                await_(dve, gate_step, n, 6)
                V.tensor_tensor(pick[:], pick[:], gates[:].unsqueeze(3).broadcast_to([P, 2, GB, E]),
                                ALU.mult).then_inc(gate_step.sem, 1)
                await_(dve, gate_step, n, 7)
                await_(dve, comb_tp, n - 1)
                V.tensor_tensor(comb[:], pick[:, 0], pick[:, 1], ALU.add).then_inc(comb_done.sem, 1)

            def gate(n, p, e):
                if isinstance(n, int) and n == 0 and e == 0:
                    dve.wait_ge(cols_done, 2)
                await_(dve, exp_ps, n, (e + 1) * FT)
                await_(dve, comb_bc[e % 2], n, 16 * (e // 2 + 1))
                if e >= 1:
                    dst = gated[e % 2]
                    if e >= 3:
                        await_(dve, y_added, n, e - 2)
                    else:
                        await_(dve, y_added, n - 1)
                else:
                    dst = y_t[p]
                V.scalar_tensor_tensor(dst[:], ps_exp[:], col(R_B2 + e), comb_b[e % 2][:],
                                       ALU.add, ALU.mult).then_inc(gated_done.sem, 1)

            def pde(n, piece):
                if piece == 0:
                    await_(dve, y_back, n)
                    await_(dve, xb_in, n)
                    V.tensor_tensor(flat(f), ps_c[:], flat(xb), ALU.add).then_inc(f_done.sem, 1)
                    await_(dve, f_done, n)
                if piece == 1:
                    V.tensor_tensor(rb[:], f[:], bc(g_b2[:], GB), ALU.mult).then_inc(pde_v.sem, 1)
                    V.tensor_tensor(ua[:], f[:], bc(ag[:, 0, :], GB), ALU.mult).then_inc(pde_v.sem, 1)
                    await_(dve, pde_v, n, 1)
                    V.tensor_tensor(u_[:, :, 1:D - 1], rb[:, :, 2:D], rb[:, :, 0:D - 2], ALU.subtract).then_inc(pde_v.sem, 1)
                if piece == 2:
                    V.tensor_tensor(eu[:], edges(rb, 3), cst[:, K_GE:K_GE + 6].rearrange("p (s k) -> p s k", s=2)
                                    .unsqueeze(1).broadcast_to([P, GB, 2, 3]), ALU.mult).then_inc(pde_v.sem, 1)
                    await_(dve, pde_v, n, 4)
                    V.tensor_reduce(u_[:, :, 0:D:D - 1], eu[:], AX.X, ALU.add).then_inc(pde_v.sem, 1)
                    await_(dve, pde_v, n, 5)
                    V.tensor_tensor(u_[:], u_[:], ua[:], ALU.subtract).then_inc(u_done.sem, 1)
                if piece == 3:
                    V.tensor_tensor(wp[:], f[:], bc(g_p[:], GB), ALU.mult).then_inc(pde_v.sem, 1)
                    V.tensor_tensor(wm[:], f[:], bc(g_m[:], GB), ALU.mult).then_inc(pde_v.sem, 1)
                if piece == 4:
                    await_(dve, pde_v, n, 7)
                    V.tensor_tensor(w_[:, :, 1:D - 1], wp[:, :, 2:D], wm[:, :, 0:D - 2], ALU.add).then_inc(pde_v.sem, 1)
                    V.tensor_tensor(ew[:], edges(f, 4), g_edge[:].unsqueeze(1).broadcast_to([P, GB, 2, 4]),
                                    ALU.mult).then_inc(pde_v.sem, 1)
                    await_(dve, pde_v, n, 9)
                    V.tensor_reduce(w_[:, :, 0:D:D - 1], ew[:], AX.X, ALU.add).then_inc(pde_v.sem, 1)
                    await_(dve, pde_pool, n)
                    V.tensor_tensor(w_[:, :, 1:D - 1], w_[:, :, 1:D - 1], bf[:, :, 1:D - 1], ALU.subtract).then_inc(pde_v.sem, 1)
                if piece == 5:
                    await_(dve, pde_v, n)
                    await_(dve, pde_ps, n)
                    V.tensor_tensor(flat(df), ps_s[:], flat(w_), ALU.add).then_inc(df_done.sem, 1)
                    await_(dve, df_done, n)
                    await_(dve, cond_ready, n)
                    for b in range(GB):
                        V.scalar_tensor_tensor(fn[:, b, :], df[:, b, :], cond_g[:, b, C_DT:C_DT + 1], f[:, b, :],
                                               ALU.mult, ALU.add).then_inc(fn_done.sem, 1)
                    await_(dve, fn_done, n)
                    V.tensor_scalar(x1in[:], fn[:], 0.0, None, ALU.max).then_inc(x1in_done.sem, 1)

            def edges(t, w):
                v = t[:]
                return bass.AP(v.tensor, v.offset, [list(v.ap[0]), list(v.ap[1]), [D - w, 2], [1, w]])

            def norm_stats(n, which):
                src = (x1in, xa2)[which]
                await_(dve, (x1in_done, xa2_done)[which], n)
                mean_var(n, lambda b: src[:, b, :], stn, mvn, ln_stats[which], ln_mv[which])

            def norm_apply(n, which):
                await_(dve, ln_rs[which], n)
                await_(dve, ln_mv[which], n)
                if which == 1:
                    await_(dve, xn_t[0], n)
                normalize(xn0, (x1in, xa2)[which], mvn, rsn).then_inc(ln_xn[which].sem, 1)

            def norm_split(n, which):
                await_(dve, hn_done[which], n)
                V.tensor_copy(hnh[:], hn[:]).then_inc(hnh_done[which].sem, 1)
                await_(dve, hnh_done[which], n)
                V.tensor_tensor(hnl[:], hn[:], hnh[:], ALU.subtract).then_inc(hn_split[which].sem, 1)

            def qk_out(n, j, which):
                await_(dve, qk_lo, n, 2 * j + which + 1)
                dst = (qs, ks)[which]
                V.scalar_tensor_tensor(dst[:, j].rearrange("p b t -> p (b t)"), ps_x[which][:], qk_b[:, which, j:j + 1],
                                       lo_part[which][:], ALU.add, ALU.subtract).then_inc(qk_done.sem, 1)

            def v_out(n):
                await_(dve, v_ps, n)
                V.tensor_tensor(vs[:, :, :, 0:DH], ps_c[:].rearrange("p (b h d) -> p b h d", b=GB, d=DH),
                                bv_b[:].rearrange("p (h d) -> p h d", d=DH).unsqueeze(1).broadcast_to([P, GB, NH, DH]),
                                ALU.add).then_inc(v_done.sem, 1)

            def maximum(n, u):
                await_(dve, s_ps, n, u + 1)
                if u >= 2:
                    await_(dve, dg_done, n, u - 1)
                V.tensor_reduce(mx[u % 2][:], ps_s[:].rearrange("p (j t) -> p j t", j=HJ), AX.X, ALU.max).then_inc(mx_done.sem, 1)

            def context(n, b):
                await_(dve, pv_turned, n, b + 1)
                c = ps_pre[:].rearrange("p (i j d) -> p i j d", i=RG, d=32)
                V.reciprocal(rden[:], c[:, :, :, DH]).then_inc(rden_done.sem, 1)
                await_(dve, rden_done, n, b + 1)
                V.tensor_tensor(cx[:, b, :].rearrange("p (j i d) -> p i j d", i=RG, d=DH), c[:, :, :, 0:DH],
                                rden[:].unsqueeze(3).broadcast_to([P, RG, HJ, DH]), ALU.mult).then_inc(cx_done.sem, 1)

            def residual_1(n):
                await_(dve, wo_ps, n)
                await_(dve, xbo_done, n)
                V.tensor_tensor(flat(xa2), ps_s[:], flat(xbo), ALU.add).then_inc(xa2_done.sem, 1)

            def blend(n):
                await_(dve, f2_ps, n)
                await_(dve, sofar_done, n)
                for b in range(GB):
                    V.scalar_tensor_tensor(res[:, b, :], ps_s[:, b * D:(b + 1) * D], cond_g[:, b, C_GATE:C_GATE + 1],
                                           x2b[:, b, :], ALU.mult, ALU.add).then_inc(res_done.sem, 1)

            def emit(g, p, back, experts, pre):
                n, m = g - 1, g + 1
                for s in range(E):
                    for j in range(FT):
                        at = s * FT + j
                        if experts and j == 2 and s >= 1:
                            gate(g, p, s - 1)
                        if experts and at >= 1:
                            hidden_split(g, at - 1)
                        if isinstance(g, int) and g == 0:
                            prepare(at)
                        if back and at == A_Y:
                            pde(n, 0)
                        if back and A_Y + 2 <= at < A_Y + 6:
                            pde(n, at - A_Y - 1)
                        if back and at == A_PDE + 1:
                            pde(n, 5)
                        if back and at == A_STATS1:
                            norm_stats(n, 0)
                        if back and at == A_NORM1 - 1:
                            norm_apply(n, 0)
                        if back and at == A_QK - 1:
                            norm_split(n, 0)
                        if back and A_QK <= at < A_QK + HJ:
                            qk_out(n, at - A_QK, 0)
                            qk_out(n, at - A_QK, 1)
                        if back and at == A_V:
                            v_out(n)
                        if pre and at == A_STATS:
                            pre_stats(m)
                        if pre and at == A_NORM:
                            pre_normalize(m)
                        for k in steps(at):
                            if back and k < NU:
                                maximum(n, k)
                            if pre and k == K_INORM:
                                inorm_stats(m)
                            if pre and k == K_INORM + 4:
                                inorm_apply(m)
                            if pre and k == K_INORM + 5:
                                h_high(m, 1 - p)
                            if pre and k == K_INORM + 6:
                                h_low(m, 1 - p)
                            if back and turned(k) is not None:
                                context(n, turned(k))
                            if pre and k == K_ROUTER:
                                top_two(m)
                            if pre and k == K_GATES + 1:
                                gates_of_two(m)
                        if back and at == A_WO:
                            residual_1(n)
                        if back and at == A_STATS2:
                            norm_stats(n, 1)
                        if back and at == A_NORM2 - 1:
                            norm_apply(n, 1)
                        if back and at == A_FFN - 1:
                            norm_split(n, 1)
                if experts:
                    hidden_split(g, E * FT - 1)
                    gate(g, p, E - 1)
                if back:
                    blend(n)

            pre_stats(0)
            pre_normalize(0)
            one_hot()
            inorm_stats(0)
            split_w1_first(dve, 0)
            softplus()
            inorm_apply(0)
            h_high(0, 0)
            h_low(0, 0)
            top_two(0)
            split_w1_first(dve, 1)
            gates_of_two(0)
            iterations(dve, emit)

        @block.tensor
        def _(pe):
            def three(o, wh, wl, xh, xl, start=True, stop=True):
                pe.matmul(o, wh, xh, start=start, stop=False)
                pe.matmul(o, wh, xl, start=False, stop=False)
                return pe.matmul(o, wl, xh, start=False, stop=stop)

            def style_network():
                pe.wait_ge(hot_step, 2)
                pe.wait_ge(net_in, 16 * N_NET_LOADS)
                pe.matmul(ps_x[0][0:64, 0:B], subj, onehot[:], start=True, stop=True).then_inc(se_ps, 1)
                pe.wait_ge(se_done, 1)
                pe.matmul(ps_x[1][:, 0:B], hw1, se[:], start=True, stop=True).then_inc(hyp1_ps, 1)
                pe.wait_ge(hyp1_done, 1)
                pe.matmul(ps_c[:, 0:B], hw2, hyp1[:], start=True, stop=True).then_inc(hyp2_ps, 1)
                pe.wait_ge(hyp2_done, 1)
                pe.matmul(ps_hid[0][0:64, 0:B], sw1, hyp2[:], start=True, stop=True).then_inc(sty1_ps, 1)
                pe.wait_ge(sty1_done, 1)
                pe.matmul(ps_hid[1][:, 0:B], sw2[:, 0:D], sty1[:], start=True, stop=True).then_inc(style_ps, 1)
                pe.matmul(ps_exp[:, 0:B], sw2[:, D:2 * D], sty1[:], start=True, stop=True).then_inc(style_ps, 1)
                pe.wait_ge(style_done, 2)

            def prepare(at):
                if at == 3:
                    pe.wait_ge(late_in, 16 * N_LATE_LOADS)
                    pe.transpose(ps_s[:, 0:R_N - R_A], rows_b, ident[0:R_N - R_A, 0:R_N - R_A]).then_inc(cols_ps, 1)
                if at == 2:
                    gates_transpose(0, False)
                if at == A_SPREAD + 3:
                    pe.wait_ge(spread, N_SPREAD)
                    pe.wait_ge(cols_done, 2)
                    for which, row in enumerate((bqe, bke)):
                        for j in range(HJ):
                            mm = pe.matmul(ps_s[:, which * HJ + j:which * HJ + j + 1], row[:, j * P:(j + 1) * P],
                                           ones1[:, 0:1], start=True, stop=True)
                    mm.then_inc(bias_ps, 1)
                if at == E * FT - 1:
                    pe.wait_ge(masks, 4)
                    pe.wait_ge(split_w[0], 4)
                    pe.wait_ge(split_w[1], 4)
                    pe.wait_ge(f2_in, 16)

            def pre_transpose(n):
                await_(pe, ln0_xn, n)
                await_(pe, comb_ct, n - 1)
                for b in range(GB):
                    mm = pe.transpose(ps_pre[:, b * T:(b + 1) * T], xn[:, b, :], ident)
                mm.then_inc(xn0_t.sem, 1)

            def router(n, back):
                await_(pe, h32_done, n)
                await_(pe, haff, n)
                if back:
                    await_(pe, cx_done, n - 2, 1)
                for b in range(GB):
                    mm = pe.matmul(ps_pre[:, b * E:(b + 1) * E], h32[:, b * T:(b + 1) * T], rw[:],
                                   start=True, stop=True)
                mm.then_inc(logits.sem, 1)

            def gates_transpose(n, back):
                await_(pe, comb_done, n)
                await_(pe, lg_copied, n)
                if back:
                    await_(pe, cx_done, n - 2, 3)
                for b in range(GB):
                    mm = pe.transpose(ps_pre[0:E, b * T:(b + 1) * T], comb[:, b, :], ident)
                mm.then_inc(comb_tp.sem, 1)

            def hidden(n, p, e, j):
                if e == 0 and j == 0:
                    await_(pe, h_split, n)
                if isinstance(n, int) and n == 0 and j == 0:
                    if e < 2:
                        pe.wait_ge(w1_split[0], 2 * (e + 1))
                    else:
                        pe.wait_ge(w1_split[1], e - 1)
                evicted(pe, n, e, j - 2)
                w = slice(e * FF + j * P, e * FF + (j + 1) * P)
                three(ps_hid[j % 2][:], w1h[:, w], w1l[:, w], hh[p][:], hl[p][:]).then_inc(hid_ps.sem, 1)

            def evicted(eng, n, e, j):
                if j < 0:
                    e, j = e - 1, j + FT
                if e < 0:
                    n, e = n - 1, E - 1
                await_(eng, hid_done, n, e * FT + j + 1)

            def expert_out(n, e, j):
                if isinstance(n, int) and n == 0 and j == 0:
                    pe.wait_ge(w2_split, e + 1)
                if j == 0 and e >= 1:
                    await_(pe, gated_done, n, e)
                elif j == 0:
                    await_(pe, gated_done, n - 1)
                t = e * FT + j
                if t in DVE_LOW:
                    await_(pe, hid_low, n, DVE_LOW.index(t) + 1)
                else:
                    await_(pe, hid_low_g, n, POOL_LOW.index(t) + 1)
                w = slice(j * D, (j + 1) * D)
                three(ps_exp[:], w2h[:, e, w], w2l[:, e, w], hid_h[:, j, :], hid_l[:, j, :],
                      start=(j == 0), stop=(j == FT - 1)).then_inc(exp_ps.sem, 1)

            def y_transpose(n, p):
                await_(pe, y_added, n)
                for b in range(GB):
                    mm = pe.transpose(ps_c[:, b * D:(b + 1) * D], y_t[p][:, b * T:(b + 1) * T], ident)
                mm.then_inc(y_back.sem, 1)

            def pde_rows(n):
                await_(pe, u_done, n)
                await_(pe, pde_pool, n, 1)
                pe.matmul(ps_s[:], cst[:, K_GX:K_GX + P], flat(u_), start=True, stop=False)
                pe.matmul(ps_s[:], cst[:, K_GXX:K_GXX + P], flat(v_), start=False, stop=True).then_inc(pde_ps.sem, 1)

            def norm_transpose(n, which):
                await_(pe, ln_xn[which], n)
                await_(pe, (f_done, cxt_done)[which], n)
                for b in range(GB):
                    mm = pe.transpose(ps_c[:, b * T:(b + 1) * T], xn0[:, b, :], ident)
                mm.then_inc(xn_t[which].sem, 1)

            def project_v(n):
                for b in range(GB):
                    t = slice(b * T, (b + 1) * T)
                    mm = three(ps_c[:, b * D:(b + 1) * D], hnh[:, t], hnl[:, t], wvh[:], wvl[:])
                mm.then_inc(v_ps.sem, 1)

            def project_qk(n, j):
                if j == 0:
                    await_(pe, hn_split[0], n)
                for which, (wh, wl) in enumerate(((wqh, wql), (wkh, wkl))):
                    if j >= 1:
                        await_(pe, qk_done, n, 2 * j - 1 + which)
                    w = slice(j * P, (j + 1) * P)
                    three(ps_x[which][:], wh[:, w], wl[:, w], hnh[:], hnl[:]).then_inc(qk_ps.sem, 1)

            def head_scores(o, lhs, rhs, b, i):
                r = slice(32 * i, 32 * i + 32)
                for j in range(HJ):
                    mm = pe.matmul(o[:, j * T:(j + 1) * T], lhs[r, j, b, :], rhs[r, j, b, :],
                                   start=False, stop=(j == HJ - 1), skip_group_check=True)
                return mm

            def scores(n, u):
                b, i = divmod(u, RG)
                if u == 0:
                    await_(pe, df_done, n)
                    await_(pe, qk_done, n)
                else:
                    await_(pe, mx_done, n, u)
                pe.matmul(ps_s[:], id16[:], bc(mask16[:], HJ), start=True, stop=False, skip_group_check=True)
                head_scores(ps_s, qs, ks, b, i).then_inc(s_ps.sem, 1)

            def scores_turned(n, u):
                b, i = divmod(u, RG)
                if u >= 2:
                    await_(pe, exp_done, n, u - 1)
                o = ps_x[u % 2]
                pe.matmul(o[:], id16[:], bc(maskT16[:], HJ), start=True, stop=False, skip_group_check=True)
                head_scores(o, ks, qs, b, i)

            def less_maximum(n, u):
                await_(pe, dg_done, n, u + 1)
                pe.matmul(ps_x[u % 2][:], ones_r[:], flat(dg[u % 2]), start=False, stop=True,
                          skip_group_check=True).then_inc(x_ps.sem, 1)

            def weighted_values(n, u):
                b, i = divmod(u, RG)
                await_(pe, exp_done, n, u + 1)
                if u == 0:
                    await_(pe, v_done, n)
                elif i == 0:
                    await_(pe, pv_out, n, b)
                for j in range(HJ):
                    mm = pe.matmul(ps_c[32 * j:32 * j + VW, i * T:(i + 1) * T], vs[:, b, j * RG + i, :],
                                   pt[u % 2][:, j, :], start=True, stop=True)
                mm.then_inc(pv_done.sem, 1)

            def turn_values(n, m, b):
                await_(pe, pv_out, n, b + 1)
                if m is not None and b < 2:
                    await_(pe, (haff, lg_copied)[b], m)
                elif m is not None and b == 3:
                    await_(pe, comb_ct, m)
                if b >= 1:
                    await_(pe, cx_done, n, b)
                for i in range(RG):
                    mm = pe.transpose(ps_pre[:, i * P:(i + 1) * P], pvt[:, i * T:(i + 1) * T], ident)
                mm.then_inc(pv_turned.sem, 1)

            def context_transpose(n):
                await_(pe, cx_done, n)
                for b in range(GB):
                    mm = pe.transpose(ps_c[:, b * T:(b + 1) * T], cx[:, b, :], ident)
                mm.then_inc(cx_t.sem, 1)

            def project_out(n):
                await_(pe, cxt_done, n)
                await_(pe, mx_done, n)
                for b in range(GB):
                    mm = pe.matmul(ps_s[:, b * D:(b + 1) * D], cxt[:, b * T:(b + 1) * T], wo[:], start=True, stop=True)
                mm.then_inc(wo_ps.sem, 1)

            def ffn_hidden(n, j):
                if j == 0:
                    await_(pe, hn_split[1], n)
                if j < 2:
                    await_(pe, exp_done, n, NU - 1 + j)
                else:
                    await_(pe, gelu_done, n, j - 1)
                w = slice(j * P, (j + 1) * P)
                three(ps_x[j % 2][:], f1h[:, w], f1l[:, w], hnh[:], hnl[:]).then_inc(f1_ps.sem, 1)

            def ffn_out(n):
                await_(pe, gelu_done, n)
                await_(pe, xa2_done, n)
                for b in range(GB):
                    for j in range(FT):
                        mm = pe.matmul(ps_s[:, b * D:(b + 1) * D], gl[:, j, b * T:(b + 1) * T], f2[:, j, :],
                                       start=(j == 0), stop=(j == FT - 1))
                mm.then_inc(f2_ps.sem, 1)

            def keep_clock():
                for _ in range(6):
                    pe.matmul(ps_hid[0][:], id16[:], bc(mask16[:], HJ), start=True, stop=True)

            def attention_step(n, m, k):
                if k < NU:
                    scores(n, k)
                if 2 <= k < NU + 2:
                    less_maximum(n, k - 2)
                if 3 <= k < NU + 3:
                    weighted_values(n, k - 3)
                if 1 <= k <= NU:
                    scores_turned(n, k - 1)
                if turned(k) is not None:
                    turn_values(n, m, turned(k))

            def emit(g, p, back, experts, pre):
                n, m = g - 1, g + 1
                for s in range(E):
                    for j in range(FT):
                        at = s * FT + j
                        if experts:
                            for t in PIECES[j] if s >= 1 else ():
                                expert_out(g, s - 1, t)
                            hidden(g, p, s, j)
                            if j == FT - 1 and s < E - 1:
                                expert_out(g, s, 0)
                        if isinstance(g, int) and g == 0:
                            prepare(at)
                        if back and at == A_Y:
                            y_transpose(n, 1 - p)
                        if back and at == A_PDE:
                            pde_rows(n)
                        if back and at == A_NORM1:
                            norm_transpose(n, 0)
                        if back and A_QK <= at < A_QK + HJ:
                            project_qk(n, at - A_QK)
                        if back and at == A_V:
                            project_v(n)
                        if pre and at == A_AFFINE:
                            pre_transpose(m)
                        for k in steps(at):
                            if back and not experts and k < 3:
                                keep_clock()
                            if back:
                                attention_step(n, m if pre else None, k)
                            if pre and k == K_ROUTER:
                                router(m, back)
                            if pre and k == K_GATES_T:
                                gates_transpose(m, back)
                        if back and at == A_CONTEXT:
                            context_transpose(n)
                        if back and at == A_WO:
                            project_out(n)
                        if back and at == A_NORM2:
                            norm_transpose(n, 1)
                        if back and A_FFN <= at < A_FFN + FT:
                            ffn_hidden(n, at - A_FFN)
                if experts:
                    for t in range(FT):
                        expert_out(g, E - 1, t)
                if back:
                    ffn_out(n)

            pe.wait_ge(cst_in, 16)
            pe.wait_ge(rows_in, 16 * N_ROW_LOADS)
            pe.transpose(ps_s[:, 0:R_A], rows_a, ident[0:R_A, 0:R_A]).then_inc(cols_ps, 1)
            pre_transpose(0)
            style_network()
            router(0, False)
            iterations(pe, emit)


def kernel(**inputs):
    import concourse.bacc as bacc
    from concourse.bass_utils import run_bass_kernel_spmd

    nc = bacc.Bacc("TRN2", target_bir_lowering=False, num_devices=1)
    arrays, args = {}, {}
    for name, value in list(inputs.items()) + [("cst", shape_constants())]:
        v = np.ascontiguousarray(value)
        arrays["in_" + name] = v
        args[name] = nc.dram_tensor("in_" + name, v.shape, mybir.dt.from_np(v.dtype), kind="ExternalInput").ap()
    out = nc.dram_tensor("out", (B, T, D), F32, kind="ExternalOutput").ap()
    cond_seq_kernel(nc, args, out)
    r = run_bass_kernel_spmd(nc, [arrays], core_ids=[0])
    return r.results[0]["out"]
```
